# Optimizing a Trainium2 kernel written in Bass

```python
import numpy as np
import jax
import jax.numpy as jnp

def _softmax(x, axis=-1):
    return jax.nn.softmax(x, axis=axis)

def _gelu(x):
    return jax.nn.gelu(x, approximate=True)

def _silu(x):
    return jax.nn.silu(x)

def _sigmoid(x):
    return jax.nn.sigmoid(x)

def _layernorm(x, axis=-1, eps=1e-05):
    m = jnp.mean(x, axis=axis, keepdims=True)
    v = jnp.var(x, axis=axis, keepdims=True)
    return (x - m) / jnp.sqrt(v + eps)

def _scatter_add(tgt, idx, src, axis=0):
    return tgt.at[idx].add(src)

def _segment_sum(src, seg, n):
    return jax.ops.segment_sum(src, seg, n)
kernel_name = 'mk_adj_resnorm_d4_adj_r2_2a14a9'

def setup_inputs(seed: int=0):
    np.random.seed(seed)
    _w = jnp.asarray

    def _rec_inputs():
        import jax
        import jax.numpy as jnp
        _gk = jax.random.key(seed)
        x = -0.001547 + 1.001 * jax.random.normal(jax.random.fold_in(_gk, 1), (16, 512, 64), jnp.float32)
        _w = (1.0 + jnp.arange(512, dtype=jnp.float32)) ** (-0.5)
        _w = _w / _w.mean()
        _pij = jnp.clip(0.015625 * _w[:, None] * _w[None, :], 0.0, 1.0)
        _a = jax.random.uniform(jax.random.fold_in(_gk, 2), (16, 512, 512)) < _pij
        _a = jnp.logical_or(_a, jnp.swapaxes(_a, -1, -2))
        _af = _a.astype(jnp.float32)
        adj = _af
        _nm = jnp.ones((16, 512), dtype=bool)
        nodemask = _nm
        return (x, adj, nodemask)
    x, adj, nodemask = _rec_inputs()

    def _L0_gnn_setup():
        import jax, jax.numpy as jnp
        import numpy as np
        B, N, C, H = (8, 256, 64, 128)
        T, K = (10, 2)
        TAUS = (0.25, 0.5, 0.75)
        WTS = (0.25, 0.5, 0.25)
        EPS_GIN = 0.0
        AVG_DEG = 32.0
        key = jax.random.key(seed)
        ks = jax.random.split(key, 6)
        x = jax.random.normal(ks[0], (B, N, C), jnp.float32)
        u = jax.random.uniform(ks[1], (B, N, N))
        a = u < AVG_DEG / N
        adj = jnp.maximum(a, jnp.swapaxes(a, 1, 2)).astype(jnp.float32)
        mask = jax.random.bernoulli(ks[2], 0.9, (B, N))
        W1 = jax.random.normal(ks[3], (C, H), jnp.float32) / np.float32(np.sqrt(C))
        b1 = jnp.zeros((H,), jnp.float32)
        W2 = jax.random.normal(ks[4], (H, C), jnp.float32) / np.float32(np.sqrt(H))
        b2 = jnp.zeros((C,), jnp.float32)
        return {'x': x, 'adj': adj, 'mask': mask, 'W1': W1, 'b1': b1, 'W2': W2, 'b2': b2}
    _L0_gnn_all = _L0_gnn_setup()
    _L0_gnn_in = {k: v for k, v in _L0_gnn_all.items() if k in ('W1', 'b1', 'W2', 'b2')}
    del _L0_gnn_all

    def _L1_gnn_setup():
        import jax, jax.numpy as jnp
        import numpy as np
        B, N, F, U = (16, 1024, 64, 64)
        key = jax.random.key(seed)
        k1, k2, k3 = jax.random.split(key, 3)
        node_features = jax.random.normal(k1, (B, N, F), dtype=jnp.float32)
        adjacency_matrix = (jax.random.uniform(k2, (B, N, N)) < 0.01).astype(jnp.float32)
        kernel = jax.random.normal(k3, (F, U), dtype=jnp.float32) * (1.0 / np.sqrt(F))
        return {'node_features': node_features, 'adjacency_matrix': adjacency_matrix, 'kernel': kernel}
    _L1_gnn_all = _L1_gnn_setup()
    _L1_gnn_in = {k: v for k, v in _L1_gnn_all.items() if k in ('kernel',)}
    del _L1_gnn_all

    def _L2_gnn_setup():
        import jax, jax.numpy as jnp
        import numpy as np
        B, L, C, OUT = (32, 512, 64, 64)
        BN_EPS = 1e-05
        key = jax.random.key(seed)
        kH, kA, kW = jax.random.split(key, 3)
        H = jax.random.normal(kH, (B, L, C), dtype=jnp.float32)
        A = jax.random.uniform(kA, (B, L, L), dtype=jnp.float32)
        gamma = jnp.ones((C,), jnp.float32)
        beta = jnp.zeros((C,), jnp.float32)
        W = jax.random.normal(kW, (C, OUT), dtype=jnp.float32) * 0.05
        b = jnp.zeros((OUT,), jnp.float32)
        return {'H': H, 'A': A, 'gamma': gamma, 'beta': beta, 'W': W, 'b': b}
    _L2_gnn_all = _L2_gnn_setup()
    _L2_gnn_in = {k: v for k, v in _L2_gnn_all.items() if k in ('gamma', 'beta', 'W', 'b')}
    del _L2_gnn_all

    def _L3_gnn_setup():
        import jax, jax.numpy as jnp
        import numpy as np
        B, N, H = (4, 2048, 64)
        key = jax.random.key(seed)
        ks = jax.random.split(key, 12)
        s = 1.0 / np.sqrt(H)
        h = jax.random.normal(ks[0], (B, N, H), dtype=jnp.float32)
        A = jax.random.uniform(ks[1], (B, N, N), dtype=jnp.float32)
        W1 = jax.random.normal(ks[2], (H, H), dtype=jnp.float32) * s
        b1 = jnp.zeros((H,), dtype=jnp.float32)
        W2 = jax.random.normal(ks[3], (H, H), dtype=jnp.float32) * s
        b2 = jnp.zeros((H,), dtype=jnp.float32)
        W_ih = jax.random.normal(ks[4], (3 * H, H), dtype=jnp.float32) * s
        b_ih = jnp.zeros((3 * H,), dtype=jnp.float32)
        W_hh = jax.random.normal(ks[5], (3 * H, H), dtype=jnp.float32) * s
        b_hh = jnp.zeros((3 * H,), dtype=jnp.float32)
        return {'h': h, 'A': A, 'W1': W1, 'b1': b1, 'W2': W2, 'b2': b2, 'W_ih': W_ih, 'b_ih': b_ih, 'W_hh': W_hh, 'b_hh': b_hh}
    _L3_gnn_all = _L3_gnn_setup()
    _L3_gnn_in = {k: v for k, v in _L3_gnn_all.items() if k in ('W1', 'b1', 'W2', 'b2', 'W_ih', 'b_ih', 'W_hh', 'b_hh')}
    del _L3_gnn_all
    return {'x': x, 'adj': adj, 'nodemask': nodemask, 'L0_gnn_W1': _L0_gnn_in['W1'], 'L0_gnn_b1': _L0_gnn_in['b1'], 'L0_gnn_W2': _L0_gnn_in['W2'], 'L0_gnn_b2': _L0_gnn_in['b2'], 'L1_gnn_kernel': _L1_gnn_in['kernel'], 'L2_gnn_gamma': _L2_gnn_in['gamma'], 'L2_gnn_beta': _L2_gnn_in['beta'], 'L2_gnn_W': _L2_gnn_in['W'], 'L2_gnn_b': _L2_gnn_in['b'], 'L3_gnn_W1': _L3_gnn_in['W1'], 'L3_gnn_b1': _L3_gnn_in['b1'], 'L3_gnn_W2': _L3_gnn_in['W2'], 'L3_gnn_b2': _L3_gnn_in['b2'], 'L3_gnn_W_ih': _L3_gnn_in['W_ih'], 'L3_gnn_b_ih': _L3_gnn_in['b_ih'], 'L3_gnn_W_hh': _L3_gnn_in['W_hh'], 'L3_gnn_b_hh': _L3_gnn_in['b_hh']}

def reference(x, adj, nodemask, L0_gnn_W1, L0_gnn_b1, L0_gnn_W2, L0_gnn_b2, L1_gnn_kernel, L2_gnn_gamma, L2_gnn_beta, L2_gnn_W, L2_gnn_b, L3_gnn_W1, L3_gnn_b1, L3_gnn_W2, L3_gnn_b2, L3_gnn_W_ih, L3_gnn_b_ih, L3_gnn_W_hh, L3_gnn_b_hh):
    import jax
    import jax.numpy as jnp

    def _L0_gnn_ref(x, adj, mask, W1, b1, W2, b2):
        import jax, jax.numpy as jnp
        import numpy as np
        B, N, C, H = (8, 256, 64, 128)
        T, K = (10, 2)
        TAUS = (0.25, 0.5, 0.75)
        WTS = (0.25, 0.5, 0.25)
        EPS_GIN = 0.0
        AVG_DEG = 32.0
        Bc, Nc, Cc = x.shape
        eye = jnp.eye(Nc, dtype=bool)
        adj_ = jnp.where(eye, 1.0, adj)
        neigh = (adj_ > 0) & ~eye
        ni = neigh.astype(jnp.int32)
        rank = jnp.cumsum(ni, axis=-1) - ni
        nb = ni.sum(-1)
        skip = jnp.where(nb > T, (nb + K - 1) // K, 1)
        skip = jnp.maximum(skip, 1)
        sk = skip[:, :, None]
        rem = neigh & (sk > 1) & (rank % sk == sk - 1) & mask[:, :, None]
        rem = rem | jnp.swapaxes(rem, 1, 2)
        adj_d = jnp.where(rem, 0.0, adj_)
        nd = adj_d > 0
        vals = jnp.where(nd[..., None], x[:, None, :, :], jnp.inf)
        s = jnp.sort(vals, axis=2)
        nv = nd.sum(2)
        agg = jnp.zeros_like(x)
        for tau, w in zip(TAUS, WTS):
            pos = jnp.asarray(tau, x.dtype) * jnp.maximum(nv - 1, 0).astype(x.dtype)
            lo = jnp.floor(pos).astype(jnp.int32)
            hi = jnp.ceil(pos).astype(jnp.int32)
            frac = (pos - lo.astype(x.dtype))[..., None]
            idx_lo = jnp.broadcast_to(lo[:, :, None, None], (Bc, Nc, 1, Cc))
            idx_hi = jnp.broadcast_to(hi[:, :, None, None], (Bc, Nc, 1, Cc))
            v_lo = jnp.take_along_axis(s, idx_lo, axis=2)[:, :, 0, :]
            v_hi = jnp.take_along_axis(s, idx_hi, axis=2)[:, :, 0, :]
            agg = agg + jnp.asarray(w, x.dtype) * (v_lo + frac * (v_hi - v_lo))
        agg = jnp.where(nv[..., None] > 0, agg, 0.0)
        out = (1.0 + EPS_GIN) * x + agg
        h = jax.nn.relu(out @ W1 + b1)
        y = h @ W2 + b2
        return y * mask[..., None].astype(y.dtype)

    def _L1_gnn_ref(node_features, adjacency_matrix, kernel):
        import jax, jax.numpy as jnp
        import numpy as np
        B, N, F, U = (16, 1024, 64, 64)
        n = adjacency_matrix.shape[-1]
        adj = adjacency_matrix + jnp.eye(n, dtype=adjacency_matrix.dtype)
        row_sum = jnp.sum(adj, axis=-1)
        d_inv_sqrt = jnp.where(row_sum > 0, row_sum ** (-0.5), 0.0)
        norm_adj = d_inv_sqrt[:, :, None] * adj * d_inv_sqrt[:, None, :]
        transformed = jnp.einsum('bnf,fu->bnu', node_features, kernel)
        out = jnp.einsum('bnm,bmu->bnu', norm_adj, transformed)
        return jax.nn.relu(out)

    def _L2_gnn_ref(H, A, gamma, beta, W, b):
        import jax, jax.numpy as jnp
        import numpy as np
        B, L, C, OUT = (32, 512, 64, 64)
        BN_EPS = 1e-05
        batch, l, c = H.shape
        Hf = H.reshape(batch * l, c)
        mean = Hf.mean(axis=0)
        var = jnp.mean((Hf - mean) ** 2, axis=0)
        Hn = ((Hf - mean) * jax.lax.rsqrt(var + BN_EPS) * gamma + beta).reshape(batch, l, c)
        d = A.sum(axis=2)
        A_norm = jnp.sqrt(d)[:, :, None] * A * jax.lax.rsqrt(d)[:, None, :]
        A_hat = jnp.eye(l, dtype=A.dtype) - A_norm
        X = Hn @ W + b
        out = jnp.einsum('bij,bjo->bio', A_hat, X)
        return jax.nn.leaky_relu(out, negative_slope=0.01)

    def _L3_gnn_ref(h, A, W1, b1, W2, b2, W_ih, b_ih, W_hh, b_hh):
        import jax, jax.numpy as jnp
        import numpy as np
        B, N, H = (4, 2048, 64)
        m = jax.nn.relu(jnp.einsum('bnh,hk->bnk', h, W1) + b1)
        m = jax.nn.relu(jnp.einsum('bnh,hk->bnk', m, W2) + b2)
        msg = jax.nn.relu(jnp.einsum('bij,bjh->bih', A, m))
        gi = jnp.einsum('bnh,gh->bng', msg, W_ih) + b_ih
        gh = jnp.einsum('bnh,gh->bng', h, W_hh) + b_hh
        i_r, i_z, i_n = jnp.split(gi, 3, axis=-1)
        h_r, h_z, h_n = jnp.split(gh, 3, axis=-1)
        r = jax.nn.sigmoid(i_r + h_r)
        z = jax.nn.sigmoid(i_z + h_z)
        n = jnp.tanh(i_n + r * h_n)
        return (1.0 - z) * n + z * h
    x = _layernorm(x + _L0_gnn_ref(x, adj, nodemask, L0_gnn_W1, L0_gnn_b1, L0_gnn_W2, L0_gnn_b2), axis=-1)
    x = _layernorm(x + _L1_gnn_ref(x, adj, L1_gnn_kernel), axis=-1)
    x = _layernorm(x + _L2_gnn_ref(x, adj, L2_gnn_gamma, L2_gnn_beta, L2_gnn_W, L2_gnn_b), axis=-1)
    x = _layernorm(x + _L3_gnn_ref(x, adj, L3_gnn_W1, L3_gnn_b1, L3_gnn_W2, L3_gnn_b2, L3_gnn_W_ih, L3_gnn_b_ih, L3_gnn_W_hh, L3_gnn_b_hh), axis=-1)
    return x

_drawn_inputs = setup_inputs


def setup_inputs(seed=0):
    import zlib

    import numpy as np

    out = dict(_drawn_inputs(seed))
    spreads = {'L0_gnn_b1': (0.0, 0.1),
     'L0_gnn_b2': (0.0, 0.1),
     'L2_gnn_gamma': (1.0, 0.2),
     'L2_gnn_beta': (0.0, 0.1),
     'L2_gnn_b': (0.0, 0.1),
     'L3_gnn_b1': (0.0, 0.1),
     'L3_gnn_b2': (0.0, 0.1),
     'L3_gnn_b_ih': (0.0, 0.62),
     'L3_gnn_b_hh': (0.0, 0.745)}
    factors = {}
    for name, (base, spread) in spreads.items():
        noise = np.random.default_rng([zlib.crc32(name.encode()), seed]).standard_normal(out[name].shape)
        drawn = base * np.exp(spread * noise) if base else spread * noise
        out[name] = jnp.asarray(drawn.astype(out[name].dtype))
    for name, factor in factors.items():
        out[name] = (out[name] * factor).astype(out[name].dtype)
    return out
```

```python
from contextlib import ExitStack

import concourse.bass as bass
from concourse import mybir

ALU = mybir.AluOpType
ACT = mybir.ActivationFunctionType
DT = mybir.dt
F32, F16, BF16, U16, I16, I32, U8 = DT.float32, DT.float16, DT.bfloat16, DT.uint16, DT.int16, DT.int32, DT.uint8

B, N, C, H = 16, 512, 64, 128
P = 128
NT = N // P
PAIRS = B // 2
G = 16
SPAN = N // G
WORD = 16
NH = N // WORD
K = 6
TRIM, KEEP = 10, 2
QW = (0.25, 0.5, 0.25)
EPS = 1e-5
SLOTS = 4
CW = 6
GROUPS = C // 8
UNITS = K * GROUPS
PER_TILE = UNITS // NT


def comparators(n):
    p = n // 2
    while p:
        q, r, d = n // 2, 0, p
        while True:
            yield p, r, d
            if q == p:
                break
            d, q, r = q - p, q // 2, p
        p //= 2


def sides(t, p, r, d):
    m = sum(1 for i in range(r, N, 2 * p) if i + p + d <= N)
    low = t[:, :, 0:2 * p * m].rearrange("q a (m t w) -> q a m t w", t=2, w=p)[:, :, :, r // p, :]
    if r:
        high = t[:, :, r + d:r + d + 2 * p * m].rearrange("q a (m t w) -> q a m t w", t=2, w=p)[:, :, :, 0, :]
    else:
        high = t[:, :, 0:2 * p * m].rearrange("q a (m t w) -> q a m t w", t=2, w=p)[:, :, :, 1, :]
    return low, high, m


def wait(eng, sem, value):
    if not isinstance(value, int) or value > 0:
        eng.wait_ge(sem, value)


def hold(eng, sem, value, passed):
    eng.wait_ge(sem, value)
    eng.sem_inc(passed, 1)


def build(nc, x_in, adj_in, mask_in, w0a, b0a, w0b, b0b, k1, gamma, beta, w2, b2,
          w3a, b3a, w3b, b3b, w_ih, b_ih, w_hh, b_hh, out):
    ctx = ExitStack()
    with ctx:
        def sb(name, shape, dt):
            return ctx.enter_context(nc.sbuf_tensor(name, shape, dt))

        def sem(name):
            return ctx.enter_context(nc.semaphore(name))

        parts_d = nc.dram_tensor("parts_d", [3, B, C, N], BF16, kind="Internal").ap()
        adjt_d = nc.dram_tensor("adjt_d", [B, P, NT, N], BF16, kind="Internal").ap()

        x_all = sb("x_all", [P, NT, B, C], F32)
        ident = sb("ident", [P, P], F32)
        identb = sb("identb", [P, P], BF16)
        rowsum = sb("rowsum", [P, B, NT], F32)
        mask_t = sb("mask_t", [P, NT, B], F32)
        stage_w = sb("stage_w", [P, 5, C], F32)
        ones_row = sb("ones_row", [1, P], F32)
        w0a_s = sb("w0a_s", [C, H], F32)
        b0a_s = sb("b0a_s", [H, 1], F32)
        w0b_s = sb("w0b_s", [H, C], F32)
        b0b_s = sb("b0b_s", [1, C], F32)
        k1_s = sb("k1_s", [C, C], F32)
        rank_t = sb("rank_t", [P, NT, B, C], F16)

        gamma_s = sb("gamma_s", [C, 1], F32)
        beta_s = sb("beta_s", [C, 1], F32)
        w2_s = sb("w2_s", [C, C], F32)
        b2_s = sb("b2_s", [1, C], F32)
        w3a_s = sb("w3a_s", [C, C], F32)
        b3a_s = sb("b3a_s", [C, 1], F32)
        w3b_s = sb("w3b_s", [C + 1, C], F32)
        wih_s = sb("wih_s", [C + 1, 3 * C], F32)
        whh_s = sb("whh_s", [C + 1, 3 * C], F32)

        with ExitStack() as bank_ctx:
            ring = [bank_ctx.enter_context(nc.psum_tensor(f"ring{i}", [P, 512], F32)) for i in range(2)]
            bcast = bank_ctx.enter_context(nc.psum_tensor("bcast", [P, 3, 512], F32))
            rows = [bank_ctx.enter_context(nc.psum_tensor(f"rows{i}", [P, 512], F32)) for i in range(2)]
            found = bank_ctx.enter_context(nc.psum_tensor("found", [P, NT, C], F32))
        bank = [ctx.enter_context(nc.psum_tensor(f"bank{i}", [P, 2, 512], F32)) for i in range(SLOTS)]

        sort_ctx = ExitStack()
        with sort_ctx:
            def ss(name, shape, dt):
                return sort_ctx.enter_context(nc.sbuf_tensor(name, shape, dt))

            keys = ss("keys", [P, PAIRS, N], F32)
            perm = ss("perm", [P, PAIRS, N], F16)
            low_new = ss("low_new", [P, PAIRS * N // 2], F32)
            swap = ss("swap", [P, PAIRS * N // 2], F16)
            delta = ss("delta", [P, PAIRS * N // 2], F16)
            keys2 = ss("keys2", [P, PAIRS, N], F32)
            parts = ss("parts", [P, 3, PAIRS, N], BF16)
            place = ss("place", [P, N], F32)
            place512 = ss("place512", [P, N], F32)
            mask_u = ss("mask_u", [B, N], U8)
            mask_f = ss("mask_f", [B, N], F32)

        outer = sb
        first_ctx = ExitStack()

        def sb(name, shape, dt):
            return first_ctx.enter_context(nc.sbuf_tensor(name, shape, dt))

        eye = sb("eye", [P, NT, N], BF16)
        upper = sb("upper", [P, N], BF16)
        group_end = sb("group_end", [P, G, C], F16)
        half_id = sb("half_id", [P, 2, G, C], F16)
        group_tag = sb("group_tag", [P, G, C], U16)
        one_u = sb("one_u", [P, C], U16)
        sel_a = sb("sel_a", [P, P * 32], BF16)
        sel_b = sb("sel_b", [P, P * 16], BF16)
        iota_p = sb("iota_p", [P, 1], I32)
        iota_m = sb("iota_m", [P, 2], I32)
        iota_a = sb("iota_a", [P, 1], F32)
        iota_b = sb("iota_b", [P, 1], F32)
        sum16 = sb("sum16", [P, 8], F32)
        ones_b = sb("ones_b", [P, 1], BF16)

        adj_f = sb("adj_f", [P, NT, N], F32)
        adj_b = sb("adj_b", [P, NT, N], BF16)
        neigh = sb("neigh", [P, NT, N], BF16)
        adj_t = sb("adj_t", [P, NT, N], BF16)
        adj_l = sb("adj_l", [P, NT, N], BF16)
        neigh_t = sb("neigh_t", [P, NT, N], BF16)
        drop2 = sb("drop2", [P, N], BF16)
        drop1, kept_t = adj_b, neigh_t
        small = sb("small", [P, 16, NT], F32)
        small_u = sb("small_u", [P, 4, NT], U16)
        mult3 = sb("mult3", [P, NT, 3], U16)
        low3 = sb("low3", [P, NT, 3], U16)
        frac3 = sb("frac3", [P, NT, 3], U16)
        limit = sb("limit", [P, NT, 3, 2], F32)
        weight = sb("weight", [P, NT, 3, 2], F32)
        weight_old = sb("weight_old", [P, NT, 3, 2], F32)
        member = sb("member", [P, NT, 3, G * C], BF16)
        mtmp = sb("mtmp", [P, 4, C], U16)
        mpow = sb("mpow", [P, 2, C], F16)
        cnt = sb("cnt", [P, G * C], F16)
        words2 = sb("words2", [P, 2, 3, G * C], U16)
        below = sb("below", [P, 3, (G + 1) * C], I16)
        chosen = sb("chosen", [P, 3, G * C], I16)
        picked = sb("picked", [P, 3, 3, G * C], I16)
        result = sb("result", [P, 3, NT, K, C], U16)
        spare = sb("spare", [P, NT * K * C], U16)
        idx = sb("idx", [P, 2, NT, K * C], BF16)
        idx_t = sb("idx_t", [P, 2, 3, N], BF16)
        table = sb("table", [P, 3, 2 * GROUPS, C], BF16)
        near = sb("near", [P, 2, 3, N], BF16)
        hot = sb("hot", [P, 2, 2, N], BF16)
        prod = sb("prod", [P, 2, N], F32)
        agg = sb("agg", [P, NT, C], F32)
        hid_t, feat_t = prod[:, 0, :], prod[0:C, 1, :]
        pre = sb("pre", [P, NT, C], F32)
        scaled = sb("scaled", [P, NT, C], F32)
        split3 = sb("split3", [P, 3, NT, C], BF16)
        stats = sb("stats", [P, NT, 6], F32)
        moments = sb("moments", [P, NT, 2], F32)
        inv = sb("inv", [P, 2, NT], F32)

        first_ctx.close()
        sb = outer

        def slots(name, shape, dt):
            return [sb(f"{name}{i}", shape, dt) for i in range(SLOTS)]

        adj_s = slots("adj_s", [P, NT, N], BF16)
        cur = slots("cur", [P, NT, C], F32)
        cur_t = slots("cur_t", [C + 1, N], F32)
        mid_t = slots("mid_t", [C + 1, N], F32)
        msg_t = slots("msg_t", [C + 1, N], F32)
        lin = slots("lin", [P, NT, C], F32)
        scl = slots("scl", [P, NT, C], F32)
        rest = slots("rest", [P, NT, C], F32)
        cut = slots("cut", [P, 3, NT, C], BF16)
        gate = slots("gate", [P, NT, 2 * C], F32)
        cand = slots("cand", [P, NT, C], F32)
        stat = slots("stat", [P, NT, 6], F32)
        mom = slots("mom", [P, NT, 2], F32)
        dev = slots("dev", [P, 2, NT], F32)
        bn_stat = sb("bn_stat", [C, B, 6], F32)
        bn_mom = sb("bn_mom", [C, 2], F32)
        bn_s = sb("bn_s", [C, 4], F32)
        w2f_s = sb("w2f_s", [C, C], F32)
        b2f_s = sb("b2f_s", [1, C], F32)
        root = sb("root", [P, B, NT], F32)
        inv_root = sb("inv_root", [P, B, NT], F32)
        last_mom = sb("last_mom", [P, 2, B, NT], F32)
        last_dev = sb("last_dev", [P, B, NT], F32)

        names = """x_loaded w_loaded const cdone xT_ps xT_ev sorted2 copied swapped parts_ready parts_out rank_ready
            rankT_ps rankT_ev mask_ready mT_ps adj_loaded adjb_ready adjT_ps adjT_ev adj_out neigh_ready neighT_ready nb_ps
            cnt_ps drop_ready rs_ps kept_ready nv_ps nv_read member_ready cw_ps cw_ev tile_read idx_ready idxT_ps idxT_ev
            table_in adjl_in bc_ps bc_ev hot_ready row_ps prod_ready found_ps acc_done
            ffn_x fx_ps fx_ev h_ps h_ev y_ps z_ready sd_ready x1_ready tr_ps split_ready g_ps g_read
            dve_chain out_done fin sp_passed pe_passed w23_ready wT_ps l1_done bT_ps bn_read bn_var bn_dev bn_shift b2f_ps w2f_ready
            roots2 roots3 cur_ready xt_ps xt_ev lin_ps cut_ready agg_ps var_ready dev_ready x3_ready ht_ps ht_ev m1_ps m1_ev m2_ps cut2_ready
            msg_ps msg_ev gate_ps rz_ready cand_ready new_ready graph_done last_var last_dev_ready tile_done ones_made""".split()
        S = {n: sem(n) for n in names}
        adjs_in = [sem(f"adjs_in{q}") for q in range(SLOTS)]
        block = ctx.enter_context(nc.Block())
        flat = "p a b -> p (a b)"

        def xb(b):
            return x_all[:, :, b, :]

        @block.sync
        def _(sp):
            sp.dma_start(x_all[:, 0], x_in.rearrange("b (t p) c -> t p b c", p=P)[0]).then_inc(S["x_loaded"], 16)
            for t in range(1, NT):
                sp.dma_start(x_all[:, t], x_in.rearrange("b (t p) c -> t p b c", p=P)[t]).then_inc(S["x_loaded"], 16)
            for dst, src in ((w0a_s[:, :], w0a), (b0a_s[:, :], b0a.rearrange("(h o) -> h o", o=1)), (w0b_s[:, :], w0b),
                             (b0b_s[:, :], b0b.rearrange("(o c) -> o c", o=1)), (k1_s[:, :], k1), (mask_u[:, :], mask_in),
                             (gamma_s[:, :], gamma.rearrange("(c o) -> c o", o=1)), (beta_s[:, :], beta.rearrange("(c o) -> c o", o=1)),
                             (w2_s[:, :], w2), (b2_s[:, :], b2.rearrange("(o c) -> o c", o=1)), (w3a_s[:, :], w3a),
                             (b3a_s[:, :], b3a.rearrange("(c o) -> c o", o=1)), (w3b_s[0:C, :], w3b),
                             (w3b_s[C:C + 1, :], b3b.rearrange("(o c) -> o c", o=1)),
                             (stage_w[0:96, 0:2, :], w_ih.rearrange("(s p) c -> p s c", p=96)),
                             (stage_w[0:96, 2:4, :], w_hh.rearrange("(s p) c -> p s c", p=96)),
                             (wih_s[C:C + 1, :], b_ih.rearrange("(o c) -> o c", o=1)),
                             (whh_s[C:C + 1, :], b_hh.rearrange("(o c) -> o c", o=1))):
                sp.dma_start(dst, src).then_inc(S["w_loaded"], 16)
            for s in range(3):
                sp.wait_ge(S["parts_ready"], s + 1)
                for h in range(2):
                    sp.dma_start(parts_d[s].rearrange("(a h) c n -> h c a n", h=2)[h], parts[C * h:C * h + C, s]).then_inc(S["parts_out"], 16)

            def load_adj(b):
                sp.dma_start(adj_f[:, :, :], adj_in[b].rearrange("(t p) n -> p t n", p=P)).then_inc(S["adj_loaded"], 16)

            sp.wait_ge(S["rankT_ev"], PAIRS)
            load_adj(0)
            sp.wait_ge(S["parts_out"], 96)

            def body(b, look):
                if look is not None:
                    if not (isinstance(look, int) and look == 0):
                        hold(sp, S["row_ps"], look * UNITS, S["sp_passed"])
                        hold(sp, S["g_ps"], look * NT, S["sp_passed"])
                    for q in range(4):
                        for s in range(3):
                            sp.dma_start(table[32 * q:32 * q + 32, s, :, 16 * q:16 * q + 16],
                                         parts_d[s, look].rearrange("(g q) (a e) -> q a g e", q=4, e=16)[q]).then_inc(S["table_in"], 16)
                    hold(sp, S["adj_out"], 16 * look + 16, S["sp_passed"])
                    sp.dma_start(adj_l[:, :, :], adjt_d[look]).then_inc(S["adjl_in"], 16)
                if b is not None:
                    hold(sp, S["adjT_ev"], NT * b + NT, S["sp_passed"])
                    sp.dma_start(adjt_d[b], adj_t[:, :, :]).then_inc(S["adj_out"], 16)
                    if not (isinstance(b, int) and b == B - 1):
                        hold(sp, S["adjb_ready"], NT * b + NT, S["sp_passed"])
                        load_adj(b + 1)

            body(0, None)
            sp.wait_ge(S["cdone"], 2)
            body(1, 0)
            with sp.Fori(2, B - 1) as b:
                body(b, b - 1)
            body(B - 1, B - 2)
            body(None, B - 1)
            sp.wait_ge(S["l1_done"], 1)
            with sp.Fori(0, B // SLOTS) as g0:
                b0 = g0 * SLOTS
                for q in range(SLOTS):
                    b = b0 + q
                    hold(sp, S["graph_done"], b + 1, S["sp_passed"])
                    sp.dma_start(adj_s[q][:, :, :], adjt_d[b]).then_inc(adjs_in[q], 16)
            for t in range(NT):
                sp.wait_ge(S["tile_done"], t + 1)
                sp.dma_start(out.rearrange("b (t p) c -> t p b c", p=P)[t], x_all[:, t]).then_inc(S["out_done"], 16)
            sp.wait_ge(S["out_done"], 64)

        @block.gpsimd
        def _(g):
            n = [0]

            def made(ins):
                ins.then_inc(S["const"], 1)
                n[0] += 1

            def here():
                g.wait_ge(S["const"], n[0])

            made(g.memset(ident[:, :], 0.0))
            made(g.iota(place[:, :], [[1, N]], base=0, channel_multiplier=0, allow_small_or_imprecise_dtypes=True))
            made(g.memset(ones_row[:, :], 1.0))
            here()
            made(g.affine_select(out=ident[:, :], in_=ident[:, :], compare_op=ALU.not_equal, fill=1.0, base=0,
                                 pattern=[[-1, P]], channel_multiplier=1))
            here()
            made(g.tensor_copy(identb[:, :], ident[:, :]))
            for a in range(PAIRS):
                made(g.tensor_copy(perm[:, a, :], place[:, :]))
            made(g.tensor_scalar(place512[:, :], place[:, :], float(N), None, ALU.mult))
            here()
            g.drain().then_inc(S["cdone"], 1)
            g.wait_ge(S["rankT_ev"], PAIRS)
            g.wait_ge(S["parts_out"], 96)
            g.wait_ge(S["mT_ps"], 1)
            made(g.memset(eye[:, :, :], 0.0))
            made(g.iota(iota_p[:, :], [[1, 1]], base=0, channel_multiplier=1))
            made(g.memset(upper[:, :], 1.0))
            made(g.memset(sel_a[:, :], 1.0))
            made(g.memset(sel_b[:, :], 1.0))
            made(g.memset(sum16[:, :], 1.0))
            made(g.memset(table[:, :, :, :], 0.0))
            made(g.memset(ones_b[:, :], 1.0))
            made(g.memset(below[:, :, 0:C], -1.0))
            made(g.memset(one_u[:, :], 1.0))
            made(g.iota(group_end[:, :, :], [[SPAN, G], [0, C]], base=SPAN, channel_multiplier=0, allow_small_or_imprecise_dtypes=True))
            made(g.iota(half_id[:, :, :, :], [[1, 2], [2, G], [0, C]], base=0, channel_multiplier=0, allow_small_or_imprecise_dtypes=True))
            made(g.iota(group_tag[:, :, :], [[1024, G], [0, C]], base=0, channel_multiplier=0, allow_small_or_imprecise_dtypes=True))
            here()
            made(g.affine_select(out=eye[:, :, :], in_=eye[:, :, :], compare_op=ALU.not_equal, fill=1.0, base=0,
                                 pattern=[[P, NT], [-1, N]], channel_multiplier=1))
            made(g.affine_select(out=upper[:, :], in_=upper[:, :], compare_op=ALU.is_ge, fill=0.0, base=0,
                                 pattern=[[1, N]], channel_multiplier=-1))
            for t, w in ((sel_a, 32), (sel_b, 16)):
                made(g.affine_select(out=t[:, :], in_=t[:, :], compare_op=ALU.is_ge, fill=0.0, base=0,
                                     pattern=[[1, P * w]], channel_multiplier=-w))
            made(g.affine_select(out=sum16[:, :], in_=sum16[:, :], compare_op=ALU.is_ge, fill=0.0, base=0,
                                 pattern=[[-16, 8]], channel_multiplier=1))
            here()
            for t, w in ((sel_a, 32), (sel_b, 16)):
                made(g.affine_select(out=t[:, :], in_=t[:, :], compare_op=ALU.is_ge, fill=0.0, base=w - 1,
                                     pattern=[[-1, P * w]], channel_multiplier=w))
            made(g.affine_select(out=sum16[:, :], in_=sum16[:, :], compare_op=ALU.is_ge, fill=0.0, base=15,
                                 pattern=[[16, 8]], channel_multiplier=-1))
            here()
            g.drain().then_inc(S["cdone"], 1)

        @block.tensor
        def _(pe):
            mm, tp = nc.tensor.matmul, nc.tensor.transpose
            pe.wait_ge(S["cdone"], 1)
            pe.wait_ge(S["x_loaded"], 16 * NT)
            for a in range(PAIRS):
                if a >= 2:
                    pe.wait_ge(S["xT_ev"], a - 1)
                for t in range(NT):
                    i = tp(ring[a % 2][:, P * t:P * t + P], x_all[:, t, 2 * a:2 * a + 2, :].rearrange(flat), ident[:, :])
                i.then_inc(S["xT_ps"], 1)
            pe.wait_ge(S["mask_ready"], 1)
            for t in range(NT):
                i = tp(bcast[:, 0, B * t:B * t + B], mask_f[:, P * t:P * t + P], ident[0:B, 0:B])
            i.then_inc(S["mT_ps"], 1)
            pe.wait_ge(S["rank_ready"], 1)
            for a in range(PAIRS):
                pe.wait_ge(S["rankT_ev"] if a >= 2 else S["xT_ev"], a - 1 if a >= 2 else PAIRS)
                for t in range(NT):
                    i = tp(ring[a % 2][:, P * t:P * t + P], keys2[:, a, P * t:P * t + P], ident[:, :])
                i.then_inc(S["rankT_ps"], 1)
            pe.wait_ge(S["cdone"], 2)

            def graph(b):
                for j in range(NT):
                    for i in range(NT):
                        if j == 0:
                            pe.wait_ge(S["adjb_ready"], NT * b + i + 1)
                        if i == 0 and j >= 2:
                            pe.wait_ge(S["adjT_ev"], NT * b + j - 1)
                        ins = tp(ring[j % 2][:, :].bitcast(BF16)[:, P * i:P * i + P], adj_b[:, i, P * j:P * j + P], identb[:, :])
                    ins.then_inc(S["adjT_ps"], 1)
                pe.wait_ge(S["neighT_ready"], b + 1)
                for i in range(NT):
                    for j in range(NT):
                        ins = mm(bcast[:, 0, i:i + 1], neigh_t[:, j, P * i:P * i + P], ones_b[:, :], start=(j == 0), stop=(j == NT - 1))
                ins.then_inc(S["nb_ps"], 1)
                for i in range(NT):
                    pe.wait_ge(S["adjT_ev"], NT * b + NT)
                    if i >= 2:
                        pe.wait_ge(S["drop_ready"], NT * b + i - 1)
                    for j in range(NT):
                        ins = mm(ring[i % 2][:, P * j:N], neigh_t[:, j, P * i:P * i + P], upper[:, 0:N - P * j], start=(j == 0), stop=(j == NT - 1))
                    ins.then_inc(S["cnt_ps"], 1)
                for j in range(NT):
                    pe.wait_ge(S["drop_ready"], NT * b + NT)
                    if j >= 2:
                        pe.wait_ge(S["kept_ready"], NT * b + j - 1)
                    mm(ring[j % 2][:, :], identb[:, :], drop1[:, j, :], start=True, stop=False)
                    for i in range(NT):
                        ins = mm(ring[j % 2][:, P * i:P * i + P], drop1[:, i, P * j:P * j + P], identb[:, :], start=False, stop=(i == NT - 1))
                    ins.then_inc(S["rs_ps"], 1)
                pe.wait_ge(S["kept_ready"], NT * b + NT)
                for i in range(NT):
                    for j in range(NT):
                        ins = mm(bcast[:, 1, i:i + 1], kept_t[:, j, P * i:P * i + P], ones_b[:, :], start=(j == 0), stop=(j == NT - 1))
                ins.then_inc(S["nv_ps"], 1)
                pe.wait_ge(S["member_ready"], NT * b + NT)

            def chunk(b, i, n):
                u = CW * i + n
                if u >= 2:
                    pe.wait_ge(S["cw_ev"], NT * CW * b + u - 1)
                for j in range(NT):
                    ins = mm(ring[u % 2][:, :], kept_t[:, j, P * i:P * i + P], member[:, j, n // 2, 512 * (n % 2):512 * (n % 2) + 512],
                             start=(j == 0), stop=(j == NT - 1))
                ins.then_inc(S["cw_ps"], 1)

            def spread(l, u):
                k, g8 = divmod(u, GROUPS)
                if u:
                    pe.wait_ge(S["bc_ev"], UNITS * l + u)
                row = (k % 2) * C + 8 * g8
                mm(bcast[:, 0, :], sel_a[:, 32 * row:32 * row + P], idx_t[:, 0, k // 2, :], start=True, stop=True)
                mm(bcast[:, 1, :], sel_a[:, 32 * row + P:32 * row + 2 * P], idx_t[:, 0, k // 2, :], start=True, stop=True)
                mm(bcast[:, 2, :], sel_b[:, 16 * row:16 * row + P], idx_t[:, 1, k // 2, :], start=True, stop=True).then_inc(S["bc_ps"], 1)

            def lookup(l, u):
                k, g8 = divmod(u, GROUPS)
                if u == 0:
                    pe.wait_ge(S["table_in"], 192 * l + 192)
                pe.wait_ge(S["hot_ready"], UNITS * l + u + 1)
                if u >= 2:
                    pe.wait_ge(S["prod_ready"], UNITS * l + u - 1)
                for h in range(2):
                    for s in range(3):
                        ins = mm(rows[u % 2][C * h:C * h + C, :], table[:, s, 2 * g8 + h, :], hot[:, u % 2, h, :], start=(s == 0), stop=(s == 2))
                ins.then_inc(S["row_ps"], 1)

            def total(l, u):
                k, g8 = divmod(u, GROUPS)
                if g8 == 0 and k >= 1:
                    pe.wait_ge(S["acc_done"], K * l + k)
                pe.wait_ge(S["prod_ready"], UNITS * l + u + 1)
                for i in range(NT):
                    ins = mm(found[:, i, 8 * g8:8 * g8 + 8], prod[:, u % 2, P * i:P * i + P], sum16[:, :], start=True, stop=True)
                ins.then_inc(S["found_ps"], 1)

            def dense(l):
                hold(pe, S["ffn_x"], l + 1, S["pe_passed"])
                for i in range(NT):
                    ins = tp(ring[0][0:C, P * i:P * i + P], scaled[:, i, :], ident[:, :])
                ins.then_inc(S["fx_ps"], 1)
                pe.wait_ge(S["fx_ev"], 2 * l + 1)
                mm(ring[1][:, :], w0a_s[:, :], feat_t[:, :], start=True, stop=True).then_inc(S["h_ps"], 1)
                pe.wait_ge(S["h_ev"], l + 1)
                for i in range(NT):
                    mm(ring[0][:, C * i:C * i + C], hid_t[:, P * i:P * i + P], w0b_s[:, :], start=True, stop=False)
                    ins = mm(ring[0][:, C * i:C * i + C], ones_row[:, :], b0b_s[:, :], start=False, stop=True)
                ins.then_inc(S["y_ps"], 1)
                hold(pe, S["x1_ready"], l + 1, S["pe_passed"])
                for i in range(NT):
                    ins = tp(ring[1][0:C, P * i:P * i + P], pre[:, i, :], ident[:, :])
                ins.then_inc(S["fx_ps"], 1)
                pe.wait_ge(S["fx_ev"], 2 * l + 2)
                for i in range(NT):
                    ins = mm(ring[0][:, C * i:C * i + C], feat_t[:, P * i:P * i + P], k1_s[:, :], start=True, stop=True)
                ins.then_inc(S["tr_ps"], 1)
                pe.wait_ge(S["split_ready"], l + 1)
                pe.wait_ge(S["adjl_in"], 16 * l + 16)
                for i in range(NT):
                    for j in range(NT):
                        for s in range(3):
                            ins = mm(ring[1][:, C * i:C * i + C], adj_l[:, j, P * i:P * i + P], split3[:, s, j, :],
                                     start=(j == 0 and s == 0), stop=(j == NT - 1 and s == 2))
                    ins.then_inc(S["g_ps"], 1)

            def body(b, l):
                if b is not None:
                    graph(b)
                    for n in range(CW):
                        chunk(b, 0, n)
                    pe.wait_ge(S["nv_read"], b + 1)
                for i in range(NT):
                    for q in range(PER_TILE):
                        u = PER_TILE * i + q
                        if b is not None and i + 1 < NT and q >= PER_TILE - CW:
                            chunk(b, i + 1, q - PER_TILE + CW)
                        if l is not None:
                            spread(l, u)
                            if u >= 1:
                                lookup(l, u - 1)
                            if u >= 2:
                                total(l, u - 2)
                if l is not None:
                    lookup(l, UNITS - 1)
                    total(l, UNITS - 2)
                    total(l, UNITS - 1)
                    if b is not None:
                        pe.wait_ge(S["cw_ev"], NT * CW * b + NT * CW)
                    dense(l)
                if b is not None:
                    pe.wait_ge(S["idx_ready"], b + 1)
                    pe.wait_ge(S["cw_ev"], NT * CW * b + NT * CW)
                    if l is not None:
                        pe.wait_ge(S["g_read"], l + 1)
                    for a in range(2):
                        for k in range(3):
                            u = 3 * a + k
                            if u >= 2:
                                pe.wait_ge(S["idxT_ev"], 6 * b + u - 1)
                            for i in range(NT):
                                ins = tp(ring[u % 2][:, :].bitcast(BF16)[:, P * i:P * i + P], idx[:, a, i, P * k:P * k + P], identb[:, :])
                            ins.then_inc(S["idxT_ps"], 1)
                    pe.wait_ge(S["idxT_ev"], 6 * b + 6)
                elif l is not None:
                    pass

            body(0, None)
            with pe.Fori(1, B) as b:
                body(b, b - 1)
            body(None, B - 1)

            pe.wait_ge(S["l1_done"], 1)
            for s in range(4):
                ins = tp(bank[0][0:C, 0, 96 * s:96 * s + 96], stage_w[0:96, s, :], ident[0:96, 0:96])
            ins.then_inc(S["wT_ps"], 1)
            pe.wait_ge(S["w23_ready"], 2)
            for b in range(B):
                if b >= 2:
                    pe.wait_ge(S["bn_read"], b - 1)
                for i in range(NT):
                    ins = tp(bank[b % 2][0:C, 0, P * i:P * i + P], x_all[:, i, b, :], ident[:, :])
                ins.then_inc(S["bT_ps"], 1)
            pe.wait_ge(S["bn_shift"], 1)
            mm(bank[2][0:1, 0, 0:C], bn_s[:, 3:4], w2_s[:, :], start=True, stop=True).then_inc(S["b2f_ps"], 1)
            pe.wait_ge(S["w2f_ready"], 1)

            def turn(q, k, src):
                for i in range(NT):
                    ins = tp(bank[q][0:C, k, P * i:P * i + P], src[:, i, :], ident[:, :])
                return ins

            with pe.Fori(0, B // SLOTS) as g0:
                b0 = g0 * SLOTS
                for q in range(SLOTS):
                    hold(pe, S["cur_ready"], b0 + q + 1, S["pe_passed"])
                    turn(q, 0, cur[q]).then_inc(S["xt_ps"], 1)
                for q in range(SLOTS):
                    pe.wait_ge(S["xt_ev"], b0 + q + 1)
                    for i in range(NT):
                        mm(bank[q][:, 1, C * i:C * i + C], cur_t[q][0:C, P * i:P * i + P], w2f_s[:, :], start=True, stop=False)
                        ins = mm(bank[q][:, 1, C * i:C * i + C], ones_row[:, :], b2f_s[:, :], start=False, stop=True)
                    ins.then_inc(S["lin_ps"], 1)
                for q in range(SLOTS):
                    pe.wait_ge(adjs_in[q], 16 * (g0 + 1))
                    pe.wait_ge(S["cut_ready"], b0 + q + 1)
                    for i in range(NT):
                        for j in range(NT):
                            for s in range(3):
                                ins = mm(bank[q][:, 0, C * i:C * i + C], adj_s[q][:, j, P * i:P * i + P], cut[q][:, s, j, :],
                                         start=(j == 0 and s == 0), stop=(j == NT - 1 and s == 2))
                    ins.then_inc(S["agg_ps"], 1)
                for q in range(SLOTS):
                    hold(pe, S["x3_ready"], b0 + q + 1, S["pe_passed"])
                    turn(q, 1, cur[q]).then_inc(S["ht_ps"], 1)
                for q in range(SLOTS):
                    hold(pe, S["ht_ev"], b0 + q + 1, S["pe_passed"])
                    mm(bank[q][0:C, 0, :], w3a_s[:, :], cur_t[q][0:C, :], start=True, stop=True).then_inc(S["m1_ps"], 1)
                for q in range(SLOTS):
                    pe.wait_ge(S["m1_ev"], b0 + q + 1)
                    for i in range(NT):
                        ins = mm(bank[q][:, 1, C * i:C * i + C], mid_t[q][:, P * i:P * i + P], w3b_s[:, :], start=True, stop=True)
                    ins.then_inc(S["m2_ps"], 1)
                for q in range(SLOTS):
                    pe.wait_ge(S["cut2_ready"], b0 + q + 1)
                    for j in range(NT):
                        for s in range(3):
                            ins = mm(bank[q][0:C, 0, :], cut[q][:, s, j, :], adj_s[q][:, j, :], start=(j == 0 and s == 0), stop=(j == NT - 1 and s == 2))
                    ins.then_inc(S["msg_ps"], 1)
                for q in range(SLOTS):
                    pe.wait_ge(S["msg_ev"], b0 + q + 1)
                    for i in range(NT):
                        dst = bank[q][:, i // 2, 256 * (i % 2):256 * (i % 2) + 256]
                        mm(dst[:, 0:3 * C], msg_t[q][:, P * i:P * i + P], wih_s[:, :], start=True, stop=False, skip_group_check=True)
                        mm(dst[:, 0:2 * C], cur_t[q][:, P * i:P * i + P], whh_s[:, 0:2 * C], start=False, stop=True, skip_group_check=True)
                        ins = mm(dst[:, 3 * C:4 * C], cur_t[q][:, P * i:P * i + P], whh_s[:, 2 * C:3 * C], start=True, stop=True, skip_group_check=True)
                    ins.then_inc(S["gate_ps"], 1)

        @block.scalar
        def _(act):
            run = nc.scalar.activation
            for a in range(PAIRS):
                act.wait_ge(S["xT_ps"], a + 1)
                run(keys[:, a, :], ring[a % 2][:, :], ACT.Copy).then_inc(S["xT_ev"], 1)
            act.wait_ge(S["w_loaded"], 16 * 18)
            run(mask_f[:, :], mask_u[:, :], ACT.Copy).then_inc(S["mask_ready"], 1)
            act.wait_ge(S["mT_ps"], 1)
            run(mask_t[:, :, :].rearrange(flat), bcast[:, 0, 0:NT * B], ACT.Copy).then_inc(S["mask_ready"], 1)
            for a in range(PAIRS):
                act.wait_ge(S["rankT_ps"], a + 1)
                run(rank_t[:, :, 2 * a:2 * a + 2, :].rearrange("p t b c -> p t (b c)"),
                    ring[a % 2][:, :].rearrange("p (t q) -> p t q", t=NT), ACT.Copy).then_inc(S["rankT_ev"], 1)

            def graph(b):
                act.wait_ge(S["adj_loaded"], 16 * b + 16)
                if not (isinstance(b, int) and b == 0):
                    act.wait_ge(S["rs_ps"], NT * b)
                else:
                    act.wait_ge(S["parts_out"], 96)
                for i in range(NT):
                    run(adj_b[:, i, :], adj_f[:, i, :], ACT.Copy, accum_out=rowsum[:, b, i:i + 1]).then_inc(S["adjb_ready"], 1)
                if not (isinstance(b, int) and b == 0):
                    act.wait_ge(S["adj_out"], 16 * b)
                for j in range(NT):
                    act.wait_ge(S["adjT_ps"], NT * b + j + 1)
                    run(adj_t[:, j, :], ring[j % 2][:, :].bitcast(BF16)[:, 0:N], ACT.Copy).then_inc(S["adjT_ev"], 1)

            def chunk(b, i, n):
                u = CW * i + n
                if n == 0 and i >= 1:
                    wait(act, S["tile_read"], 2 * (NT * b + i) - 1)
                if n == 2 and i >= 2:
                    act.wait_ge(S["tile_read"], 2 * (NT * b + i - 1))
                act.wait_ge(S["cw_ps"], NT * CW * b + u + 1)
                dst = cnt[:, 512 * n:512 * n + 512] if n < 2 else words2[:, i % 2, n // 2, 512 * (n % 2):512 * (n % 2) + 512]
                run(dst, ring[u % 2][:, :], ACT.Copy).then_inc(S["cw_ev"], 1)

            def spread(l, u):
                act.wait_ge(S["bc_ps"], UNITS * l + u + 1)
                if u >= 2:
                    act.wait_ge(S["prod_ready"], UNITS * l + u - 1)
                run(near[:, u % 2].rearrange(flat), bcast[:, :, :].rearrange(flat), ACT.Copy).then_inc(S["bc_ev"], 1)

            def dense(l):
                act.wait_ge(S["fx_ps"], 2 * l + 1)
                run(feat_t[:, :], ring[0][0:C, :], ACT.Copy).then_inc(S["fx_ev"], 1)
                act.wait_ge(S["h_ps"], l + 1)
                run(hid_t[:, :], ring[1][:, :], ACT.Relu, bias=b0a_s[:, :]).then_inc(S["h_ev"], 1)
                act.wait_ge(S["z_ready"], 3 * l + 1)
                run(inv[:, 0, :], small[:, 14, :], ACT.Sqrt).then_inc(S["sd_ready"], 1)
                act.wait_ge(S["z_ready"], 3 * l + 2)
                run(inv[:, 1, :], small[:, 13, :], ACT.Sqrt).then_inc(S["sd_ready"], 1)
                act.wait_ge(S["fx_ps"], 2 * l + 2)
                run(feat_t[:, :], ring[1][0:C, :], ACT.Copy).then_inc(S["fx_ev"], 1)
                act.wait_ge(S["z_ready"], 3 * l + 3)
                run(inv[:, 0, :], small[:, 14, :], ACT.Sqrt).then_inc(S["sd_ready"], 1)

            def body(b, l):
                if b is not None:
                    graph(b)
                    for n in range(CW):
                        chunk(b, 0, n)
                for i in range(NT):
                    for q in range(PER_TILE):
                        if b is not None and i + 1 < NT and q >= PER_TILE - CW:
                            chunk(b, i + 1, q - PER_TILE + CW)
                        if l is not None:
                            spread(l, PER_TILE * i + q)
                if l is not None:
                    dense(l)
                if b is not None:
                    for u in range(6):
                        act.wait_ge(S["idxT_ps"], 6 * b + u + 1)
                        run(idx_t[:, u // 3, u % 3, :], ring[u % 2][:, :].bitcast(BF16)[:, 0:N], ACT.Copy).then_inc(S["idxT_ev"], 1)

            body(0, None)
            with act.Fori(1, B) as b:
                body(b, b - 1)
            body(None, B - 1)

            act.wait_ge(S["wT_ps"], 1)
            run(wih_s[0:C, :], bank[0][0:C, 0, 0:3 * C], ACT.Copy).then_inc(S["w23_ready"], 1)
            run(whh_s[0:C, :], bank[0][0:C, 0, 3 * C:6 * C], ACT.Copy).then_inc(S["w23_ready"], 1)
            run(root[:, :, :], rowsum[:, :, :], ACT.Sqrt).then_inc(S["roots2"], 1)
            act.wait_ge(S["bn_var"], 1)
            run(bn_s[:, 1:2], bn_s[:, 0:1], ACT.Sqrt).then_inc(S["bn_dev"], 1)
            with act.Fori(0, B // SLOTS) as g0:
                b0 = g0 * SLOTS
                for q in range(SLOTS):
                    act.wait_ge(S["xt_ps"], b0 + q + 1)
                    run(cur_t[q][0:C, :], bank[q][0:C, 0, :], ACT.Copy).then_inc(S["xt_ev"], 1)
                for q in range(SLOTS):
                    act.wait_ge(S["var_ready"], b0 + q + 1)
                    run(dev[q][:, 1, :], dev[q][:, 0, :], ACT.Sqrt).then_inc(S["dev_ready"], 1)
                for q in range(SLOTS):
                    act.wait_ge(S["ht_ps"], b0 + q + 1)
                    run(cur_t[q][0:C, :], bank[q][0:C, 1, :], ACT.Copy).then_inc(S["ht_ev"], 1)
                for q in range(SLOTS):
                    act.wait_ge(S["m1_ps"], b0 + q + 1)
                    run(mid_t[q][0:C, :], bank[q][0:C, 0, :], ACT.Relu, bias=b3a_s[:, :]).then_inc(S["m1_ev"], 1)
                for q in range(SLOTS):
                    act.wait_ge(S["msg_ps"], b0 + q + 1)
                    run(msg_t[q][0:C, :], bank[q][0:C, 0, :], ACT.Relu).then_inc(S["msg_ev"], 1)
                for q in range(SLOTS):
                    act.wait_ge(S["gate_ps"], b0 + q + 1)
                    run(gate[q][:, :, :], bank[q][:, :, :].rearrange("p k (i n) -> p (k i) n", i=2)[:, :, 0:2 * C], ACT.Sigmoid).then_inc(S["rz_ready"], 1)
                for q in range(SLOTS):
                    act.wait_ge(S["cand_ready"], b0 + q + 1)
                    run(cand[q][:, :, :], scl[q][:, :, :], ACT.Tanh).then_inc(S["new_ready"], 1)
            act.wait_ge(S["last_var"], 1)
            run(last_dev[:, :, :], last_mom[:, 1], ACT.Sqrt).then_inc(S["last_dev_ready"], 1)

        @block.vector
        def _(dve):
            v = nc.vector
            tt, ts, stt = v.tensor_tensor, v.tensor_scalar, v.scalar_tensor_tensor
            count = [0]

            def did(ins):
                ins.then_inc(S["dve_chain"], 1)
                count[0] += 1
                return count[0]

            def need(n):
                if n > 0:
                    dve.wait_ge(S["dve_chain"], n)

            def then(ins):
                need(did(ins))

            def restart():
                need(count[0])
                dve.sem_clear(S["dve_chain"])
                count[0] = 0

            def tell(name):
                need(count[0])
                v.engine_nop().then_inc(S[name], 1)

            dve.wait_ge(S["cdone"], 1)
            dve.wait_ge(S["xT_ev"], PAIRS)
            for p, r, d in comparators(N):
                lo, hi, m = sides(keys, p, r, d)
                plo, phi, _ = sides(perm, p, r, d)
                size = PAIRS * m * p
                new, sw, de = (t[:, 0:size].rearrange("q (a m w) -> q a m w", a=PAIRS, w=p) for t in (low_new, swap, delta))
                if count[0]:
                    need(count[0] - 2)
                did(tt(sw, lo, hi, ALU.is_gt))
                mn = did(tt(new, lo, hi, ALU.min))
                need(mn - 2)
                dd = did(tt(de, phi, plo, ALU.subtract))
                need(mn)
                mx = did(tt(hi, lo, hi, ALU.max))
                need(dd)
                dm = did(tt(de, de, sw, ALU.mult))
                need(mx)
                did(v.tensor_copy(lo, new))
                need(dm)
                did(tt(plo, plo, de, ALU.add))
                did(tt(phi, phi, de, ALU.subtract))
            need(count[0])
            then(stt(out=keys2[:, :, :], in0=perm[:, :, :], scalar=float(N), in1=place[:, :].unsqueeze(1).to_broadcast([P, PAIRS, N]), op0=ALU.mult, op1=ALU.add))
            then(v.tensor_copy(parts[:, 0], keys[:, :, :]))
            tell("parts_ready")
            then(tt(keys[:, :, :], keys[:, :, :], parts[:, 0], ALU.subtract))
            then(v.tensor_copy(parts[:, 1], keys[:, :, :]))
            tell("parts_ready")
            then(tt(parts[:, 2], keys[:, :, :], parts[:, 1], ALU.subtract))
            tell("parts_ready")
            for p, r, d in comparators(N):
                lo, hi, m = sides(keys2, p, r, d)
                new = low_new[:, 0:PAIRS * m * p].rearrange("q (a m w) -> q a m w", a=PAIRS, w=p)
                then(tt(new, lo, hi, ALU.min))
                then(tt(hi, lo, hi, ALU.max))
                then(v.tensor_copy(lo, new))
            then(tt(keys2[:, :, :], keys2[:, :, :], place512[:, :].unsqueeze(1).to_broadcast([P, PAIRS, N]), ALU.subtract))
            tell("rank_ready")
            dve.wait_ge(S["cdone"], 2)
            did(ts(iota_m[:, 0:1], iota_p[:, :], 31, None, ALU.bitwise_and))
            then(ts(iota_m[:, 1:2], iota_p[:, :], 15, None, ALU.bitwise_and))
            did(v.tensor_copy(iota_a[:, :], iota_m[:, 0:1]))
            then(v.tensor_copy(iota_b[:, :], iota_m[:, 1:2]))
            dve.wait_ge(S["mask_ready"], 2)
            restart()

            def members(b, j):
                if j == 0 and not (isinstance(b, int) and b == 0):
                    dve.wait_ge(S["cw_ps"], NT * CW * b)
                r = rank_t[:, j, b, :]
                spread_r = r.unsqueeze(1).to_broadcast([P, G, C])
                did(tt(member[:, j, 0, :].rearrange("p (g c) -> p g c", g=G), spread_r, group_end[:, :, :], ALU.is_lt))
                then(v.tensor_copy(mtmp[:, 0, :], r))
                did(ts(mtmp[:, 1, :], mtmp[:, 0, :], 4, None, ALU.logical_shift_right))
                then(ts(mtmp[:, 2, :], mtmp[:, 0, :], WORD - 1, None, ALU.bitwise_and))
                did(v.tensor_copy(mpow[:, 0, :], mtmp[:, 1, :]))
                then(tt(mtmp[:, 3, :], one_u[:, :], mtmp[:, 2, :], ALU.logical_shift_left))
                halves = member[:, j, 1:3, :].rearrange("p s (g c) -> p (s g) c", g=G)
                then(tt(halves, mpow[:, 0, :].unsqueeze(1).to_broadcast([P, 2 * G, C]), half_id[:, :, :, :].rearrange("p s g c -> p (s g) c"), ALU.is_equal))
                then(tt(halves, halves, mtmp[:, 3, :].unsqueeze(1).to_broadcast([P, 2 * G, C]), ALU.mult))
                tell("member_ready")

            nb, en, f1, f2, s1, s2 = (small[:, n, :] for n in range(6))

            def graph(b):
                dve.wait_ge(S["adjb_ready"], NT * b + NT)
                then(tt(neigh[:, :, :], adj_b[:, :, :], eye[:, :, :], ALU.is_gt))
                members(b, 0)
                dve.wait_ge(S["adjT_ev"], NT * b + NT)
                then(tt(neigh_t[:, :, :], adj_t[:, :, :], eye[:, :, :], ALU.is_gt))
                tell("neighT_ready")
                members(b, 1)
                members(b, 2)
                dve.wait_ge(S["nb_ps"], b + 1)
                did(ts(en, bcast[:, 0, 0:NT], float(TRIM), None, ALU.is_gt))
                then(ts(small_u[:, 0, :], bcast[:, 0, 0:NT], 1.0, None, ALU.add))
                did(tt(en, en, mask_t[:, :, b], ALU.mult))
                then(ts(small_u[:, 1, :], small_u[:, 0, :], 1, None, ALU.logical_shift_right))
                did(ts(f1, small_u[:, 1, :], 1.0, None, ALU.add))
                then(ts(f2, small_u[:, 1, :], 2.0, 1.0, ALU.mult, ALU.add))
                did(tt(f1, f1, en, ALU.mult))
                then(tt(f2, f2, en, ALU.mult))
                did(ts(s1, f1, -1.0, None, ALU.add))
                then(ts(s2, f2, -1.0, None, ALU.add))
                for i in range(NT):
                    dve.wait_ge(S["cnt_ps"], NT * b + i + 1)
                    did(stt(out=drop1[:, i, :], in0=ring[i % 2][:, :], scalar=s1[:, i:i + 1], in1=neigh[:, i, :], op0=ALU.is_equal, op1=ALU.mult))
                    then(stt(out=drop2[:, :], in0=ring[i % 2][:, :], scalar=s2[:, i:i + 1], in1=neigh[:, i, :], op0=ALU.is_equal, op1=ALU.mult))
                    then(tt(drop1[:, i, :], drop1[:, i, :], drop2[:, :], ALU.add))
                    tell("drop_ready")
                members(b, 3)
                for j in range(NT):
                    dve.wait_ge(S["rs_ps"], NT * b + j + 1)
                    then(stt(out=kept_t[:, j, :], in0=ring[j % 2][:, :], scalar=0.0, in1=neigh_t[:, j, :], op0=ALU.is_equal, op1=ALU.mult))
                    then(tt(kept_t[:, j, P * j:P * j + P], kept_t[:, j, P * j:P * j + P], eye[:, j, P * j:P * j + P], ALU.add))
                    tell("kept_ready")
                dve.wait_ge(S["nv_ps"], b + 1)
                for t in range(3):
                    did(ts(mult3[:, :, t], bcast[:, 1, 0:NT], float(t + 1), -float(t + 1), ALU.mult, ALU.add))
                tell("nv_read")
                did(ts(low3[:, :, :], mult3[:, :, :], 2, None, ALU.logical_shift_right))
                then(ts(frac3[:, :, :], mult3[:, :, :], 3, None, ALU.bitwise_and))
                did(v.tensor_copy(weight_old[:, :, :, :], weight[:, :, :, :]) if not (isinstance(b, int) and b == 0) else v.memset(weight_old[:, :, :, :], 0.0))
                did(ts(limit[:, :, :, 0], low3[:, :, :], 0.0, None, ALU.add))
                then(ts(limit[:, :, :, 1], low3[:, :, :], 1.0, None, ALU.add))
                for t in range(3):
                    did(ts(weight[:, :, t, 1], frac3[:, :, t], QW[t] / 4, None, ALU.mult))
                need(count[0])
                for t in range(3):
                    did(ts(weight[:, :, t, 0], weight[:, :, t, 1], -1.0, QW[t], ALU.mult, ALU.add))
                need(count[0])

            def hot_rows(l, u):
                dve.wait_ge(S["bc_ev"], UNITS * l + u + 1)
                if u >= 2:
                    dve.wait_ge(S["row_ps"], UNITS * l + u - 1)
                ts(hot[:, u % 2].rearrange(flat), near[:, u % 2, 0:2, :].rearrange(flat), iota_a[:, :], None, ALU.is_equal).then_inc(S["hot_ready"], 1)

            def value(l, u):
                dve.wait_ge(S["row_ps"], UNITS * l + u + 1)
                if u >= 2:
                    dve.wait_ge(S["found_ps"], UNITS * l + u - 1)
                stt(out=prod[:, u % 2, :], in0=near[:, u % 2, 2, :], scalar=iota_b[:, :], in1=rows[u % 2][:, :], op0=ALU.is_equal, op1=ALU.mult).then_inc(S["prod_ready"], 1)

            def add_up(l, k):
                dve.wait_ge(S["found_ps"], UNITS * l + GROUPS * (k + 1))
                for i in range(NT):
                    w = weight_old[:, i, k // 2, k % 2:k % 2 + 1]
                    if k == 0:
                        did(ts(agg[:, i, :], found[:, i, :], w, None, ALU.mult))
                    else:
                        did(stt(out=agg[:, i, :], in0=found[:, i, :], scalar=w, in1=agg[:, i, :], op0=ALU.mult, op1=ALU.add))
                tell("acc_done")

            def unit(l, u):
                if l is None:
                    return
                hot_rows(l, u)
                if u >= 1:
                    value(l, u - 1)
                if u % GROUPS == 2 and u > GROUPS:
                    add_up(l, u // GROUPS - 1)

            def select(b, i, l):
                u = PER_TILE * i
                if b is None:
                    for q in range(PER_TILE):
                        unit(l, u + q)
                    return
                W = words2[:, i % 2]
                dve.wait_ge(S["cw_ev"], NT * CW * b + CW * i + 2)
                did(v.tensor_copy(W[:, 0, 0:C], group_tag[:, 0, :]))
                did(tt(W[:, 0, C:], cnt[:, 0:(G - 1) * C], group_tag[:, 1:, :].rearrange(flat), ALU.add))
                for h in range(2):
                    for k in range(3):
                        q = 3 * h + k
                        did(ts(below[:, k, C:], cnt[:, :], limit[:, i, q // 2, q % 2:q % 2 + 1], -1.0, ALU.is_le, ALU.mult))
                    need(count[0])
                    if h == 1:
                        tell("tile_read")
                    unit(l, u + 6 * h)
                    if h == 0:
                        dve.wait_ge(S["cw_ev"], NT * CW * b + CW * i + CW)
                    then(tt(chosen[:, :, :], below[:, :, 0:G * C], below[:, :, C:], ALU.bitwise_xor))
                    unit(l, u + 6 * h + 1)
                    for w in range(3):
                        did(tt(picked[:, w], chosen[:, :, :], W[:, w, :].bitcast(I16).unsqueeze(1).to_broadcast([P, 3, G * C]), ALU.bitwise_and))
                        if w == 1:
                            unit(l, u + 6 * h + 2)
                    need(count[0])
                    if h == 1:
                        tell("tile_read")
                    unit(l, u + 6 * h + 3)
                    a = picked[:, :, :, :].rearrange("p w k n -> p (w k) n")
                    n = G * C // 2
                    while n > C:
                        then(tt(a[:, :, 0:n], a[:, :, 0:n], a[:, :, n:2 * n], ALU.bitwise_or))
                        if n == G * C // 2:
                            unit(l, u + 6 * h + 4)
                        n //= 2
                    for w in range(3):
                        did(tt(result[:, w, i, 3 * h:3 * h + 3, :].bitcast(I16), picked[:, w, :, 0:C], picked[:, w, :, C:2 * C], ALU.bitwise_or))
                    unit(l, u + 6 * h + 5)

            big = NT * K * C

            def r3(n):
                return result[:, n].rearrange("p t k c -> p (t k c)")

            pool9 = picked[:, :, :, :].rearrange("p w k n -> p (w k n)").bitcast(U16)
            more = chosen[:, :, :].rearrange(flat).bitcast(U16)
            tmp = [pool9[:, big * n:big * n + big] for n in range(6)] + [more[:, big * n:big * n + big] for n in range(2)] + [spare[:, :]]

            def pop(word, x2, x4, x8, t):
                then(ts(t, word, 1, 0x5555, ALU.logical_shift_right, ALU.bitwise_and))
                then(tt(x2, word, t, ALU.subtract))
                did(ts(t, x2, 2, 0x3333, ALU.logical_shift_right, ALU.bitwise_and))
                then(ts(x4, x2, 0x3333, None, ALU.bitwise_and))
                then(tt(x4, x4, t, ALU.add))
                then(ts(t, x4, 4, None, ALU.logical_shift_right))
                then(tt(t, t, x4, ALU.add))
                then(ts(x8, t, 0x0F0F, None, ALU.bitwise_and))

            cx, wl, wh = r3(0), r3(1), r3(2)
            x2, x4, x8, t, r, bit, sh, blk, t2 = tmp

            def bits_first():
                then(ts(t, cx, 1023, None, ALU.bitwise_and))
                rr = r.rearrange("p (q c) -> p q c", c=C)
                lim = limit[:, :, :, :].rearrange("p i t s -> p (i t s)").unsqueeze(2).to_broadcast([P, NT * K, C])
                then(tt(rr, lim, t.rearrange("p (q c) -> p q c", c=C), ALU.subtract))
                pop(wl, x2, x4, x8, t)
                did(ts(t, x8, 8, None, ALU.logical_shift_right))
                need(count[0])
                then(tt(t, t, x8, ALU.add))
                then(ts(t, t, 31, None, ALU.bitwise_and))
                then(tt(bit, r, t, ALU.is_ge))
                did(ts(blk, cx, 10, 1, ALU.logical_shift_right, ALU.logical_shift_left))
                then(tt(t, t, bit, ALU.mult))
                did(tt(wh, wl, wh, ALU.bitwise_xor))
                then(tt(r, r, t, ALU.subtract))
                then(ts(t.bitcast(I16), bit, -1.0, None, ALU.mult))
                did(tt(idx[:, 0].rearrange(flat), blk, bit, ALU.add))
                then(tt(t, t, wh, ALU.bitwise_and))
                then(tt(wl, wl, t, ALU.bitwise_xor))

            def bits_second():
                then(ts(t, x8, 255, None, ALU.bitwise_and))
                then(tt(bit, r, t, ALU.is_ge))
                did(tt(t, t, bit, ALU.mult))
                then(ts(sh, bit, 3, None, ALU.logical_shift_left))
                then(tt(r, r, t, ALU.subtract))
                for field, size in ((x4, 4), (x2, 2)):
                    then(tt(t, field, sh, ALU.logical_shift_right))
                    then(ts(t, t, 2 ** size - 1, None, ALU.bitwise_and))
                    then(tt(bit, r, t, ALU.is_ge))
                    did(tt(t, t, bit, ALU.mult))
                    then(ts(bit, bit, size // 2, None, ALU.logical_shift_left))
                    did(tt(r, r, t, ALU.subtract))
                    then(tt(sh, sh, bit, ALU.add))
                then(tt(t, wl, sh, ALU.logical_shift_right))
                then(ts(t, t, 1, None, ALU.bitwise_and))
                then(tt(bit, r, t, ALU.is_ge))
                then(tt(idx[:, 1].rearrange(flat), sh, bit, ALU.add))

            def norm_a():
                for i in range(NT):
                    did(v.bn_stats(stats[:, i, :], pre[:, i, :]))
                need(count[0])
                for i in range(NT):
                    did(v.bn_aggr(moments[:, i, :], stats[:, i, :]))
                need(count[0])
                then(ts(small[:, 14, :], moments[:, :, 1], EPS, None, ALU.add))
                tell("z_ready")

            def norm_b():
                then(v.reciprocal(inv[:, 0, :], inv[:, 0, :]))
                for i in range(NT):
                    did(ts(pre[:, i, :], pre[:, i, :], moments[:, i, 0:1], inv[:, 0, i:i + 1], ALU.subtract, ALU.mult))
                need(count[0])

            def ffn_start(l):
                value(l, UNITS - 1)
                add_up(l, K - 1)
                need(count[0])
                then(tt(scaled[:, :, :], xb(l), agg[:, :, :], ALU.add))
                tell("ffn_x")

            def ffn_end(l):
                dve.wait_ge(S["y_ps"], l + 1)
                for i in range(NT):
                    did(stt(out=pre[:, i, :], in0=ring[0][:, C * i:C * i + C], scalar=mask_t[:, i, bass.ds(l, 1)], in1=x_all[:, i, l, :], op0=ALU.mult, op1=ALU.add))
                need(count[0])
                norm_a()

            def gcn_start(l):
                dve.wait_ge(S["sd_ready"], 3 * l + 1)
                norm_b()
                tell("x1_ready")
                then(ts(small[:, 12, :], rowsum[:, l, :], 1.0, None, ALU.add))
                did(ts(small[:, 11, :], small[:, 12, :], 0.0, None, ALU.is_gt))
                then(ts(small[:, 13, :], small[:, 12, :], 1e-30, None, ALU.max))
                tell("z_ready")
                dve.wait_ge(S["sd_ready"], 3 * l + 2)
                then(v.reciprocal(inv[:, 1, :], inv[:, 1, :]))
                then(tt(inv[:, 1, :], inv[:, 1, :], small[:, 11, :], ALU.mult))
                dve.wait_ge(S["tr_ps"], l + 1)
                for i in range(NT):
                    did(ts(scaled[:, i, :], ring[0][:, C * i:C * i + C], inv[:, 1, i:i + 1], None, ALU.mult))
                need(count[0])
                split()
                tell("split_ready")

            def split():
                then(v.tensor_copy(split3[:, 0], scaled[:, :, :]))
                then(tt(agg[:, :, :], scaled[:, :, :], split3[:, 0], ALU.subtract))
                then(v.tensor_copy(split3[:, 1], agg[:, :, :]))
                then(tt(split3[:, 2], agg[:, :, :], split3[:, 1], ALU.subtract))

            def gcn_end(l):
                dve.wait_ge(S["g_ps"], NT * l + NT)
                then(tt(scaled[:, :, :].rearrange(flat), ring[1][:, 0:NT * C], scaled[:, :, :].rearrange(flat), ALU.add))
                for i in range(NT):
                    did(ts(scaled[:, i, :], scaled[:, i, :], inv[:, 1, i:i + 1], 0.0, ALU.mult, ALU.max))
                need(count[0])
                then(tt(pre[:, :, :], pre[:, :, :], scaled[:, :, :], ALU.add))
                norm_a()
                dve.wait_ge(S["sd_ready"], 3 * l + 3)
                norm_b()
                then(v.tensor_copy(xb(l), pre[:, :, :]))
                tell("g_read")

            def body(b, l):
                if b is not None:
                    graph(b)
                for i in range(NT):
                    select(b, i, l)
                need(count[0]) if count[0] else None
                if l is not None:
                    ffn_start(l)
                if b is not None:
                    bits_first()
                if l is not None:
                    ffn_end(l)
                if b is not None:
                    pop(wl, x2, x4, x8, t)
                if l is not None:
                    gcn_start(l)
                if b is not None:
                    bits_second()
                    tell("idx_ready")
                elif l is not None:
                    pass
                if l is not None:
                    gcn_end(l)
                if b is None:
                    pass
                restart()
                if b is not None:
                    pass

            body(0, None)
            with dve.Fori(1, B) as b:
                body(b, b - 1)
            dve.wait_ge(S["idxT_ev"], 6 * B)
            then(v.tensor_copy(weight_old[:, :, :, :], weight[:, :, :, :]))
            body(None, B - 1)

            for q in range(SLOTS):
                for t in (cur_t, mid_t, msg_t):
                    did(v.memset(t[q][C:C + 1, :], 1.0))
            tell("l1_done")
            for b in range(B):
                dve.wait_ge(S["bT_ps"], b + 1)
                did(v.bn_stats(bn_stat[:, b, :], bank[b % 2][0:C, 0, :]))
                tell("bn_read")
            then(v.bn_aggr(bn_mom[:, :], bn_stat[:, :, :].rearrange(flat)))
            then(ts(bn_s[:, 0:1], bn_mom[:, 1:2], EPS, None, ALU.add))
            tell("bn_var")
            dve.wait_ge(S["bn_dev"], 1)
            then(v.reciprocal(bn_s[:, 1:2], bn_s[:, 1:2]))
            then(tt(bn_s[:, 2:3], bn_s[:, 1:2], gamma_s[:, :], ALU.mult))
            then(tt(bn_s[:, 3:4], bn_s[:, 2:3], bn_mom[:, 0:1], ALU.mult))
            then(tt(bn_s[:, 3:4], beta_s[:, :], bn_s[:, 3:4], ALU.subtract))
            tell("bn_shift")
            did(ts(w2f_s[:, :], w2_s[:, :], bn_s[:, 2:3], None, ALU.mult))
            dve.wait_ge(S["b2f_ps"], 1)
            did(tt(b2f_s[:, :], bank[2][0:1, 0, 0:C], b2_s[:, :], ALU.add))
            dve.wait_ge(S["roots2"], 1)
            did(v.reciprocal(inv_root[:, :, :], root[:, :, :]))
            tell("w2f_ready")
            dve.wait_ge(S["w23_ready"], 2)
            v.engine_nop().then_inc(S["graph_done"], SLOTS)
            restart()

            def cut3(q):
                then(v.tensor_copy(cut[q][:, 0], scl[q][:, :, :]))
                then(tt(rest[q][:, :, :], scl[q][:, :, :], cut[q][:, 0], ALU.subtract))
                then(v.tensor_copy(cut[q][:, 1], rest[q][:, :, :]))
                then(tt(cut[q][:, 2], rest[q][:, :, :], cut[q][:, 1], ALU.subtract))

            def moments_of(q, src):
                for i in range(NT):
                    did(v.bn_stats(stat[q][:, i, :], src[:, i, :]))
                need(count[0])
                for i in range(NT):
                    did(v.bn_aggr(mom[q][:, i, :], stat[q][:, i, :]))
                need(count[0])

            with dve.Fori(0, B // SLOTS) as g0:
                b0 = g0 * SLOTS
                for q in range(SLOTS):
                    then(v.tensor_copy(cur[q][:, :, :], x_all[:, :, b0 + q, :]))
                    tell("cur_ready")
                for q in range(SLOTS):
                    dve.wait_ge(S["lin_ps"], b0 + q + 1)
                    did(v.tensor_copy(lin[q][:, :, :].rearrange(flat), bank[q][:, 1, 0:NT * C]))
                    for i in range(NT):
                        did(ts(scl[q][:, i, :], bank[q][:, 1, C * i:C * i + C], inv_root[:, b0 + q, i:i + 1], None, ALU.mult))
                    need(count[0])
                    cut3(q)
                    tell("cut_ready")
                for q in range(SLOTS):
                    dve.wait_ge(S["agg_ps"], b0 + q + 1)
                    for i in range(NT):
                        did(ts(rest[q][:, i, :], bank[q][:, 0, C * i:C * i + C], root[:, b0 + q, i:i + 1], None, ALU.mult))
                    need(count[0])
                    then(tt(lin[q][:, :, :], lin[q][:, :, :], rest[q][:, :, :], ALU.subtract))
                    then(stt(out=lin[q][:, :, :], in0=lin[q][:, :, :], scalar=0.01, in1=lin[q][:, :, :], op0=ALU.mult, op1=ALU.max))
                    then(tt(cur[q][:, :, :], cur[q][:, :, :], lin[q][:, :, :], ALU.add))
                    moments_of(q, cur[q])
                    then(ts(dev[q][:, 0, :], mom[q][:, :, 1], EPS, None, ALU.add))
                    tell("var_ready")
                for q in range(SLOTS):
                    dve.wait_ge(S["dev_ready"], b0 + q + 1)
                    then(v.reciprocal(dev[q][:, 1, :], dev[q][:, 1, :]))
                    for i in range(NT):
                        did(ts(cur[q][:, i, :], cur[q][:, i, :], mom[q][:, i, 0:1], dev[q][:, 1, i:i + 1], ALU.subtract, ALU.mult))
                    tell("x3_ready")
                for q in range(SLOTS):
                    dve.wait_ge(S["m2_ps"], b0 + q + 1)
                    then(ts(scl[q][:, :, :].rearrange(flat), bank[q][:, 1, 0:NT * C], 0.0, None, ALU.max))
                    cut3(q)
                    tell("cut2_ready")
                for q in range(SLOTS):
                    dve.wait_ge(S["rz_ready"], b0 + q + 1)
                    pieces = bank[q][:, :, :].rearrange("p k (i n) -> p (k i) n", i=2)
                    then(tt(scl[q][:, :, :], pieces[:, :, 3 * C:4 * C], gate[q][:, :, 0:C], ALU.mult))
                    then(tt(scl[q][:, :, :], pieces[:, :, 2 * C:3 * C], scl[q][:, :, :], ALU.add))
                    tell("cand_ready")
                for q in range(SLOTS):
                    dve.wait_ge(S["new_ready"], b0 + q + 1)
                    then(tt(rest[q][:, :, :], cur[q][:, :, :], cand[q][:, :, :], ALU.subtract))
                    then(tt(rest[q][:, :, :], rest[q][:, :, :], gate[q][:, :, C:2 * C], ALU.mult))
                    then(tt(cand[q][:, :, :], cand[q][:, :, :], rest[q][:, :, :], ALU.add))
                    then(tt(cur[q][:, :, :], cur[q][:, :, :], cand[q][:, :, :], ALU.add))
                    moments_of(q, cur[q])
                    did(v.tensor_copy(last_mom[:, 0, b0 + q, :], mom[q][:, :, 0]))
                    did(ts(last_mom[:, 1, b0 + q, :], mom[q][:, :, 1], EPS, None, ALU.add))
                    did(v.tensor_copy(x_all[:, :, b0 + q, :], cur[q][:, :, :]))
                    tell("graph_done")
                restart()
            v.engine_nop().then_inc(S["last_var"], 1)
            dve.wait_ge(S["last_dev_ready"], 1)
            then(v.reciprocal(last_dev[:, :, :], last_dev[:, :, :]))
            for i in range(NT):
                then(tt(x_all[:, i], x_all[:, i], last_mom[:, 0, :, i].unsqueeze(2).to_broadcast([P, B, C]), ALU.subtract))
                then(tt(x_all[:, i], x_all[:, i], last_dev[:, :, i].unsqueeze(2).to_broadcast([P, B, C]), ALU.mult))
                tell("tile_done")


_INS = ['x', 'adj', 'nodemask', 'L0_gnn_W1', 'L0_gnn_b1', 'L0_gnn_W2', 'L0_gnn_b2', 'L1_gnn_kernel', 'L2_gnn_gamma',
        'L2_gnn_beta', 'L2_gnn_W', 'L2_gnn_b', 'L3_gnn_W1', 'L3_gnn_b1', 'L3_gnn_W2', 'L3_gnn_b2', 'L3_gnn_W_ih',
        'L3_gnn_b_ih', 'L3_gnn_W_hh', 'L3_gnn_b_hh']
_OUTS = [((B, N, C), 'float32')]


def kernel(**inputs):
    import numpy as _np
    import concourse.bacc as _bacc
    from concourse import mybir as _mybir
    from concourse.bass_utils import run_bass_kernel_spmd as _run

    nc = _bacc.Bacc("TRN2", target_bir_lowering=False, num_devices=1)
    arrays, args = {}, []
    for name in _INS:
        a = _np.ascontiguousarray(inputs[name])
        if a.dtype.kind == "b":
            a = a.view(_np.uint8)
        arrays[f"in_{name}_dram"] = a
        args.append(nc.dram_tensor(f"in_{name}_dram", a.shape, _mybir.dt.from_np(a.dtype), kind="ExternalInput").ap())
    for i, (shape, dtype) in enumerate(_OUTS):
        dt = _mybir.dt.from_np(_np.dtype(dtype))
        args.append(nc.dram_tensor(f"out_{i}_dram", shape, dt, kind="ExternalOutput").ap())
    build(nc, *args)
    r = _run(nc, [arrays], core_ids=[0])
    return r.results[0]["out_0_dram"]
```

```python
from contextlib import ExitStack

import concourse.bass as bass
from concourse import mybir

ALU = mybir.AluOpType
ACT = mybir.ActivationFunctionType
DT = mybir.dt
F32, F16, BF16, U16, I16, I32, U8 = DT.float32, DT.float16, DT.bfloat16, DT.uint16, DT.int16, DT.int32, DT.uint8

B, N, C, H = 16, 512, 64, 128
P = 128
NT = N // P
PAIRS = B // 2
G = 16
SPAN = N // G
WORD = 16
NH = N // WORD
K = 6
TRIM, KEEP = 10, 2
QW = (0.25, 0.5, 0.25)
EPS = 1e-5
SLOTS = 4
CW = 6
GROUPS = C // 8
DEEP = 4
UNITS = K * GROUPS
PER_TILE = UNITS // NT
TURNS = K + K // 2


def comparators(n):
    p = n // 2
    while p:
        q, r, d = n // 2, 0, p
        while True:
            yield p, r, d
            if q == p:
                break
            d, q, r = q - p, q // 2, p
        p //= 2


def sides(t, p, r, d):
    m = sum(1 for i in range(r, N, 2 * p) if i + p + d <= N)
    low = t[:, :, 0:2 * p * m].rearrange("q a (m t w) -> q a m t w", t=2, w=p)[:, :, :, r // p, :]
    if r:
        high = t[:, :, r + d:r + d + 2 * p * m].rearrange("q a (m t w) -> q a m t w", t=2, w=p)[:, :, :, 0, :]
    else:
        high = t[:, :, 0:2 * p * m].rearrange("q a (m t w) -> q a m t w", t=2, w=p)[:, :, :, 1, :]
    return low, high, m


def staying(t, p, d):
    m = (d + p) // (2 * p)
    blocks = t.rearrange("q a (m t w) -> q a m t w", t=2, w=p)
    return blocks[:, :, 0:m, 0, :], blocks[:, :, N // (2 * p) - m:, 1, :]


def wait(eng, sem, value):
    if not isinstance(value, int) or value > 0:
        eng.wait_ge(sem, value)


def hold(eng, sem, value, passed):
    eng.wait_ge(sem, value)
    eng.sem_inc(passed, 1)


def build(nc, x_in, adj_in, mask_in, w0a, b0a, w0b, b0b, k1, gamma, beta, w2, b2,
          w3a, b3a, w3b, b3b, w_ih, b_ih, w_hh, b_hh, out):
    ctx = ExitStack()
    with ctx:
        def sb(name, shape, dt):
            return ctx.enter_context(nc.sbuf_tensor(name, shape, dt))

        def sem(name):
            return ctx.enter_context(nc.semaphore(name))

        parts_d = nc.dram_tensor("parts_d", [3, B, C, N], BF16, kind="Internal").ap()
        adjt_d = nc.dram_tensor("adjt_d", [B, P, NT, N], BF16, kind="Internal").ap()

        x_all = sb("x_all", [P, NT, B, C], F32)
        ident = sb("ident", [P, P], F32)
        identb = sb("identb", [P, P], BF16)
        rowsum = sb("rowsum", [P, B, NT], F32)
        mask_t = sb("mask_t", [P, NT, B], F32)
        stage_w = sb("stage_w", [P, 5, C], F32)
        ones_row = sb("ones_row", [1, P], F32)
        w0a_s = sb("w0a_s", [C, H], F32)
        b0a_s = sb("b0a_s", [H, 1], F32)
        w0b_s = sb("w0b_s", [H, C], F32)
        b0b_s = sb("b0b_s", [1, C], F32)
        k1_s = sb("k1_s", [C, C], F32)
        rank_t = sb("rank_t", [P, NT, B, C], F16)

        gamma_s = sb("gamma_s", [C, 1], F32)
        beta_s = sb("beta_s", [C, 1], F32)
        w2_s = sb("w2_s", [C, C], F32)
        b2_s = sb("b2_s", [1, C], F32)
        w3a_s = sb("w3a_s", [C, C], F32)
        b3a_s = sb("b3a_s", [C, 1], F32)
        w3b_s = sb("w3b_s", [C + 1, C], F32)
        wih_s = sb("wih_s", [C + 1, 3 * C], F32)
        whh_s = sb("whh_s", [C + 1, 3 * C], F32)

        with ExitStack() as bank_ctx:
            ring = [bank_ctx.enter_context(nc.psum_tensor(f"ring{i}", [P, 512], F32)) for i in range(2)]
            bcast = bank_ctx.enter_context(nc.psum_tensor("bcast", [P, 3, 512], F32))
            rows = [bank_ctx.enter_context(nc.psum_tensor(f"rows{i}", [P, 512], F32)) for i in range(2)]
            found = bank_ctx.enter_context(nc.psum_tensor("found", [P, NT, C], F32))
        bank = [ctx.enter_context(nc.psum_tensor(f"bank{i}", [P, 2, 512], F32)) for i in range(SLOTS)]

        sort_ctx = ExitStack()
        with sort_ctx:
            def ss(name, shape, dt):
                return sort_ctx.enter_context(nc.sbuf_tensor(name, shape, dt))

            keys = [ss(f"keys{n}", [P, PAIRS, N], F32) for n in range(2)]
            parts = ss("parts", [P, 3, PAIRS, N], BF16)
            steps, size = [], 0
            for p, r, d in comparators(N):
                m = sum(1 for i in range(r, N, 2 * p) if i + p + d <= N)
                steps.append((p, r, d, m, size))
                size += PAIRS * m * p
            rank_at = -(-size // 4) * 4 - 4 * PAIRS * N
            swapped = ss("swapped", [P, rank_at + 4 * PAIRS * N], U8)
            ranks = swapped[:, rank_at:].bitcast(F32).rearrange("p (a n) -> p a n", a=PAIRS)
            swap = ss("swap", [P, 2, PAIRS * N // 2], F16)
            delta = ss("delta", [P, PAIRS * N // 2], F16)
            perm = ss("perm", [P, PAIRS, N], F16)
            place = ss("place", [P, N], F32)
            mask_u = ss("mask_u", [B, N], U8)
            mask_f = ss("mask_f", [B, N], F32)

        outer = sb
        first_ctx = ExitStack()

        def sb(name, shape, dt):
            return first_ctx.enter_context(nc.sbuf_tensor(name, shape, dt))

        eye = sb("eye", [P, NT, N], BF16)
        upper = sb("upper", [P, N], BF16)
        group_end = sb("group_end", [P, G, C], F16)
        half_id = sb("half_id", [P, 2, G, C], F16)
        group_tag = sb("group_tag", [P, G, C], U16)
        one_u = sb("one_u", [P, C], U16)
        sel_a = sb("sel_a", [P, C * 32], BF16)
        sel_a2 = sb("sel_a2", [P, C * 32], BF16)
        eq_bias = sb("eq_bias", [P, 1], F32)
        sel_b = sb("sel_b", [P, P * 16], BF16)
        iota_p = sb("iota_p", [P, 1], I32)
        iota_m = sb("iota_m", [P, 2], I32)
        iota_a = sb("iota_a", [P, 1], F32)
        iota_b = sb("iota_b", [P, 1], F32)
        sum16 = sb("sum16", [P, 8], F32)
        ones_b = sb("ones_b", [P, 1], BF16)

        below = sb("below", [P, 3, G * C], I16)
        table = sb("table", [P, 3, 2 * GROUPS, C], BF16)
        adj_f = sb("adj_f", [P, NT, N], F32)
        adj_b = sb("adj_b", [P, NT, N], BF16)
        neigh = sb("neigh", [P, NT, N], BF16)
        adj_t = sb("adj_t", [P, NT, N], BF16)
        adj_l = sb("adj_l", [P, NT, N], BF16)
        neigh_t = sb("neigh_t", [P, NT, N], BF16)
        drop2 = sb("drop2", [P, N], BF16)
        drop1, kept_t = adj_b, neigh_t
        small = sb("small", [P, 16, NT], F32)
        small_u = sb("small_u", [P, 4, NT], U16)
        mult3 = sb("mult3", [P, NT, 3], U16)
        low3 = sb("low3", [P, NT, 3], U16)
        frac3 = sb("frac3", [P, NT, 3], U16)
        limit = sb("limit", [P, NT, 3, 2], F32)
        weight = sb("weight", [P, NT, 3, 2], F32)
        weight_old = sb("weight_old", [P, NT, 3, 2], F32)
        member = sb("member", [P, NT, 3, G * C], BF16)
        mtmp = sb("mtmp", [P, 4, C], U16)
        mpow = sb("mpow", [P, 2, C], F16)
        cnt2 = sb("cnt2", [P, 2, G * C], F16)
        words = sb("words", [P, 3, G * C], U16)
        change = sb("change", [P, 3, G * C], U16)
        picked = sb("picked", [P, 3, 3, G * C], I16)
        result = sb("result", [P, 3, NT, K, C], U16)
        spare = sb("spare", [P, NT * K * C], U16)
        idx = sb("idx", [P, NT, K, 2, C], BF16)
        idx_b = sb("idx_b", [P, NT, K * C], BF16)
        idx_t = sb("idx_t", [P, K, N], BF16)
        idx_bt = sb("idx_bt", [P, 3, N], BF16)
        near = sb("near", [P, DEEP, N], BF16)
        hot = sb("hot", [P, DEEP, 2, N], BF16)
        prod = sb("prod", [P, 2, N], F32)
        agg = sb("agg", [P, NT, C], F32)
        hid_t, feat_t = prod[:, 0, :], prod[0:C, 1, :]
        pre = sb("pre", [P, NT, C], F32)
        scaled = sb("scaled", [P, NT, C], F32)
        split3 = sb("split3", [P, 3, NT, C], BF16)
        stats = sb("stats", [P, NT, 6], F32)
        moments = sb("moments", [P, NT, 2], F32)
        inv = sb("inv", [P, 2, NT], F32)

        first_ctx.close()
        sb = outer

        def slots(name, shape, dt):
            return [sb(f"{name}{i}", shape, dt) for i in range(SLOTS)]

        adj_s = slots("adj_s", [P, NT, N], BF16)
        cur = slots("cur", [P, NT, C], F32)
        cur_t = slots("cur_t", [C + 1, N], F32)
        mid_t = slots("mid_t", [C + 1, N], F32)
        msg_t = slots("msg_t", [C + 1, N], F32)
        lin = slots("lin", [P, NT, C], F32)
        scl = slots("scl", [P, NT, C], F32)
        rest = slots("rest", [P, NT, C], F32)
        cut = slots("cut", [P, 3, NT, C], BF16)
        gate = slots("gate", [P, NT, 2 * C], F32)
        cand = slots("cand", [P, NT, C], F32)
        stat = slots("stat", [P, NT, 6], F32)
        mom = slots("mom", [P, NT, 2], F32)
        dev = slots("dev", [P, 2, NT], F32)
        bn_stat = sb("bn_stat", [C, B, 6], F32)
        bn_mom = sb("bn_mom", [C, 2], F32)
        bn_s = sb("bn_s", [C, 4], F32)
        w2f_s = sb("w2f_s", [C, C], F32)
        b2f_s = sb("b2f_s", [1, C], F32)
        root = sb("root", [P, B, NT], F32)
        inv_root = sb("inv_root", [P, B, NT], F32)
        last_mom = sb("last_mom", [P, 2, B, NT], F32)
        last_dev = sb("last_dev", [P, B, NT], F32)

        names = """x_loaded w_loaded const cdone xT_ps xT_ev step_done stay_done swap_ready swap_used parts_ready parts_out rank_ready
            rankT_ps rankT_ev mask_ready mT_ps adj_loaded adjb_ready adjT_ps adjT_ev adj_out neigh_ready neighT_ready nb_ps
            cnt_ps drop_ready rs_ps kept_ready nv_ps nv_read member_ready cw_ps cw_ev tile_read idx_ready idxT_ps idxT_ev
            table_in adjl_in bc_ps place_ps near_ready hot_ready row_ps prod_ready found_ps acc_done
            ffn_x fx_ps fx_ev h_ps h_ev y_ps z_ready sd_ready x1_ready tr_ps split_ready g_ps g_read
            dve_chain out_done fin sp_passed pe_passed w23_ready wT_ps l1_done bT_ps bn_read bn_var bn_dev bn_shift b2f_ps w2f_ready
            roots2 roots3 cur_ready xt_ps xt_ev lin_ps cut_ready agg_ps var_ready dev_ready x3_ready ht_ps ht_ev m1_ps m1_ev m2_ps cut2_ready
            msg_ps msg_ev gate_ps rz_ready cand_ready new_ready graph_done last_var last_dev_ready tile_done ones_made""".split()
        S = {n: sem(n) for n in names}
        adjs_in = [sem(f"adjs_in{q}") for q in range(SLOTS)]
        block = ctx.enter_context(nc.Block())
        flat = "p a b -> p (a b)"

        def xb(b):
            return x_all[:, :, b, :]

        @block.sync
        def _(sp):
            sp.dma_start(x_all[:, 0], x_in.rearrange("b (t p) c -> t p b c", p=P)[0]).then_inc(S["x_loaded"], 16)
            for t in range(1, NT):
                sp.dma_start(x_all[:, t], x_in.rearrange("b (t p) c -> t p b c", p=P)[t]).then_inc(S["x_loaded"], 16)
            for dst, src in ((w0a_s[:, :], w0a), (b0a_s[:, :], b0a.rearrange("(h o) -> h o", o=1)), (w0b_s[:, :], w0b),
                             (b0b_s[:, :], b0b.rearrange("(o c) -> o c", o=1)), (k1_s[:, :], k1), (mask_u[:, :], mask_in),
                             (gamma_s[:, :], gamma.rearrange("(c o) -> c o", o=1)), (beta_s[:, :], beta.rearrange("(c o) -> c o", o=1)),
                             (w2_s[:, :], w2), (b2_s[:, :], b2.rearrange("(o c) -> o c", o=1)), (w3a_s[:, :], w3a),
                             (b3a_s[:, :], b3a.rearrange("(c o) -> c o", o=1)), (w3b_s[0:C, :], w3b),
                             (w3b_s[C:C + 1, :], b3b.rearrange("(o c) -> o c", o=1)),
                             (stage_w[0:96, 0:2, :], w_ih.rearrange("(s p) c -> p s c", p=96)),
                             (stage_w[0:96, 2:4, :], w_hh.rearrange("(s p) c -> p s c", p=96)),
                             (wih_s[C:C + 1, :], b_ih.rearrange("(o c) -> o c", o=1)),
                             (whh_s[C:C + 1, :], b_hh.rearrange("(o c) -> o c", o=1))):
                sp.dma_start(dst, src).then_inc(S["w_loaded"], 16)
            for s in range(3):
                sp.wait_ge(S["parts_ready"], s + 1)
                for h in range(2):
                    sp.dma_start(parts_d[s].rearrange("(a h) c n -> h c a n", h=2)[h], parts[C * h:C * h + C, s]).then_inc(S["parts_out"], 16)

            def load_adj(b):
                sp.dma_start(adj_f[:, :, :], adj_in[b].rearrange("(t p) n -> p t n", p=P)).then_inc(S["adj_loaded"], 16)

            sp.wait_ge(S["parts_out"], 96)
            load_adj(0)

            def body(b, look):
                if look is not None:
                    if not (isinstance(look, int) and look == 0):
                        hold(sp, S["row_ps"], look * UNITS, S["sp_passed"])
                        hold(sp, S["g_ps"], look * NT, S["sp_passed"])
                    for q in range(4):
                        for s in range(3):
                            sp.dma_start(table[32 * q:32 * q + 32, s, :, 16 * q:16 * q + 16],
                                         parts_d[s, look].rearrange("(g q) (a e) -> q a g e", q=4, e=16)[q]).then_inc(S["table_in"], 16)
                    hold(sp, S["adj_out"], 16 * look + 16, S["sp_passed"])
                    sp.dma_start(adj_l[:, :, :], adjt_d[look]).then_inc(S["adjl_in"], 16)
                if b is not None:
                    hold(sp, S["adjT_ev"], NT * b + NT, S["sp_passed"])
                    sp.dma_start(adjt_d[b], adj_t[:, :, :]).then_inc(S["adj_out"], 16)
                    if not (isinstance(b, int) and b == B - 1):
                        hold(sp, S["adjb_ready"], NT * b + NT, S["sp_passed"])
                        load_adj(b + 1)

            body(0, None)
            sp.wait_ge(S["cdone"], 2)
            body(1, 0)
            with sp.Fori(2, B - 1) as b:
                body(b, b - 1)
            body(B - 1, B - 2)
            body(None, B - 1)
            sp.wait_ge(S["l1_done"], 1)
            with sp.Fori(0, B // SLOTS) as g0:
                b0 = g0 * SLOTS
                for q in range(SLOTS):
                    b = b0 + q
                    hold(sp, S["graph_done"], b + 1, S["sp_passed"])
                    sp.dma_start(adj_s[q][:, :, :], adjt_d[b]).then_inc(adjs_in[q], 16)
            for t in range(NT):
                sp.wait_ge(S["tile_done"], t + 1)
                sp.dma_start(out.rearrange("b (t p) c -> t p b c", p=P)[t], x_all[:, t]).then_inc(S["out_done"], 16)
            sp.wait_ge(S["out_done"], 64)

        @block.gpsimd
        def _(g):
            n = [0]

            def made(ins):
                ins.then_inc(S["const"], 1)
                n[0] += 1

            def here():
                g.wait_ge(S["const"], n[0])

            made(g.memset(ident[:, :], 0.0))
            made(g.iota(place[:, :], [[1, N]], base=0, channel_multiplier=0, allow_small_or_imprecise_dtypes=True))
            made(g.memset(ones_row[:, :], 1.0))
            here()
            made(g.affine_select(out=ident[:, :], in_=ident[:, :], compare_op=ALU.not_equal, fill=1.0, base=0,
                                 pattern=[[-1, P]], channel_multiplier=1))
            here()
            made(g.tensor_copy(identb[:, :], ident[:, :]))
            for a in range(PAIRS):
                made(g.tensor_copy(perm[:, a, :], place[:, :]))
            here()
            g.drain().then_inc(S["cdone"], 1)
            g.wait_ge(S["parts_out"], 96)
            made(g.memset(eye[:, :, :], 0.0))
            made(g.iota(iota_p[:, :], [[1, 1]], base=0, channel_multiplier=1))
            made(g.memset(upper[:, :], 1.0))
            made(g.iota(sel_a2[:, :], [[0, C], [2, 32]], base=-32, channel_multiplier=0, allow_small_or_imprecise_dtypes=True))
            made(g.memset(sel_a[:, :], -1.0))
            made(g.memset(sel_b[:, :], 1.0))
            made(g.memset(sum16[:, :], 1.0))
            made(g.memset(table[:, :, :, :], 0.0))
            made(g.memset(ones_b[:, :], 1.0))
            made(g.memset(below[:, :, (G - 1) * C:], -1.0))
            made(g.memset(one_u[:, :], 1.0))
            made(g.iota(group_end[:, :, :], [[SPAN, G], [0, C]], base=SPAN, channel_multiplier=0, allow_small_or_imprecise_dtypes=True))
            made(g.iota(half_id[:, :, :, :], [[1, 2], [2, G], [0, C]], base=0, channel_multiplier=0, allow_small_or_imprecise_dtypes=True))
            made(g.iota(group_tag[:, :, :], [[1024, G], [0, C]], base=0, channel_multiplier=0, allow_small_or_imprecise_dtypes=True))
            here()
            made(g.affine_select(out=eye[:, :, :], in_=eye[:, :, :], compare_op=ALU.not_equal, fill=1.0, base=0,
                                 pattern=[[P, NT], [-1, N]], channel_multiplier=1))
            made(g.affine_select(out=upper[:, :], in_=upper[:, :], compare_op=ALU.is_ge, fill=0.0, base=0,
                                 pattern=[[1, N]], channel_multiplier=-1))
            made(g.affine_select(out=sel_a2[:, :], in_=sel_a2[:, :], compare_op=ALU.is_ge, fill=0.0, base=0,
                                 pattern=[[1, C * 32]], channel_multiplier=-32))
            made(g.affine_select(out=sel_a[:, :], in_=sel_a[:, :], compare_op=ALU.is_ge, fill=0.0, base=C * 32,
                                 pattern=[[1, C * 32]], channel_multiplier=-32))
            made(g.affine_select(out=sel_b[:, :], in_=sel_b[:, :], compare_op=ALU.is_ge, fill=0.0, base=0,
                                 pattern=[[1, P * 16]], channel_multiplier=-16))
            made(g.affine_select(out=sum16[:, :], in_=sum16[:, :], compare_op=ALU.is_ge, fill=0.0, base=0,
                                 pattern=[[-16, 8]], channel_multiplier=1))
            here()
            made(g.affine_select(out=sel_a2[:, :], in_=sel_a2[:, :], compare_op=ALU.is_ge, fill=0.0, base=31,
                                 pattern=[[-1, C * 32]], channel_multiplier=32))
            made(g.affine_select(out=sel_a[:, :], in_=sel_a[:, :], compare_op=ALU.is_ge, fill=0.0, base=31 - C * 32,
                                 pattern=[[-1, C * 32]], channel_multiplier=32))
            made(g.affine_select(out=sel_b[:, :], in_=sel_b[:, :], compare_op=ALU.is_ge, fill=0.0, base=15,
                                 pattern=[[-1, P * 16]], channel_multiplier=16))
            made(g.affine_select(out=sum16[:, :], in_=sum16[:, :], compare_op=ALU.is_ge, fill=0.0, base=15,
                                 pattern=[[16, 8]], channel_multiplier=-1))
            here()
            made(g.tensor_tensor(sel_a[:, :], sel_a[:, :], sel_a2[:, :], ALU.add))
            here()
            g.drain().then_inc(S["cdone"], 1)

        @block.tensor
        def _(pe):
            mm, tp = nc.tensor.matmul, nc.tensor.transpose
            pe.wait_ge(S["cdone"], 1)
            pe.wait_ge(S["x_loaded"], 16 * NT)
            for a in range(PAIRS):
                if a >= 2:
                    pe.wait_ge(S["xT_ev"], a - 1)
                for t in range(NT):
                    i = tp(ring[a % 2][:, P * t:P * t + P], x_all[:, t, 2 * a:2 * a + 2, :].rearrange(flat), ident[:, :])
                i.then_inc(S["xT_ps"], 1)
            pe.wait_ge(S["mask_ready"], 1)
            for t in range(NT):
                i = tp(bcast[:, 0, B * t:B * t + B], mask_f[:, P * t:P * t + P], ident[0:B, 0:B])
            i.then_inc(S["mT_ps"], 1)
            pe.wait_ge(S["rank_ready"], 1)
            for a in range(PAIRS):
                pe.wait_ge(S["rankT_ev"] if a >= 2 else S["xT_ev"], a - 1 if a >= 2 else PAIRS)
                for t in range(NT):
                    i = tp(ring[a % 2][:, P * t:P * t + P], ranks[:, a, P * t:P * t + P], ident[:, :])
                i.then_inc(S["rankT_ps"], 1)
            pe.wait_ge(S["cdone"], 2)

            def graph(b, l):
                for j in range(NT):
                    for i in range(NT):
                        if j == 0:
                            pe.wait_ge(S["adjb_ready"], NT * b + i + 1)
                        if i == 0 and j >= 2:
                            pe.wait_ge(S["adjT_ev"], NT * b + j - 1)
                        ins = tp(ring[j % 2][:, :].bitcast(BF16)[:, P * i:P * i + P], adj_b[:, i, P * j:P * j + P], identb[:, :])
                    ins.then_inc(S["adjT_ps"], 1)
                if l is not None:
                    spread(l, 0)
                    spread(l, 1)
                    lookup(l, 0)
                    lookup(l, 1)
                pe.wait_ge(S["neighT_ready"], b + 1)
                for i in range(NT):
                    for j in range(NT):
                        ins = mm(bcast[:, 0, i:i + 1], neigh_t[:, j, P * i:P * i + P], ones_b[:, :], start=(j == 0), stop=(j == NT - 1))
                ins.then_inc(S["nb_ps"], 1)
                for i in range(NT):
                    pe.wait_ge(S["adjT_ev"], NT * b + NT)
                    if i >= 2:
                        pe.wait_ge(S["drop_ready"], NT * b + i - 1)
                    for j in range(NT):
                        ins = mm(ring[i % 2][:, P * j:N], neigh_t[:, j, P * i:P * i + P], upper[:, 0:N - P * j], start=(j == 0), stop=(j == NT - 1))
                    ins.then_inc(S["cnt_ps"], 1)
                for j in range(NT):
                    pe.wait_ge(S["drop_ready"], NT * b + NT)
                    if j >= 2:
                        pe.wait_ge(S["kept_ready"], NT * b + j - 1)
                    mm(ring[j % 2][:, :], identb[:, :], drop1[:, j, :], start=True, stop=False)
                    for i in range(NT):
                        ins = mm(ring[j % 2][:, P * i:P * i + P], drop1[:, i, P * j:P * j + P], identb[:, :], start=False, stop=(i == NT - 1))
                    ins.then_inc(S["rs_ps"], 1)
                pe.wait_ge(S["kept_ready"], NT * b + NT)
                for i in range(NT):
                    for j in range(NT):
                        ins = mm(bcast[:, 1, i:i + 1], kept_t[:, j, P * i:P * i + P], ones_b[:, :], start=(j == 0), stop=(j == NT - 1))
                ins.then_inc(S["nv_ps"], 1)
                pe.wait_ge(S["member_ready"], NT * b + NT)

            def chunk(b, i, n):
                u = CW * i + n
                if u >= 2:
                    pe.wait_ge(S["cw_ev"], NT * CW * b + u - 1)
                for j in range(NT):
                    ins = mm(ring[u % 2][:, :], kept_t[:, j, P * i:P * i + P], member[:, j, n // 2, 512 * (n % 2):512 * (n % 2) + 512],
                             start=(j == 0), stop=(j == NT - 1))
                ins.then_inc(S["cw_ps"], 1)

            def spread(l, u):
                k, g8 = divmod(u, GROUPS)
                at, row = 32 * 8 * g8, (k % 2) * C + 8 * g8
                if u:
                    pe.wait_ge(S["near_ready"], UNITS * l + u)
                mm(bcast[:, 2, :], sel_b[:, 16 * row:16 * row + P], idx_bt[:, k // 2, :], start=True, stop=True).then_inc(S["place_ps"], 1)
                if u:
                    pe.wait_ge(S["hot_ready"], UNITS * l + u)
                mm(bcast[:, 0, :], sel_a[:, at:at + P], idx_t[:, k, :], start=True, stop=True)
                mm(bcast[:, 1, :], sel_a[:, at + P:at + 2 * P], idx_t[:, k, :], start=True, stop=True).then_inc(S["bc_ps"], 1)

            def lookup(l, u):
                k, g8 = divmod(u, GROUPS)
                if u == 0:
                    pe.wait_ge(S["table_in"], 192 * l + 192)
                pe.wait_ge(S["hot_ready"], UNITS * l + u + 1)
                if u >= 2:
                    pe.wait_ge(S["prod_ready"], UNITS * l + u - 1)
                for h in range(2):
                    for s in range(3):
                        ins = mm(rows[u % 2][C * h:C * h + C, :], table[:, s, 2 * g8 + h, :], hot[:, u % DEEP, h, :], start=(s == 0), stop=(s == 2))
                ins.then_inc(S["row_ps"], 1)

            def total(l, u):
                k, g8 = divmod(u, GROUPS)
                if g8 == 0 and k >= 1:
                    pe.wait_ge(S["acc_done"], K * l + k)
                pe.wait_ge(S["prod_ready"], UNITS * l + u + 1)
                for i in range(NT):
                    ins = mm(found[:, i, 8 * g8:8 * g8 + 8], prod[:, u % 2, P * i:P * i + P], sum16[:, :], start=True, stop=True)
                ins.then_inc(S["found_ps"], 1)

            def dense(l):
                hold(pe, S["ffn_x"], l + 1, S["pe_passed"])
                for i in range(NT):
                    ins = tp(ring[0][0:C, P * i:P * i + P], scaled[:, i, :], ident[:, :])
                ins.then_inc(S["fx_ps"], 1)
                pe.wait_ge(S["fx_ev"], 2 * l + 1)
                mm(ring[1][:, :], w0a_s[:, :], feat_t[:, :], start=True, stop=True).then_inc(S["h_ps"], 1)
                pe.wait_ge(S["h_ev"], l + 1)
                for i in range(NT):
                    mm(ring[0][:, C * i:C * i + C], hid_t[:, P * i:P * i + P], w0b_s[:, :], start=True, stop=False)
                    ins = mm(ring[0][:, C * i:C * i + C], ones_row[:, :], b0b_s[:, :], start=False, stop=True)
                ins.then_inc(S["y_ps"], 1)
                hold(pe, S["x1_ready"], l + 1, S["pe_passed"])
                for i in range(NT):
                    ins = tp(ring[1][0:C, P * i:P * i + P], pre[:, i, :], ident[:, :])
                ins.then_inc(S["fx_ps"], 1)
                pe.wait_ge(S["fx_ev"], 2 * l + 2)
                for i in range(NT):
                    ins = mm(ring[0][:, C * i:C * i + C], feat_t[:, P * i:P * i + P], k1_s[:, :], start=True, stop=True)
                ins.then_inc(S["tr_ps"], 1)
                pe.wait_ge(S["split_ready"], l + 1)
                pe.wait_ge(S["adjl_in"], 16 * l + 16)
                for i in range(NT):
                    for j in range(NT):
                        for s in range(3):
                            ins = mm(ring[1][:, C * i:C * i + C], adj_l[:, j, P * i:P * i + P], split3[:, s, j, :],
                                     start=(j == 0 and s == 0), stop=(j == NT - 1 and s == 2))
                    ins.then_inc(S["g_ps"], 1)

            def body(b, l):
                if b is not None:
                    graph(b, l)
                    for n in range(CW):
                        chunk(b, 0, n)
                    pe.wait_ge(S["nv_read"], b + 1)
                elif l is not None:
                    spread(l, 0)
                    spread(l, 1)
                    lookup(l, 0)
                    lookup(l, 1)
                for i in range(NT):
                    for q in range(PER_TILE):
                        u = PER_TILE * i + q
                        if b is not None and i + 1 < NT and q % 2 == 1:
                            chunk(b, i + 1, q // 2)
                        if l is not None:
                            if u + 2 < UNITS:
                                spread(l, u + 2)
                            if u >= 2:
                                lookup(l, u)
                            if u >= 2:
                                total(l, u - 2)
                if l is not None:
                    total(l, UNITS - 2)
                    total(l, UNITS - 1)
                    if b is not None:
                        pe.wait_ge(S["cw_ev"], NT * CW * b + NT * CW)
                    dense(l)
                if b is not None:
                    pe.wait_ge(S["idx_ready"], b + 1)
                    pe.wait_ge(S["cw_ev"], NT * CW * b + NT * CW)
                    if l is not None:
                        pe.wait_ge(S["g_read"], l + 1)
                    for u in range(TURNS):
                        if u >= 2:
                            pe.wait_ge(S["idxT_ev"], TURNS * b + u - 1)
                        for i in range(NT):
                            src = idx[:, i, u, :, :].rearrange(flat) if u < K else idx_b[:, i, P * (u - K):P * (u - K) + P]
                            ins = tp(ring[u % 2][:, :].bitcast(BF16)[:, P * i:P * i + P], src, identb[:, :])
                        ins.then_inc(S["idxT_ps"], 1)
                    pe.wait_ge(S["idxT_ev"], TURNS * b + TURNS)

            body(0, None)
            with pe.Fori(1, B) as b:
                body(b, b - 1)
            body(None, B - 1)

            pe.wait_ge(S["l1_done"], 1)
            for s in range(4):
                ins = tp(bank[0][0:C, 0, 96 * s:96 * s + 96], stage_w[0:96, s, :], ident[0:96, 0:96])
            ins.then_inc(S["wT_ps"], 1)
            pe.wait_ge(S["w23_ready"], 2)
            for b in range(B):
                if b >= 2:
                    pe.wait_ge(S["bn_read"], b - 1)
                for i in range(NT):
                    ins = tp(bank[b % 2][0:C, 0, P * i:P * i + P], x_all[:, i, b, :], ident[:, :])
                ins.then_inc(S["bT_ps"], 1)
            pe.wait_ge(S["bn_shift"], 1)
            mm(bank[2][0:1, 0, 0:C], bn_s[:, 3:4], w2_s[:, :], start=True, stop=True).then_inc(S["b2f_ps"], 1)
            pe.wait_ge(S["w2f_ready"], 1)

            def turn(q, k, src):
                for i in range(NT):
                    ins = tp(bank[q][0:C, k, P * i:P * i + P], src[:, i, :], ident[:, :])
                return ins

            with pe.Fori(0, B // SLOTS) as g0:
                b0 = g0 * SLOTS
                for q in range(SLOTS):
                    hold(pe, S["cur_ready"], b0 + q + 1, S["pe_passed"])
                    turn(q, 0, cur[q]).then_inc(S["xt_ps"], 1)
                for q in range(SLOTS):
                    pe.wait_ge(S["xt_ev"], b0 + q + 1)
                    for i in range(NT):
                        mm(bank[q][:, 1, C * i:C * i + C], cur_t[q][0:C, P * i:P * i + P], w2f_s[:, :], start=True, stop=False)
                        ins = mm(bank[q][:, 1, C * i:C * i + C], ones_row[:, :], b2f_s[:, :], start=False, stop=True)
                    ins.then_inc(S["lin_ps"], 1)
                for q in range(SLOTS):
                    pe.wait_ge(adjs_in[q], 16 * (g0 + 1))
                    pe.wait_ge(S["cut_ready"], b0 + q + 1)
                    for i in range(NT):
                        for j in range(NT):
                            for s in range(3):
                                ins = mm(bank[q][:, 0, C * i:C * i + C], adj_s[q][:, j, P * i:P * i + P], cut[q][:, s, j, :],
                                         start=(j == 0 and s == 0), stop=(j == NT - 1 and s == 2))
                    ins.then_inc(S["agg_ps"], 1)
                for q in range(SLOTS):
                    hold(pe, S["x3_ready"], b0 + q + 1, S["pe_passed"])
                    turn(q, 1, cur[q]).then_inc(S["ht_ps"], 1)
                for q in range(SLOTS):
                    hold(pe, S["ht_ev"], b0 + q + 1, S["pe_passed"])
                    mm(bank[q][0:C, 0, :], w3a_s[:, :], cur_t[q][0:C, :], start=True, stop=True).then_inc(S["m1_ps"], 1)
                for q in range(SLOTS):
                    pe.wait_ge(S["m1_ev"], b0 + q + 1)
                    for i in range(NT):
                        ins = mm(bank[q][:, 1, C * i:C * i + C], mid_t[q][:, P * i:P * i + P], w3b_s[:, :], start=True, stop=True)
                    ins.then_inc(S["m2_ps"], 1)
                for q in range(SLOTS):
                    pe.wait_ge(S["cut2_ready"], b0 + q + 1)
                    for j in range(NT):
                        for s in range(3):
                            ins = mm(bank[q][0:C, 0, :], cut[q][:, s, j, :], adj_s[q][:, j, :], start=(j == 0 and s == 0), stop=(j == NT - 1 and s == 2))
                    ins.then_inc(S["msg_ps"], 1)
                for q in range(SLOTS):
                    pe.wait_ge(S["msg_ev"], b0 + q + 1)
                    for i in range(NT):
                        dst = bank[q][:, i // 2, 256 * (i % 2):256 * (i % 2) + 256]
                        mm(dst[:, 0:3 * C], msg_t[q][:, P * i:P * i + P], wih_s[:, :], start=True, stop=False, skip_group_check=True)
                        mm(dst[:, 0:2 * C], cur_t[q][:, P * i:P * i + P], whh_s[:, 0:2 * C], start=False, stop=True, skip_group_check=True)
                        ins = mm(dst[:, 3 * C:4 * C], cur_t[q][:, P * i:P * i + P], whh_s[:, 2 * C:3 * C], start=True, stop=True, skip_group_check=True)
                    ins.then_inc(S["gate_ps"], 1)

        @block.scalar
        def _(act):
            run = nc.scalar.activation
            for a in range(PAIRS):
                act.wait_ge(S["xT_ps"], a + 1)
                run(keys[0][:, a, :], ring[a % 2][:, :], ACT.Copy).then_inc(S["xT_ev"], 1)
            act.wait_ge(S["w_loaded"], 16 * 18)
            run(mask_f[:, :], mask_u[:, :], ACT.Copy).then_inc(S["mask_ready"], 1)
            act.wait_ge(S["mT_ps"], 1)
            run(mask_t[:, :, :].rearrange(flat), bcast[:, 0, 0:NT * B], ACT.Copy).then_inc(S["mask_ready"], 1)
            stays = 0
            for n, (p, r, d, m, at) in enumerate(steps):
                if r:
                    act.wait_ge(S["step_done"], n)
                    wait(act, S["stay_done"], stays)
                    for src, dst in zip(staying(keys[n % 2], p, d), staying(keys[1 - n % 2], p, d)):
                        ins = run(dst, src, ACT.Copy)
                    ins.then_inc(S["stay_done"], 1)
                    stays += 1
            act.wait_ge(S["step_done"], len(steps))
            for e, (p, r, d, m, at) in enumerate(reversed(steps)):
                if e >= 2:
                    act.wait_ge(S["swap_used"], e - 1)
                run(swap[:, e % 2, 0:PAIRS * m * p], swapped[:, at:at + PAIRS * m * p], ACT.Copy).then_inc(S["swap_ready"], 1)
            for a in range(PAIRS):
                act.wait_ge(S["rankT_ps"], a + 1)
                run(rank_t[:, :, 2 * a:2 * a + 2, :].rearrange("p t b c -> p t (b c)"),
                    ring[a % 2][:, :].rearrange("p (t q) -> p t q", t=NT), ACT.Copy).then_inc(S["rankT_ev"], 1)

            def convert(b):
                act.wait_ge(S["adj_loaded"], 16 * b + 16)
                if not (isinstance(b, int) and b == 0):
                    act.wait_ge(S["rs_ps"], NT * b)
                else:
                    act.wait_ge(S["parts_out"], 96)
                for i in range(NT):
                    run(adj_b[:, i, :], adj_f[:, i, :], ACT.Copy, accum_out=rowsum[:, b, i:i + 1]).then_inc(S["adjb_ready"], 1)

            def graph(b):
                if not (isinstance(b, int) and b == 0):
                    act.wait_ge(S["adj_out"], 16 * b)
                for j in range(NT):
                    act.wait_ge(S["adjT_ps"], NT * b + j + 1)
                    run(adj_t[:, j, :], ring[j % 2][:, :].bitcast(BF16)[:, 0:N], ACT.Copy).then_inc(S["adjT_ev"], 1)

            def chunk(b, i, n):
                u = CW * i + n
                if n == 0 and i >= 2:
                    act.wait_ge(S["tile_read"], 2 * (NT * b + i - 1))
                if n == 2 and i >= 1:
                    act.wait_ge(S["tile_read"], 2 * (NT * b + i) - 1)
                act.wait_ge(S["cw_ps"], NT * CW * b + u + 1)
                dst = cnt2[:, i % 2, 512 * n:512 * n + 512] if n < 2 else words[:, n // 2, 512 * (n % 2):512 * (n % 2) + 512]
                run(dst, ring[u % 2][:, :], ACT.Copy).then_inc(S["cw_ev"], 1)

            def spread(l, u):
                act.wait_ge(S["place_ps"], UNITS * l + u + 1)
                if u >= DEEP:
                    act.wait_ge(S["prod_ready"], UNITS * l + u - DEEP + 1)
                run(near[:, u % DEEP], bcast[:, 2, :], ACT.Copy).then_inc(S["near_ready"], 1)
                act.wait_ge(S["bc_ps"], UNITS * l + u + 1)
                run(hot[:, u % DEEP].rearrange(flat), bcast[:, 0:2, :].rearrange(flat), ACT.Relu, bias=eq_bias[:, :]).then_inc(S["hot_ready"], 1)

            def dense(l):
                act.wait_ge(S["fx_ps"], 2 * l + 1)
                run(feat_t[:, :], ring[0][0:C, :], ACT.Copy).then_inc(S["fx_ev"], 1)
                act.wait_ge(S["h_ps"], l + 1)
                run(hid_t[:, :], ring[1][:, :], ACT.Relu, bias=b0a_s[:, :]).then_inc(S["h_ev"], 1)
                act.wait_ge(S["z_ready"], 3 * l + 1)
                run(inv[:, 0, :], small[:, 14, :], ACT.Sqrt).then_inc(S["sd_ready"], 1)
                act.wait_ge(S["z_ready"], 3 * l + 2)
                run(inv[:, 1, :], small[:, 13, :], ACT.Sqrt).then_inc(S["sd_ready"], 1)
                act.wait_ge(S["fx_ps"], 2 * l + 2)
                run(feat_t[:, :], ring[1][0:C, :], ACT.Copy).then_inc(S["fx_ev"], 1)
                act.wait_ge(S["z_ready"], 3 * l + 3)
                run(inv[:, 0, :], small[:, 14, :], ACT.Sqrt).then_inc(S["sd_ready"], 1)

            def body(b, l, more=True):
                if b is not None:
                    graph(b)
                if l is not None:
                    spread(l, 0)
                    spread(l, 1)
                if b is not None:
                    for n in range(CW):
                        chunk(b, 0, n)
                for i in range(NT):
                    for q in range(PER_TILE):
                        if b is not None and i + 1 < NT and q % 2 == 1:
                            chunk(b, i + 1, q // 2)
                        if l is not None:
                            u = PER_TILE * i + q
                            if u + 2 < UNITS:
                                spread(l, u + 2)
                if l is not None:
                    dense(l)
                if b is not None:
                    if more:
                        convert(b + 1)
                    for u in range(TURNS):
                        act.wait_ge(S["idxT_ps"], TURNS * b + u + 1)
                        run(idx_t[:, u, :] if u < K else idx_bt[:, u - K, :], ring[u % 2][:, :].bitcast(BF16)[:, 0:N], ACT.Copy).then_inc(S["idxT_ev"], 1)

            convert(0)
            body(0, None)
            with act.Fori(1, B - 1) as b:
                body(b, b - 1)
            body(B - 1, B - 2, more=False)
            body(None, B - 1)

            act.wait_ge(S["wT_ps"], 1)
            run(wih_s[0:C, :], bank[0][0:C, 0, 0:3 * C], ACT.Copy).then_inc(S["w23_ready"], 1)
            run(whh_s[0:C, :], bank[0][0:C, 0, 3 * C:6 * C], ACT.Copy).then_inc(S["w23_ready"], 1)
            run(root[:, :, :], rowsum[:, :, :], ACT.Sqrt).then_inc(S["roots2"], 1)
            act.wait_ge(S["bn_var"], 1)
            run(bn_s[:, 1:2], bn_s[:, 0:1], ACT.Sqrt).then_inc(S["bn_dev"], 1)
            with act.Fori(0, B // SLOTS) as g0:
                b0 = g0 * SLOTS
                for q in range(SLOTS):
                    act.wait_ge(S["xt_ps"], b0 + q + 1)
                    run(cur_t[q][0:C, :], bank[q][0:C, 0, :], ACT.Copy).then_inc(S["xt_ev"], 1)
                for q in range(SLOTS):
                    act.wait_ge(S["var_ready"], b0 + q + 1)
                    run(dev[q][:, 1, :], dev[q][:, 0, :], ACT.Sqrt).then_inc(S["dev_ready"], 1)
                for q in range(SLOTS):
                    act.wait_ge(S["ht_ps"], b0 + q + 1)
                    run(cur_t[q][0:C, :], bank[q][0:C, 1, :], ACT.Copy).then_inc(S["ht_ev"], 1)
                for q in range(SLOTS):
                    act.wait_ge(S["m1_ps"], b0 + q + 1)
                    run(mid_t[q][0:C, :], bank[q][0:C, 0, :], ACT.Relu, bias=b3a_s[:, :]).then_inc(S["m1_ev"], 1)
                for q in range(SLOTS):
                    act.wait_ge(S["msg_ps"], b0 + q + 1)
                    run(msg_t[q][0:C, :], bank[q][0:C, 0, :], ACT.Relu).then_inc(S["msg_ev"], 1)
                for q in range(SLOTS):
                    act.wait_ge(S["gate_ps"], b0 + q + 1)
                    run(gate[q][:, :, :], bank[q][:, :, :].rearrange("p k (i n) -> p (k i) n", i=2)[:, :, 0:2 * C], ACT.Sigmoid).then_inc(S["rz_ready"], 1)
                for q in range(SLOTS):
                    act.wait_ge(S["cand_ready"], b0 + q + 1)
                    run(cand[q][:, :, :], scl[q][:, :, :], ACT.Tanh).then_inc(S["new_ready"], 1)
            act.wait_ge(S["last_var"], 1)
            run(last_dev[:, :, :], last_mom[:, 1], ACT.Sqrt).then_inc(S["last_dev_ready"], 1)

        @block.vector
        def _(dve):
            v = nc.vector
            tt, ts, stt = v.tensor_tensor, v.tensor_scalar, v.scalar_tensor_tensor
            count = [0]

            def did(ins):
                ins.then_inc(S["dve_chain"], 1)
                count[0] += 1
                return count[0]

            def need(n):
                if n > 0:
                    dve.wait_ge(S["dve_chain"], n)

            def then(ins):
                need(did(ins))

            def restart():
                need(count[0])
                dve.sem_clear(S["dve_chain"])
                count[0] = 0

            def tell(name):
                need(count[0])
                v.engine_nop().then_inc(S[name], 1)

            dve.wait_ge(S["cdone"], 1)
            dve.wait_ge(S["xT_ev"], PAIRS)

            def apart(t, m, p):
                return t.rearrange("q (a m w) -> q a m w", a=PAIRS, w=p)

            stays = 0
            for n, (p, r, d, m, at) in enumerate(steps):
                lo, hi, _ = sides(keys[n % 2], p, r, d)
                new_lo, new_hi, _ = sides(keys[1 - n % 2], p, r, d)
                wait(dve, S["step_done"], n)
                wait(dve, S["stay_done"], stays)
                tt(apart(swapped[:, at:at + PAIRS * m * p], m, p), lo, hi, ALU.is_gt)
                tt(new_lo, lo, hi, ALU.min)
                tt(new_hi, lo, hi, ALU.max).then_inc(S["step_done"], 1)
                stays += 1 if r else 0
            dve.wait_ge(S["step_done"], len(steps))
            dve.wait_ge(S["stay_done"], stays)
            ordered = keys[len(steps) % 2]
            then(v.tensor_copy(parts[:, 0], ordered[:, :, :]))
            tell("parts_ready")
            then(tt(ordered[:, :, :], ordered[:, :, :], parts[:, 0], ALU.subtract))
            then(v.tensor_copy(parts[:, 1], ordered[:, :, :]))
            tell("parts_ready")
            then(tt(parts[:, 2], ordered[:, :, :], parts[:, 1], ALU.subtract))
            tell("parts_ready")
            for e, (p, r, d, m, at) in enumerate(reversed(steps)):
                plo, phi, _ = sides(perm, p, r, d)
                de, sw = apart(delta[:, 0:PAIRS * m * p], m, p), apart(swap[:, e % 2, 0:PAIRS * m * p], m, p)
                need(count[0])
                then(tt(de, phi, plo, ALU.subtract))
                dve.wait_ge(S["swap_ready"], e + 1)
                tt(de, de, sw, ALU.mult).then_inc(S["swap_used"], 1)
                dve.wait_ge(S["swap_used"], e + 1)
                did(tt(plo, plo, de, ALU.add))
                did(tt(phi, phi, de, ALU.subtract))
            need(count[0])
            then(v.tensor_copy(ranks, perm[:, :, :]))
            tell("rank_ready")
            dve.wait_ge(S["cdone"], 2)
            did(ts(iota_m[:, 0:1], iota_p[:, :], 31, None, ALU.bitwise_and))
            then(ts(iota_m[:, 1:2], iota_p[:, :], 15, None, ALU.bitwise_and))
            did(v.tensor_copy(iota_a[:, :], iota_m[:, 0:1]))
            then(v.tensor_copy(iota_b[:, :], iota_m[:, 1:2]))
            then(ts(iota_a[:, :], iota_a[:, :], -16.0, None, ALU.add))
            then(tt(iota_a[:, :], iota_a[:, :], iota_a[:, :], ALU.mult))
            then(ts(eq_bias[:, :], iota_a[:, :], -1.0, 1.0, ALU.mult, ALU.add))
            dve.wait_ge(S["mask_ready"], 2)
            dve.wait_ge(S["rankT_ev"], PAIRS)
            restart()

            def members(b, j):
                if j == 0 and not (isinstance(b, int) and b == 0):
                    dve.wait_ge(S["cw_ps"], NT * CW * b)
                if j:
                    dve.wait_ge(S["member_ready"], NT * b + j)
                r = rank_t[:, j, b, :]
                spread_r = r.unsqueeze(1).to_broadcast([P, G, C])
                did(tt(member[:, j, 0, :].rearrange("p (g c) -> p g c", g=G), spread_r, group_end[:, :, :], ALU.is_lt))
                then(v.tensor_copy(mtmp[:, 0, :], r))
                did(ts(mtmp[:, 1, :], mtmp[:, 0, :], 4, None, ALU.logical_shift_right))
                then(ts(mtmp[:, 2, :], mtmp[:, 0, :], WORD - 1, None, ALU.bitwise_and))
                did(v.tensor_copy(mpow[:, 0, :], mtmp[:, 1, :]))
                then(tt(mtmp[:, 3, :], one_u[:, :], mtmp[:, 2, :], ALU.logical_shift_left))
                halves = member[:, j, 1:3, :].rearrange("p s (g c) -> p (s g) c", g=G)
                then(tt(halves, mpow[:, 0, :].unsqueeze(1).to_broadcast([P, 2 * G, C]), half_id[:, :, :, :].rearrange("p s g c -> p (s g) c"), ALU.is_equal))
                tt(halves, halves, mtmp[:, 3, :].unsqueeze(1).to_broadcast([P, 2 * G, C]), ALU.mult).then_inc(S["member_ready"], 1)

            nb, en, f1, f2, s1, s2 = (small[:, n, :] for n in range(6))

            def graph(b):
                members(b, 0)
                dve.wait_ge(S["adjb_ready"], NT * b + NT)
                then(tt(neigh[:, :, :], adj_b[:, :, :], eye[:, :, :], ALU.is_gt))
                dve.wait_ge(S["adjT_ev"], NT * b + NT)
                then(tt(neigh_t[:, :, :], adj_t[:, :, :], eye[:, :, :], ALU.is_gt))
                tell("neighT_ready")
                members(b, 1)
                members(b, 2)
                dve.wait_ge(S["nb_ps"], b + 1)
                did(ts(en, bcast[:, 0, 0:NT], float(TRIM), None, ALU.is_gt))
                then(ts(small_u[:, 0, :], bcast[:, 0, 0:NT], 1.0, None, ALU.add))
                did(tt(en, en, mask_t[:, :, b], ALU.mult))
                then(ts(small_u[:, 1, :], small_u[:, 0, :], 1, None, ALU.logical_shift_right))
                did(ts(f1, small_u[:, 1, :], 1.0, None, ALU.add))
                then(ts(f2, small_u[:, 1, :], 2.0, 1.0, ALU.mult, ALU.add))
                did(tt(f1, f1, en, ALU.mult))
                then(tt(f2, f2, en, ALU.mult))
                did(ts(s1, f1, -1.0, None, ALU.add))
                then(ts(s2, f2, -1.0, None, ALU.add))
                for i in range(NT):
                    dve.wait_ge(S["cnt_ps"], NT * b + i + 1)
                    if i:
                        dve.wait_ge(S["drop_ready"], NT * b + i)
                    did(stt(out=drop1[:, i, :], in0=ring[i % 2][:, :], scalar=s1[:, i:i + 1], in1=neigh[:, i, :], op0=ALU.is_equal, op1=ALU.mult))
                    then(stt(out=drop2[:, :], in0=ring[i % 2][:, :], scalar=s2[:, i:i + 1], in1=neigh[:, i, :], op0=ALU.is_equal, op1=ALU.mult))
                    tt(drop1[:, i, :], drop1[:, i, :], drop2[:, :], ALU.add).then_inc(S["drop_ready"], 1)
                members(b, 3)
                for j in range(NT):
                    dve.wait_ge(S["rs_ps"], NT * b + j + 1)
                    then(stt(out=kept_t[:, j, :], in0=ring[j % 2][:, :], scalar=0.0, in1=neigh_t[:, j, :], op0=ALU.is_equal, op1=ALU.mult))
                    tt(kept_t[:, j, P * j:P * j + P], kept_t[:, j, P * j:P * j + P], eye[:, j, P * j:P * j + P], ALU.add).then_inc(S["kept_ready"], 1)
                dve.wait_ge(S["nv_ps"], b + 1)
                for t in range(3):
                    did(ts(mult3[:, :, t], bcast[:, 1, 0:NT], float(t + 1), -float(t + 1), ALU.mult, ALU.add))
                tell("nv_read")
                did(ts(low3[:, :, :], mult3[:, :, :], 2, None, ALU.logical_shift_right))
                then(ts(frac3[:, :, :], mult3[:, :, :], 3, None, ALU.bitwise_and))
                did(v.tensor_copy(weight_old[:, :, :, :], weight[:, :, :, :]) if not (isinstance(b, int) and b == 0) else v.memset(weight_old[:, :, :, :], 0.0))
                did(ts(limit[:, :, :, 0], low3[:, :, :], 0.0, None, ALU.add))
                then(ts(limit[:, :, :, 1], low3[:, :, :], 1.0, None, ALU.add))
                for t in range(3):
                    did(ts(weight[:, :, t, 1], frac3[:, :, t], QW[t] / 4, None, ALU.mult))
                need(count[0])
                for t in range(3):
                    did(ts(weight[:, :, t, 0], weight[:, :, t, 1], -1.0, QW[t], ALU.mult, ALU.add))
                need(count[0])

            def value(l, u):
                dve.wait_ge(S["row_ps"], UNITS * l + u + 1)
                if u >= 2:
                    dve.wait_ge(S["found_ps"], UNITS * l + u - 1)
                stt(out=prod[:, u % 2, :], in0=near[:, u % DEEP, :], scalar=iota_b[:, :], in1=rows[u % 2][:, :], op0=ALU.is_equal, op1=ALU.mult).then_inc(S["prod_ready"], 1)

            def add_up(l, k):
                dve.wait_ge(S["found_ps"], UNITS * l + GROUPS * (k + 1))
                if k:
                    dve.wait_ge(S["acc_done"], K * l + k)
                for i in range(NT):
                    w = weight_old[:, i, k // 2, k % 2:k % 2 + 1]
                    if k == 0:
                        ins = ts(agg[:, i, :], found[:, i, :], w, None, ALU.mult)
                    else:
                        ins = stt(out=agg[:, i, :], in0=found[:, i, :], scalar=w, in1=agg[:, i, :], op0=ALU.mult, op1=ALU.add)
                ins.then_inc(S["acc_done"], 1)

            def unit(l, u):
                if l is None:
                    return
                value(l, u)
                if u % GROUPS == 1 and u > GROUPS:
                    add_up(l, u // GROUPS - 1)

            def select(b, i, l):
                u = PER_TILE * i
                if b is None:
                    for q in range(PER_TILE):
                        unit(l, u + q)
                    return
                cnt = cnt2[:, i % 2]
                dve.wait_ge(S["cw_ev"], NT * CW * b + CW * i + 2)
                did(v.tensor_copy(words[:, 0, 0:C], group_tag[:, 0, :]))
                did(tt(words[:, 0, C:], cnt[:, 0:(G - 1) * C], group_tag[:, 1:, :].rearrange(flat), ALU.add))
                need(count[0])
                last = (G - 1) * C
                for h in range(2):
                    for k in range(3):
                        q = 3 * h + k
                        ins = ts(below[:, k, 0:last], cnt[:, 0:last], limit[:, i, q // 2, q % 2:q % 2 + 1], -1.0, ALU.is_le, ALU.mult)
                    if h == 0:
                        did(ins)
                    else:
                        ins.then_inc(S["tile_read"], 1)
                    unit(l, u + 6 * h)
                    if h == 0:
                        dve.wait_ge(S["cw_ev"], NT * CW * b + CW * i + CW)
                        did(tt(change[:, :, 0:last], words[:, :, 0:last], words[:, :, C:], ALU.bitwise_xor))
                        v.tensor_copy(change[:, :, last:], words[:, :, 0:C]).then_inc(S["tile_read"], 1)
                    unit(l, u + 6 * h + 1)
                    dve.wait_ge(S["tile_read"], 2 * (NT * b + i) + h + 1)
                    for w in range(3):
                        did(tt(picked[:, w], below[:, :, :], change[:, w, :].bitcast(I16).unsqueeze(1).to_broadcast([P, 3, G * C]), ALU.bitwise_and))
                        if w == 1:
                            unit(l, u + 6 * h + 2)
                    need(count[0])
                    unit(l, u + 6 * h + 3)
                    a = picked[:, :, :, :].rearrange("p w k n -> p (w k) n")
                    n = G * C // 2
                    while n > C:
                        then(tt(a[:, :, 0:n], a[:, :, 0:n], a[:, :, n:2 * n], ALU.bitwise_xor))
                        if n == G * C // 2:
                            unit(l, u + 6 * h + 4)
                        n //= 2
                    for w in range(3):
                        did(tt(result[:, w, i, 3 * h:3 * h + 3, :].bitcast(I16), picked[:, w, :, 0:C], picked[:, w, :, C:2 * C], ALU.bitwise_xor))
                    unit(l, u + 6 * h + 5)

            big = NT * K * C

            def r3(n):
                return result[:, n].rearrange("p t k c -> p (t k c)")

            pool9 = picked[:, :, :, :].rearrange("p w k n -> p (w k n)").bitcast(U16)
            more = change[:, :, :].rearrange(flat)
            tmp = [pool9[:, big * n:big * n + big] for n in range(6)] + [more[:, big * n:big * n + big] for n in range(2)] + [spare[:, :]]

            def pop(word, x2, x4, x8, t):
                then(ts(t, word, 1, 0x5555, ALU.logical_shift_right, ALU.bitwise_and))
                then(tt(x2, word, t, ALU.subtract))
                did(ts(t, x2, 2, 0x3333, ALU.logical_shift_right, ALU.bitwise_and))
                then(ts(x4, x2, 0x3333, None, ALU.bitwise_and))
                then(tt(x4, x4, t, ALU.add))
                then(ts(t, x4, 4, None, ALU.logical_shift_right))
                then(tt(t, t, x4, ALU.add))
                then(ts(x8, t, 0x0F0F, None, ALU.bitwise_and))

            cx, wl, wh = r3(0), r3(1), r3(2)
            x2, x4, x8, t, r, bit, sh, blk, t2 = tmp

            def bits_first():
                then(ts(t, cx, 1023, None, ALU.bitwise_and))
                rr = r.rearrange("p (q c) -> p q c", c=C)
                lim = limit[:, :, :, :].rearrange("p i t s -> p (i t s)").unsqueeze(2).to_broadcast([P, NT * K, C])
                then(tt(rr, lim, t.rearrange("p (q c) -> p q c", c=C), ALU.subtract))
                pop(wl, x2, x4, x8, t)
                did(ts(t, x8, 8, None, ALU.logical_shift_right))
                need(count[0])
                then(tt(t, t, x8, ALU.add))
                then(ts(t, t, 31, None, ALU.bitwise_and))
                then(tt(bit, r, t, ALU.is_ge))
                did(ts(blk, cx, 10, 1, ALU.logical_shift_right, ALU.logical_shift_left))
                then(tt(t, t, bit, ALU.mult))
                did(tt(wh, wl, wh, ALU.bitwise_xor))
                then(tt(r, r, t, ALU.subtract))
                then(ts(t.bitcast(I16), bit, -1.0, None, ALU.mult))
                q3 = "p (q c) -> p q c"
                x16 = idx[:, :, :, 0, :].rearrange("p t k c -> p (t k) c")
                did(stt(out=x16, in0=blk.rearrange(q3, c=C), scalar=-16.0, in1=bit.rearrange(q3, c=C), op0=ALU.add, op1=ALU.add))
                then(tt(t, t, wh, ALU.bitwise_and))
                then(tt(wl, wl, t, ALU.bitwise_xor))
                did(tt(idx[:, :, :, 1, :].rearrange("p t k c -> p (t k) c"), x16, x16, ALU.mult))

            def bits_second():
                then(ts(t, x8, 255, None, ALU.bitwise_and))
                then(tt(bit, r, t, ALU.is_ge))
                did(tt(t, t, bit, ALU.mult))
                then(ts(sh, bit, 3, None, ALU.logical_shift_left))
                then(tt(r, r, t, ALU.subtract))
                for field, size in ((x4, 4), (x2, 2)):
                    then(tt(t, field, sh, ALU.logical_shift_right))
                    then(ts(t, t, 2 ** size - 1, None, ALU.bitwise_and))
                    then(tt(bit, r, t, ALU.is_ge))
                    did(tt(t, t, bit, ALU.mult))
                    then(ts(bit, bit, size // 2, None, ALU.logical_shift_left))
                    did(tt(r, r, t, ALU.subtract))
                    then(tt(sh, sh, bit, ALU.add))
                then(tt(t, wl, sh, ALU.logical_shift_right))
                then(ts(t, t, 1, None, ALU.bitwise_and))
                then(tt(bit, r, t, ALU.is_ge))
                then(tt(idx_b[:, :, :].rearrange(flat), sh, bit, ALU.add))

            def norm_a():
                for i in range(NT):
                    did(v.bn_stats(stats[:, i, :], pre[:, i, :]))
                need(count[0])
                for i in range(NT):
                    did(v.bn_aggr(moments[:, i, :], stats[:, i, :]))
                need(count[0])
                then(ts(small[:, 14, :], moments[:, :, 1], EPS, None, ALU.add))
                tell("z_ready")

            def norm_b():
                then(v.reciprocal(inv[:, 0, :], inv[:, 0, :]))
                for i in range(NT):
                    did(ts(pre[:, i, :], pre[:, i, :], moments[:, i, 0:1], inv[:, 0, i:i + 1], ALU.subtract, ALU.mult))
                need(count[0])

            def ffn_start(l):
                add_up(l, K - 1)
                dve.wait_ge(S["acc_done"], K * l + K)
                then(tt(scaled[:, :, :], xb(l), agg[:, :, :], ALU.add))
                tell("ffn_x")

            def ffn_end(l):
                dve.wait_ge(S["y_ps"], l + 1)
                for i in range(NT):
                    did(stt(out=pre[:, i, :], in0=ring[0][:, C * i:C * i + C], scalar=mask_t[:, i, bass.ds(l, 1)], in1=x_all[:, i, l, :], op0=ALU.mult, op1=ALU.add))
                need(count[0])
                norm_a()

            def gcn_start(l):
                dve.wait_ge(S["sd_ready"], 3 * l + 1)
                norm_b()
                tell("x1_ready")
                then(ts(small[:, 12, :], rowsum[:, l, :], 1.0, None, ALU.add))
                did(ts(small[:, 11, :], small[:, 12, :], 0.0, None, ALU.is_gt))
                then(ts(small[:, 13, :], small[:, 12, :], 1e-30, None, ALU.max))
                tell("z_ready")
                dve.wait_ge(S["sd_ready"], 3 * l + 2)
                then(v.reciprocal(inv[:, 1, :], inv[:, 1, :]))
                then(tt(inv[:, 1, :], inv[:, 1, :], small[:, 11, :], ALU.mult))
                dve.wait_ge(S["tr_ps"], l + 1)
                for i in range(NT):
                    did(ts(scaled[:, i, :], ring[0][:, C * i:C * i + C], inv[:, 1, i:i + 1], None, ALU.mult))
                need(count[0])
                split()
                tell("split_ready")

            def split():
                then(v.tensor_copy(split3[:, 0], scaled[:, :, :]))
                then(tt(agg[:, :, :], scaled[:, :, :], split3[:, 0], ALU.subtract))
                then(v.tensor_copy(split3[:, 1], agg[:, :, :]))
                then(tt(split3[:, 2], agg[:, :, :], split3[:, 1], ALU.subtract))

            def gcn_end(l):
                dve.wait_ge(S["g_ps"], NT * l + NT)
                then(tt(scaled[:, :, :].rearrange(flat), ring[1][:, 0:NT * C], scaled[:, :, :].rearrange(flat), ALU.add))
                for i in range(NT):
                    did(ts(scaled[:, i, :], scaled[:, i, :], inv[:, 1, i:i + 1], 0.0, ALU.mult, ALU.max))
                need(count[0])
                then(tt(pre[:, :, :], pre[:, :, :], scaled[:, :, :], ALU.add))
                norm_a()
                dve.wait_ge(S["sd_ready"], 3 * l + 3)
                norm_b()
                then(v.tensor_copy(xb(l), pre[:, :, :]))
                tell("g_read")

            def body(b, l):
                if b is not None:
                    graph(b)
                for i in range(NT):
                    select(b, i, l)
                need(count[0]) if count[0] else None
                if l is not None:
                    ffn_start(l)
                if b is not None:
                    bits_first()
                if l is not None:
                    ffn_end(l)
                if b is not None:
                    pop(wl, x2, x4, x8, t)
                if l is not None:
                    gcn_start(l)
                if b is not None:
                    bits_second()
                    tell("idx_ready")
                if l is not None:
                    gcn_end(l)
                restart()

            body(0, None)
            with dve.Fori(1, B) as b:
                body(b, b - 1)
            dve.wait_ge(S["idxT_ev"], TURNS * B)
            then(v.tensor_copy(weight_old[:, :, :, :], weight[:, :, :, :]))
            body(None, B - 1)

            for q in range(SLOTS):
                for t in (cur_t, mid_t, msg_t):
                    did(v.memset(t[q][C:C + 1, :], 1.0))
            tell("l1_done")
            for b in range(B):
                dve.wait_ge(S["bT_ps"], b + 1)
                did(v.bn_stats(bn_stat[:, b, :], bank[b % 2][0:C, 0, :]))
                tell("bn_read")
            then(v.bn_aggr(bn_mom[:, :], bn_stat[:, :, :].rearrange(flat)))
            then(ts(bn_s[:, 0:1], bn_mom[:, 1:2], EPS, None, ALU.add))
            tell("bn_var")
            dve.wait_ge(S["bn_dev"], 1)
            then(v.reciprocal(bn_s[:, 1:2], bn_s[:, 1:2]))
            then(tt(bn_s[:, 2:3], bn_s[:, 1:2], gamma_s[:, :], ALU.mult))
            then(tt(bn_s[:, 3:4], bn_s[:, 2:3], bn_mom[:, 0:1], ALU.mult))
            then(tt(bn_s[:, 3:4], beta_s[:, :], bn_s[:, 3:4], ALU.subtract))
            tell("bn_shift")
            did(ts(w2f_s[:, :], w2_s[:, :], bn_s[:, 2:3], None, ALU.mult))
            dve.wait_ge(S["b2f_ps"], 1)
            did(tt(b2f_s[:, :], bank[2][0:1, 0, 0:C], b2_s[:, :], ALU.add))
            dve.wait_ge(S["roots2"], 1)
            did(v.reciprocal(inv_root[:, :, :], root[:, :, :]))
            tell("w2f_ready")
            dve.wait_ge(S["w23_ready"], 2)
            v.engine_nop().then_inc(S["graph_done"], SLOTS)
            restart()

            def cut3(q):
                then(v.tensor_copy(cut[q][:, 0], scl[q][:, :, :]))
                then(tt(rest[q][:, :, :], scl[q][:, :, :], cut[q][:, 0], ALU.subtract))
                then(v.tensor_copy(cut[q][:, 1], rest[q][:, :, :]))
                then(tt(cut[q][:, 2], rest[q][:, :, :], cut[q][:, 1], ALU.subtract))

            def moments_of(q, src):
                for i in range(NT):
                    did(v.bn_stats(stat[q][:, i, :], src[:, i, :]))
                need(count[0])
                for i in range(NT):
                    did(v.bn_aggr(mom[q][:, i, :], stat[q][:, i, :]))
                need(count[0])

            with dve.Fori(0, B // SLOTS) as g0:
                b0 = g0 * SLOTS
                for q in range(SLOTS):
                    then(v.tensor_copy(cur[q][:, :, :], x_all[:, :, b0 + q, :]))
                    tell("cur_ready")
                for q in range(SLOTS):
                    dve.wait_ge(S["lin_ps"], b0 + q + 1)
                    did(v.tensor_copy(lin[q][:, :, :].rearrange(flat), bank[q][:, 1, 0:NT * C]))
                    for i in range(NT):
                        did(ts(scl[q][:, i, :], bank[q][:, 1, C * i:C * i + C], inv_root[:, b0 + q, i:i + 1], None, ALU.mult))
                    need(count[0])
                    cut3(q)
                    tell("cut_ready")
                for q in range(SLOTS):
                    dve.wait_ge(S["agg_ps"], b0 + q + 1)
                    for i in range(NT):
                        did(ts(rest[q][:, i, :], bank[q][:, 0, C * i:C * i + C], root[:, b0 + q, i:i + 1], None, ALU.mult))
                    need(count[0])
                    then(tt(lin[q][:, :, :], lin[q][:, :, :], rest[q][:, :, :], ALU.subtract))
                    then(stt(out=lin[q][:, :, :], in0=lin[q][:, :, :], scalar=0.01, in1=lin[q][:, :, :], op0=ALU.mult, op1=ALU.max))
                    then(tt(cur[q][:, :, :], cur[q][:, :, :], lin[q][:, :, :], ALU.add))
                    moments_of(q, cur[q])
                    then(ts(dev[q][:, 0, :], mom[q][:, :, 1], EPS, None, ALU.add))
                    tell("var_ready")
                for q in range(SLOTS):
                    dve.wait_ge(S["dev_ready"], b0 + q + 1)
                    then(v.reciprocal(dev[q][:, 1, :], dev[q][:, 1, :]))
                    for i in range(NT):
                        did(ts(cur[q][:, i, :], cur[q][:, i, :], mom[q][:, i, 0:1], dev[q][:, 1, i:i + 1], ALU.subtract, ALU.mult))
                    tell("x3_ready")
                for q in range(SLOTS):
                    dve.wait_ge(S["m2_ps"], b0 + q + 1)
                    then(ts(scl[q][:, :, :].rearrange(flat), bank[q][:, 1, 0:NT * C], 0.0, None, ALU.max))
                    cut3(q)
                    tell("cut2_ready")
                for q in range(SLOTS):
                    dve.wait_ge(S["rz_ready"], b0 + q + 1)
                    pieces = bank[q][:, :, :].rearrange("p k (i n) -> p (k i) n", i=2)
                    then(tt(scl[q][:, :, :], pieces[:, :, 3 * C:4 * C], gate[q][:, :, 0:C], ALU.mult))
                    then(tt(scl[q][:, :, :], pieces[:, :, 2 * C:3 * C], scl[q][:, :, :], ALU.add))
                    tell("cand_ready")
                for q in range(SLOTS):
                    dve.wait_ge(S["new_ready"], b0 + q + 1)
                    then(tt(rest[q][:, :, :], cur[q][:, :, :], cand[q][:, :, :], ALU.subtract))
                    then(tt(rest[q][:, :, :], rest[q][:, :, :], gate[q][:, :, C:2 * C], ALU.mult))
                    then(tt(cand[q][:, :, :], cand[q][:, :, :], rest[q][:, :, :], ALU.add))
                    then(tt(cur[q][:, :, :], cur[q][:, :, :], cand[q][:, :, :], ALU.add))
                    moments_of(q, cur[q])
                    did(v.tensor_copy(last_mom[:, 0, b0 + q, :], mom[q][:, :, 0]))
                    did(ts(last_mom[:, 1, b0 + q, :], mom[q][:, :, 1], EPS, None, ALU.add))
                    did(v.tensor_copy(x_all[:, :, b0 + q, :], cur[q][:, :, :]))
                    tell("graph_done")
                restart()
            v.engine_nop().then_inc(S["last_var"], 1)
            dve.wait_ge(S["last_dev_ready"], 1)
            then(v.reciprocal(last_dev[:, :, :], last_dev[:, :, :]))
            for i in range(NT):
                then(tt(x_all[:, i], x_all[:, i], last_mom[:, 0, :, i].unsqueeze(2).to_broadcast([P, B, C]), ALU.subtract))
                then(tt(x_all[:, i], x_all[:, i], last_dev[:, :, i].unsqueeze(2).to_broadcast([P, B, C]), ALU.mult))
                tell("tile_done")


_INS = ['x', 'adj', 'nodemask', 'L0_gnn_W1', 'L0_gnn_b1', 'L0_gnn_W2', 'L0_gnn_b2', 'L1_gnn_kernel', 'L2_gnn_gamma',
        'L2_gnn_beta', 'L2_gnn_W', 'L2_gnn_b', 'L3_gnn_W1', 'L3_gnn_b1', 'L3_gnn_W2', 'L3_gnn_b2', 'L3_gnn_W_ih',
        'L3_gnn_b_ih', 'L3_gnn_W_hh', 'L3_gnn_b_hh']
_OUTS = [((B, N, C), 'float32')]


def kernel(**inputs):
    import numpy as _np
    import concourse.bacc as _bacc
    from concourse import mybir as _mybir
    from concourse.bass_utils import run_bass_kernel_spmd as _run

    nc = _bacc.Bacc("TRN2", target_bir_lowering=False, num_devices=1)
    arrays, args = {}, []
    for name in _INS:
        a = _np.ascontiguousarray(inputs[name])
        if a.dtype.kind == "b":
            a = a.view(_np.uint8)
        arrays[f"in_{name}_dram"] = a
        args.append(nc.dram_tensor(f"in_{name}_dram", a.shape, _mybir.dt.from_np(a.dtype), kind="ExternalInput").ap())
    for i, (shape, dtype) in enumerate(_OUTS):
        dt = _mybir.dt.from_np(_np.dtype(dtype))
        args.append(nc.dram_tensor(f"out_{i}_dram", shape, dt, kind="ExternalOutput").ap())
    build(nc, *args)
    r = _run(nc, [arrays], core_ids=[0])
    return r.results[0]["out_0_dram"]
```

```python
from contextlib import ExitStack

import concourse.bass as bass
from concourse import mybir

ALU = mybir.AluOpType
ACT = mybir.ActivationFunctionType
DT = mybir.dt
F32, F16, BF16, U16, I16, I32, U8 = DT.float32, DT.float16, DT.bfloat16, DT.uint16, DT.int16, DT.int32, DT.uint8

B, N, C, H = 16, 512, 64, 128
P = 128
NT = N // P
PAIRS = B // 2
G = 16
SPAN = N // G
WORD = 16
NH = N // WORD
K = 6
TRIM, KEEP = 10, 2
QW = (0.25, 0.5, 0.25)
EPS = 1e-5
SLOTS = 4
CW = 6
GROUPS = C // 8
STEEP = 64.0
MASKS = 2 * NT - 1
DEEP = 4
UNITS = K * GROUPS
PER_TILE = UNITS // NT
TURNS = K + K // 2


def comparators(n):
    p = n // 2
    while p:
        q, r, d = n // 2, 0, p
        while True:
            yield p, r, d
            if q == p:
                break
            d, q, r = q - p, q // 2, p
        p //= 2


def sides(t, p, r, d):
    m = sum(1 for i in range(r, N, 2 * p) if i + p + d <= N)
    low = t[:, :, 0:2 * p * m].rearrange("q a (m t w) -> q a m t w", t=2, w=p)[:, :, :, r // p, :]
    if r:
        high = t[:, :, r + d:r + d + 2 * p * m].rearrange("q a (m t w) -> q a m t w", t=2, w=p)[:, :, :, 0, :]
    else:
        high = t[:, :, 0:2 * p * m].rearrange("q a (m t w) -> q a m t w", t=2, w=p)[:, :, :, 1, :]
    return low, high, m


def staying(t, p, d):
    m = (d + p) // (2 * p)
    blocks = t.rearrange("q a (m t w) -> q a m t w", t=2, w=p)
    return blocks[:, :, 0:m, 0, :], blocks[:, :, N // (2 * p) - m:, 1, :]


def wait(eng, sem, value):
    if not isinstance(value, int) or value > 0:
        eng.wait_ge(sem, value)


def hold(eng, sem, value, passed):
    eng.wait_ge(sem, value)
    eng.sem_inc(passed, 1)


def half(g, h):
    return [(q, g * SLOTS + q, g) for q in range(h * SLOTS // 2, (h + 1) * SLOTS // 2)]


def build(nc, x_in, adj_in, mask_in, w0a, b0a, w0b, b0b, k1, gamma, beta, w2, b2,
          w3a, b3a, w3b, b3b, w_ih, b_ih, w_hh, b_hh, out):
    ctx = ExitStack()
    with ctx:
        def sb(name, shape, dt):
            return ctx.enter_context(nc.sbuf_tensor(name, shape, dt))

        def sem(name):
            return ctx.enter_context(nc.semaphore(name))

        parts_d = nc.dram_tensor("parts_d", [3, B, C, N], BF16, kind="Internal").ap()
        adjt_d = nc.dram_tensor("adjt_d", [B, P, NT, N], BF16, kind="Internal").ap()

        x_all = sb("x_all", [P, NT, B, C], F32)
        ident = sb("ident", [P, P], F32)
        identb = sb("identb", [P, P], BF16)
        rowsum = sb("rowsum", [P, B, NT], F32)
        mask_t = sb("mask_t", [P, NT, B], F32)
        stage_w = sb("stage_w", [P, 5, C], F32)
        ones_row = sb("ones_row", [1, P], F32)
        w0a_s = sb("w0a_s", [C, H], F32)
        b0a_s = sb("b0a_s", [H, 1], F32)
        w0b_s = sb("w0b_s", [H, C], F32)
        b0b_s = sb("b0b_s", [1, C], F32)
        k1_s = sb("k1_s", [C, C], F32)
        rank_t = sb("rank_t", [P, NT, B, C], F16)

        gamma_s = sb("gamma_s", [C, 1], F32)
        beta_s = sb("beta_s", [C, 1], F32)
        w2_s = sb("w2_s", [C, C], F32)
        b2_s = sb("b2_s", [C + 1, C], F32)
        w3a_s = sb("w3a_s", [C, C], F32)
        b3a_s = sb("b3a_s", [C, 1], F32)
        w3b_s = sb("w3b_s", [C + 1, C], F32)
        wih_s = sb("wih_s", [C + 1, 3 * C], F32)
        whh_s = sb("whh_s", [C + 1, 3 * C], F32)

        with ExitStack() as bank_ctx:
            ring = [bank_ctx.enter_context(nc.psum_tensor(f"ring{i}", [P, 512], F32)) for i in range(2)]
            bcast = bank_ctx.enter_context(nc.psum_tensor("bcast", [P, 3, 512], F32))
            rows = [bank_ctx.enter_context(nc.psum_tensor(f"rows{i}", [P, 512], F32)) for i in range(2)]
            found_bank = bank_ctx.enter_context(nc.psum_tensor("found_bank", [P, 512], F32))
        found = found_bank[:, 0:NT * C].rearrange("p (t c) -> p t c", t=NT)
        nb_sum, nv_sum = (found_bank[:, NT * C + NT * n:NT * C + NT * n + NT] for n in range(2))
        bank = [ctx.enter_context(nc.psum_tensor(f"bank{i}", [P, 2, 512], F32)) for i in range(SLOTS)]

        sort_ctx = ExitStack()
        with sort_ctx:
            def ss(name, shape, dt):
                return sort_ctx.enter_context(nc.sbuf_tensor(name, shape, dt))

            keys = [ss(f"keys{n}", [P, PAIRS, N], F32) for n in range(2)]
            parts = ss("parts", [P, 3, PAIRS, N], BF16)
            steps, size = [], 0
            for p, r, d in comparators(N):
                m = sum(1 for i in range(r, N, 2 * p) if i + p + d <= N)
                steps.append((p, r, d, m, size))
                size += PAIRS * m * p
            rank_at = -(-size // 4) * 4 - 4 * PAIRS * N
            swapped = ss("swapped", [P, rank_at + 4 * PAIRS * N], U8)
            ranks = swapped[:, rank_at:].bitcast(F32).rearrange("p (a n) -> p a n", a=PAIRS)
            swap = ss("swap", [P, 2, PAIRS * N // 2], F16)
            delta = ss("delta", [P, PAIRS * N // 2], F16)
            perm = ss("perm", [P, PAIRS, N], F16)
            place = ss("place", [P, N], F32)
            mask_u = ss("mask_u", [B, N], U8)
            mask_f = ss("mask_f", [B, N], F32)

        outer = sb
        first_ctx = ExitStack()

        def sb(name, shape, dt):
            return first_ctx.enter_context(nc.sbuf_tensor(name, shape, dt))

        eye = sb("eye", [P, NT, N], BF16)
        upper = sb("upper", [P, N], BF16)
        group_end = sb("group_end", [P, G, C], F16)
        half_id = sb("half_id", [P, 2, G, C], F16)
        group_tag = sb("group_tag", [P, G, C], U16)
        one_u = sb("one_u", [P, C], U16)
        sel_a = sb("sel_a", [P, C * 32], BF16)
        eq_bias = sb("eq_bias", [P, 1], F32)
        sel_b = sb("sel_b", [P, P * 16], BF16)
        iota_p = sb("iota_p", [P, 1], I32)
        iota_m = sb("iota_m", [P, 2], I32)
        iota_a = sb("iota_a", [P, 1], F32)
        iota_b = sb("iota_b", [P, 1], F32)
        sum16 = sb("sum16", [P, 8], F32)
        ones_b = sb("ones_b", [P, 1], BF16)

        below = sb("below", [P, 2, 3, G * C], BF16)
        table = sb("table", [P, 3, 2 * GROUPS, C], BF16)
        adj_f = sb("adj_f", [P, NT, N], F32)
        adj_b = sb("adj_b", [P, NT, N], BF16)
        neigh = sb("neigh", [P, NT, N], BF16)
        adj_t = sb("adj_t", [P, NT, N], BF16)
        adj_l = sb("adj_l", [P, NT, N], BF16)
        neigh_t = sb("neigh_t", [P, NT, N], BF16)
        drop2 = sb("drop2", [P, N], BF16)
        drop1, kept_t = adj_b, neigh_t
        small = sb("small", [P, 16, NT], F32)
        small_u = sb("small_u", [P, 4, NT], U16)
        mult3 = sb("mult3", [P, NT, 3], U16)
        low3 = sb("low3", [P, NT, 3], U16)
        frac3 = sb("frac3", [P, NT, 3], U16)
        limit = sb("limit", [P, NT, 3, 2], F32)
        edge = sb("edge", [P, NT, 3, 2], F32)
        weight = sb("weight", [P, NT, 3, 2], F32)
        weight_old = sb("weight_old", [P, NT, 3, 2], F32)
        member = sb("member", [P, NT, 3, G * C], BF16)
        rank_u = sb("rank_u", [P, 2, NT, C], U16)
        half_of = sb("half_of", [P, NT, C], F16)
        cnt2 = sb("cnt2", [P, 2, G * C], F16)
        words = sb("words", [P, 3, G * C], U16)
        change = sb("change", [P, 3, G * C], U16)
        picked = sb("picked", [P, 3, 3, G * C], U16)
        result = sb("result", [P, 3, NT, K, C], U16)
        idx = sb("idx", [P, NT, K, 2, C], BF16)
        idx_b = sb("idx_b", [P, NT, K * C], BF16)
        idx_t = sb("idx_t", [P, K, N], BF16)
        idx_bt = sb("idx_bt", [P, 3, N], BF16)
        near = sb("near", [P, DEEP, N], BF16)
        hot = sb("hot", [P, DEEP, 2, N], BF16)
        prod = sb("prod", [P, 3, N], F32)
        agg = sb("agg", [P, NT, C], F32)
        hid_t, feat_t = prod[:, 0, :], prod[0:C, 1, :]
        pre = sb("pre", [P, NT, C], F32)
        scaled = sb("scaled", [P, NT, C], F32)
        split3 = near[:, 0:2, :].rearrange("p a n -> p (a n)")[:, 0:3 * NT * C].rearrange("p (s t c) -> p s t c", s=3, t=NT)
        stats = sb("stats", [P, NT, 6], F32)
        moments = sb("moments", [P, NT, 2], F32)
        inv = sb("inv", [P, 2, NT], F32)

        first_ctx.close()
        sb = outer

        def slots(name, shape, dt):
            return [sb(f"{name}{i}", shape, dt) for i in range(SLOTS)]

        adj_s = slots("adj_s", [P, NT, N], BF16)
        cur = slots("cur", [P, NT, C], F32)
        cur_t = slots("cur_t", [C + 1, N], F32)
        mid_t = slots("mid_t", [C + 1, N], F32)
        msg_t = slots("msg_t", [C + 1, N], F32)
        lin = slots("lin", [P, NT, C], F32)
        scl = slots("scl", [P, NT, C], F32)
        rest = slots("rest", [P, NT, C], F32)
        cut = slots("cut", [P, 3, NT, C], BF16)
        gate = slots("gate", [P, NT, 2 * C], F32)
        cand = slots("cand", [P, NT, C], F32)
        stat = slots("stat", [P, NT, 6], F32)
        mom = slots("mom", [P, NT, 2], F32)
        dev = slots("dev", [P, 2, NT], F32)
        bn_stat = sb("bn_stat", [C, B, 6], F32)
        bn_mom = sb("bn_mom", [C, 2], F32)
        bn_s = sb("bn_s", [C, 4], F32)
        w2f_s = sb("w2f_s", [C + 1, C], F32)
        root = sb("root", [P, B, NT], F32)
        inv_root = sb("inv_root", [P, B, NT], F32)
        last_mom = sb("last_mom", [P, 2, B, NT], F32)
        last_dev = sb("last_dev", [P, B, NT], F32)

        names = """x_loaded w_loaded const cdone xT_ps xT_ev step_done stay_done swap_ready swap_used parts_ready
            parts_out rank_ready rankT_ps rankT_ev mask_ready mT_ps adj_loaded adjb_ready adjT_ps adjT_ev adj_out
            neighT_ready nb_ps cnt_ps drop_ready rs_ps kept_ready nv_ps nv_read member_ready cw_ps cw_ev
            tile_read limit_ready mask_made mask_used idx_ready idxT_ps idxT_ev table_in adjl_in bc_ps place_ps
            near_ready hot_ready row_ps prod_ready found_ps acc_done ffn_x fx_ps fx_ev h_ps h_ev y_ps z_ready
            sd_ready x1_ready tr_ps split_ready g_ps dve_chain out_done sp_passed pe_passed w23_ready wT_ps
            l1_done bT_ps bn_read bn_var bn_dev bn_shift b2f_ps w2f_ready roots2 cur_ready xt_ps xt_ev lin_ps
            cut_ready agg_ps var_ready dev_ready x3_ready ht_ps ht_ev m1_ps m1_ev m2_ps cut2_ready msg_ps msg_ev
            gate_ps rz_ready cand_ready new_ready graph_done last_var last_dev_ready tile_done""".split()
        S = {n: sem(n) for n in names}
        adjs_in = [sem(f"adjs_in{q}") for q in range(SLOTS)]
        block = ctx.enter_context(nc.Block())
        flat = "p a b -> p (a b)"

        def xb(b):
            return x_all[:, :, b, :]

        @block.sync
        def _(sp):
            for t in range(0, NT, 2):
                sp.dma_start(x_all[:, t], x_in.rearrange("b (t p) c -> t p b c", p=P)[t]).then_inc(S["x_loaded"], 16)
            for dst, src in ((w0a_s[:, :], w0a), (b0a_s[:, :], b0a.rearrange("(h o) -> h o", o=1)), (w0b_s[:, :], w0b),
                             (b0b_s[:, :], b0b.rearrange("(o c) -> o c", o=1)), (k1_s[:, :], k1), (mask_u[:, :], mask_in),
                             (gamma_s[:, :], gamma.rearrange("(c o) -> c o", o=1)), (beta_s[:, :], beta.rearrange("(c o) -> c o", o=1)),
                             (w2_s[:, :], w2), (b2_s[C:C + 1, :], b2.rearrange("(o c) -> o c", o=1)), (w3a_s[:, :], w3a),
                             (b3a_s[:, :], b3a.rearrange("(c o) -> c o", o=1)), (w3b_s[0:C, :], w3b),
                             (w3b_s[C:C + 1, :], b3b.rearrange("(o c) -> o c", o=1)),
                             (stage_w[0:96, 0:2, :], w_ih.rearrange("(s p) c -> p s c", p=96)),
                             (stage_w[0:96, 2:4, :], w_hh.rearrange("(s p) c -> p s c", p=96)),
                             (wih_s[C:C + 1, :], b_ih.rearrange("(o c) -> o c", o=1)),
                             (whh_s[C:C + 1, :], b_hh.rearrange("(o c) -> o c", o=1))):
                sp.dma_start(dst, src).then_inc(S["w_loaded"], 16)
            for s in range(3):
                sp.wait_ge(S["parts_ready"], s + 1)
                for h in range(2):
                    sp.dma_start(parts_d[s].rearrange("(a h) c n -> h c a n", h=2)[h], parts[C * h:C * h + C, s]).then_inc(S["parts_out"], 16)

            def load_adj(b):
                sp.dma_start(adj_f[:, :, :], adj_in[b].rearrange("(t p) n -> p t n", p=P)).then_inc(S["adj_loaded"], 16)

            sp.wait_ge(S["parts_out"], 96)
            load_adj(0)

            def body(b, look):
                if look is not None:
                    if not (isinstance(look, int) and look == 0):
                        hold(sp, S["row_ps"], look * UNITS, S["sp_passed"])
                        hold(sp, S["g_ps"], look * NT, S["sp_passed"])
                    for q in range(4):
                        for s in range(3):
                            sp.dma_start(table[32 * q:32 * q + 32, s, :, 16 * q:16 * q + 16],
                                         parts_d[s, look].rearrange("(g q) (a e) -> q a g e", q=4, e=16)[q]).then_inc(S["table_in"], 16)
                    hold(sp, S["adj_out"], 16 * look + 16, S["sp_passed"])
                    sp.dma_start(adj_l[:, :, :], adjt_d[look]).then_inc(S["adjl_in"], 16)
                if b is not None:
                    hold(sp, S["adjT_ev"], NT * b + NT, S["sp_passed"])
                    sp.dma_start(adjt_d[b], adj_t[:, :, :]).then_inc(S["adj_out"], 16)
                    if not (isinstance(b, int) and b == B - 1):
                        hold(sp, S["adjb_ready"], NT * b + NT, S["sp_passed"])
                        load_adj(b + 1)

            body(0, None)
            sp.wait_ge(S["cdone"], 2)
            body(1, 0)
            with sp.Fori(2, B - 1) as b:
                body(b, b - 1)
            body(B - 1, B - 2)
            body(None, B - 1)
            sp.wait_ge(S["l1_done"], 1)
            with sp.Fori(0, B // SLOTS) as g0:
                b0 = g0 * SLOTS
                for q in range(SLOTS):
                    b = b0 + q
                    hold(sp, S["graph_done"], b + 1, S["sp_passed"])
                    sp.dma_start(adj_s[q][:, :, :], adjt_d[b]).then_inc(adjs_in[q], 16)
            for t in range(NT):
                sp.wait_ge(S["tile_done"], t + 1)
                sp.dma_start(out.rearrange("b (t p) c -> t p b c", p=P)[t], x_all[:, t]).then_inc(S["out_done"], 16)
            sp.wait_ge(S["out_done"], 64)

        @block.gpsimd
        def _(g):
            n = [0]

            def made(ins):
                ins.then_inc(S["const"], 1)
                n[0] += 1

            def here():
                g.wait_ge(S["const"], n[0])

            made(g.memset(ident[:, :], 0.0))
            made(g.iota(place[:, :], [[1, N]], base=0, channel_multiplier=0, allow_small_or_imprecise_dtypes=True))
            made(g.memset(ones_row[:, :], 1.0))
            here()
            made(g.affine_select(out=ident[:, :], in_=ident[:, :], compare_op=ALU.not_equal, fill=1.0, base=0,
                                 pattern=[[-1, P]], channel_multiplier=1))
            here()
            made(g.tensor_copy(identb[:, :], ident[:, :]))
            for a in range(PAIRS):
                made(g.tensor_copy(perm[:, a, :], place[:, :]))
            here()
            g.drain().then_inc(S["cdone"], 1)
            g.wait_ge(S["parts_out"], 96)
            made(g.memset(eye[:, :, :], 0.0))
            made(g.iota(iota_p[:, :], [[1, 1]], base=0, channel_multiplier=1))
            made(g.memset(upper[:, :], 1.0))
            sel_a2 = table[:, 0:2, :, :].rearrange("p s g c -> p (s g c)")
            made(g.iota(sel_a2, [[0, C], [2, 32]], base=-32, channel_multiplier=0, allow_small_or_imprecise_dtypes=True))
            made(g.memset(sel_a[:, :], -1.0))
            made(g.memset(sel_b[:, :], 1.0))
            made(g.memset(sum16[:, :], 1.0))
            made(g.memset(ones_b[:, :], 1.0))
            made(g.memset(below[:, :, :, (G - 1) * C:], 1.0))
            made(g.memset(one_u[:, :], 1.0))
            made(g.iota(group_end[:, :, :], [[SPAN, G], [0, C]], base=SPAN, channel_multiplier=0, allow_small_or_imprecise_dtypes=True))
            made(g.iota(half_id[:, :, :, :], [[1, 2], [2, G], [0, C]], base=0, channel_multiplier=0, allow_small_or_imprecise_dtypes=True))
            made(g.iota(group_tag[:, :, :], [[1024, G], [0, C]], base=0, channel_multiplier=0, allow_small_or_imprecise_dtypes=True))
            here()
            made(g.affine_select(out=eye[:, :, :], in_=eye[:, :, :], compare_op=ALU.not_equal, fill=1.0, base=0,
                                 pattern=[[P, NT], [-1, N]], channel_multiplier=1))
            made(g.affine_select(out=upper[:, :], in_=upper[:, :], compare_op=ALU.is_ge, fill=0.0, base=0,
                                 pattern=[[1, N]], channel_multiplier=-1))
            made(g.affine_select(out=sel_a2, in_=sel_a2, compare_op=ALU.is_ge, fill=0.0, base=0,
                                 pattern=[[1, C * 32]], channel_multiplier=-32))
            made(g.affine_select(out=sel_a[:, :], in_=sel_a[:, :], compare_op=ALU.is_ge, fill=0.0, base=C * 32,
                                 pattern=[[1, C * 32]], channel_multiplier=-32))
            made(g.affine_select(out=sel_b[:, :], in_=sel_b[:, :], compare_op=ALU.is_ge, fill=0.0, base=0,
                                 pattern=[[1, P * 16]], channel_multiplier=-16))
            made(g.affine_select(out=sum16[:, :], in_=sum16[:, :], compare_op=ALU.is_ge, fill=0.0, base=0,
                                 pattern=[[-16, 8]], channel_multiplier=1))
            here()
            made(g.affine_select(out=sel_a2, in_=sel_a2, compare_op=ALU.is_ge, fill=0.0, base=31,
                                 pattern=[[-1, C * 32]], channel_multiplier=32))
            made(g.affine_select(out=sel_a[:, :], in_=sel_a[:, :], compare_op=ALU.is_ge, fill=0.0, base=31 - C * 32,
                                 pattern=[[-1, C * 32]], channel_multiplier=32))
            made(g.affine_select(out=sel_b[:, :], in_=sel_b[:, :], compare_op=ALU.is_ge, fill=0.0, base=15,
                                 pattern=[[-1, P * 16]], channel_multiplier=16))
            made(g.affine_select(out=sum16[:, :], in_=sum16[:, :], compare_op=ALU.is_ge, fill=0.0, base=15,
                                 pattern=[[16, 8]], channel_multiplier=-1))
            here()
            made(g.tensor_tensor(sel_a[:, :], sel_a[:, :], sel_a2, ALU.add))
            here()
            made(g.memset(table[:, :, :, :], 0.0))
            here()
            g.drain().then_inc(S["cdone"], 1)

        @block.tensor
        def _(pe):
            mm, tp = nc.tensor.matmul, nc.tensor.transpose
            pe.wait_ge(S["cdone"], 1)
            pe.wait_ge(S["x_loaded"], 16 * NT)
            for a in range(PAIRS):
                if a >= 2:
                    pe.wait_ge(S["xT_ev"], a - 1)
                for t in range(NT):
                    i = tp(ring[a % 2][:, P * t:P * t + P], x_all[:, t, 2 * a:2 * a + 2, :].rearrange(flat), ident[:, :])
                i.then_inc(S["xT_ps"], 1)
            pe.wait_ge(S["mask_ready"], 1)
            for t in range(NT):
                i = tp(bcast[:, 0, B * t:B * t + B], mask_f[:, P * t:P * t + P], ident[0:B, 0:B])
            i.then_inc(S["mT_ps"], 1)
            pe.wait_ge(S["rank_ready"], 1)
            for a in range(PAIRS):
                pe.wait_ge(S["rankT_ev"] if a >= 2 else S["xT_ev"], a - 1 if a >= 2 else PAIRS)
                for t in range(NT):
                    i = tp(ring[a % 2][:, P * t:P * t + P], ranks[:, a, P * t:P * t + P], ident[:, :])
                i.then_inc(S["rankT_ps"], 1)
            pe.wait_ge(S["cdone"], 2)

            def turn_adj(b):
                for j in range(NT):
                    for i in range(NT):
                        if j == 0:
                            pe.wait_ge(S["adjb_ready"], NT * b + i + 1)
                        if i == 0 and j >= 2:
                            pe.wait_ge(S["adjT_ev"], NT * b + j - 1)
                        ins = tp(bcast[:, j % 2, :].bitcast(BF16)[:, P * i:P * i + P], adj_b[:, i, P * j:P * j + P], identb[:, :])
                    ins.then_inc(S["adjT_ps"], 1)

            def graph(b, l):
                pe.wait_ge(S["neighT_ready"], b + 1)
                for i in range(NT):
                    for j in range(NT):
                        ins = mm(nb_sum[:, i:i + 1], neigh_t[:, j, P * i:P * i + P], ones_b[:, :], start=(j == 0), stop=(j == NT - 1))
                ins.then_inc(S["nb_ps"], 1)
                for i in range(NT):
                    pe.wait_ge(S["adjT_ev"], NT * b + NT)
                    if i >= 2:
                        pe.wait_ge(S["drop_ready"], NT * b + i - 1)
                    for j in range(NT):
                        ins = mm(ring[i % 2][:, P * j:N], neigh_t[:, j, P * i:P * i + P], upper[:, 0:N - P * j], start=(j == 0), stop=(j == NT - 1))
                    ins.then_inc(S["cnt_ps"], 1)
                    if l is not None and i in (1, 2):
                        spread(l, i - 1)
                        lookup(l, i - 1)
                for j in range(NT):
                    pe.wait_ge(S["drop_ready"], NT * b + NT)
                    if j >= 2:
                        pe.wait_ge(S["kept_ready"], NT * b + j - 1)
                    mm(ring[j % 2][:, :], identb[:, :], drop1[:, j, :], start=True, stop=False)
                    for i in range(NT):
                        ins = mm(ring[j % 2][:, P * i:P * i + P], drop1[:, i, P * j:P * j + P], identb[:, :], start=False, stop=(i == NT - 1))
                    ins.then_inc(S["rs_ps"], 1)
                pe.wait_ge(S["kept_ready"], NT * b + NT)
                for i in range(NT):
                    for j in range(NT):
                        ins = mm(nv_sum[:, i:i + 1], kept_t[:, j, P * i:P * i + P], ones_b[:, :], start=(j == 0), stop=(j == NT - 1))
                ins.then_inc(S["nv_ps"], 1)
                pe.wait_ge(S["member_ready"], NT * b + NT)

            def chunk(b, i, n):
                u = CW * i + n
                if u >= 2:
                    pe.wait_ge(S["cw_ev"], NT * CW * b + u - 1)
                for j in range(NT):
                    ins = mm(ring[u % 2][:, :], kept_t[:, j, P * i:P * i + P], member[:, j, n // 2, 512 * (n % 2):512 * (n % 2) + 512],
                             start=(j == 0), stop=(j == NT - 1))
                ins.then_inc(S["cw_ps"], 1)

            def spread(l, u):
                k, g8 = divmod(u, GROUPS)
                at, row = 32 * 8 * g8, (k % 2) * C + 8 * g8
                if u:
                    pe.wait_ge(S["near_ready"], UNITS * l + u)
                mm(bcast[:, 2, :], sel_b[:, 16 * row:16 * row + P], idx_bt[:, k // 2, :], start=True, stop=True).then_inc(S["place_ps"], 1)
                if u:
                    pe.wait_ge(S["hot_ready"], UNITS * l + u)
                mm(bcast[:, 0, :], sel_a[:, at:at + P], idx_t[:, k, :], start=True, stop=True)
                mm(bcast[:, 1, :], sel_a[:, at + P:at + 2 * P], idx_t[:, k, :], start=True, stop=True).then_inc(S["bc_ps"], 1)

            def lookup(l, u):
                k, g8 = divmod(u, GROUPS)
                if u == 0:
                    pe.wait_ge(S["table_in"], 192 * l + 192)
                pe.wait_ge(S["hot_ready"], UNITS * l + u + 1)
                if u >= 2:
                    pe.wait_ge(S["prod_ready"], UNITS * l + u - 1)
                for h in range(2):
                    for s in range(3):
                        ins = mm(rows[u % 2][C * h:C * h + C, :], table[:, s, 2 * g8 + h, :], hot[:, u % DEEP, h, :], start=(s == 0), stop=(s == 2))
                ins.then_inc(S["row_ps"], 1)

            def total(l, u):
                k, g8 = divmod(u, GROUPS)
                if g8 == 0 and k >= 1:
                    pe.wait_ge(S["acc_done"], K * l + k)
                pe.wait_ge(S["prod_ready"], UNITS * l + u + 1)
                for i in range(NT):
                    ins = mm(found[:, i, 8 * g8:8 * g8 + 8], prod[:, u % 3, P * i:P * i + P], sum16[:, :], start=True, stop=True)
                ins.then_inc(S["found_ps"], 1)

            def dense(l):
                hold(pe, S["ffn_x"], l + 1, S["pe_passed"])
                for i in range(NT):
                    ins = tp(ring[0][0:C, P * i:P * i + P], scaled[:, i, :], ident[:, :])
                ins.then_inc(S["fx_ps"], 1)
                pe.wait_ge(S["fx_ev"], 2 * l + 1)
                mm(ring[1][:, :], w0a_s[:, :], feat_t[:, :], start=True, stop=True).then_inc(S["h_ps"], 1)
                pe.wait_ge(S["h_ev"], l + 1)
                for i in range(NT):
                    mm(ring[0][:, C * i:C * i + C], hid_t[:, P * i:P * i + P], w0b_s[:, :], start=True, stop=False)
                    ins = mm(ring[0][:, C * i:C * i + C], ones_row[:, :], b0b_s[:, :], start=False, stop=True)
                ins.then_inc(S["y_ps"], 1)
                hold(pe, S["x1_ready"], l + 1, S["pe_passed"])
                for i in range(NT):
                    ins = tp(ring[1][0:C, P * i:P * i + P], pre[:, i, :], ident[:, :])
                ins.then_inc(S["fx_ps"], 1)
                pe.wait_ge(S["fx_ev"], 2 * l + 2)
                for i in range(NT):
                    ins = mm(ring[0][:, C * i:C * i + C], feat_t[:, P * i:P * i + P], k1_s[:, :], start=True, stop=True)
                ins.then_inc(S["tr_ps"], 1)
                pe.wait_ge(S["split_ready"], l + 1)
                pe.wait_ge(S["adjl_in"], 16 * l + 16)
                for i in range(NT):
                    for j in range(NT):
                        for s in range(3):
                            ins = mm(ring[1][:, C * i:C * i + C], adj_l[:, j, P * i:P * i + P], split3[:, s, j, :],
                                     start=(j == 0 and s == 0), stop=(j == NT - 1 and s == 2))
                    ins.then_inc(S["g_ps"], 1)

            def body(b, l, more=True):
                if b is not None:
                    graph(b, l)
                    for n in range(CW):
                        chunk(b, 0, n)
                        if n == 1:
                            pe.wait_ge(S["nv_read"], b + 1)
                            if l is not None:
                                spread(l, 2)
                        if n == 3 and l is not None:
                            lookup(l, 2)
                            total(l, 0)
                    if l is not None:
                        spread(l, 3)
                        lookup(l, 3)
                elif l is not None:
                    spread(l, 0)
                    spread(l, 1)
                    lookup(l, 0)
                    lookup(l, 1)
                    spread(l, 2)
                    lookup(l, 2)
                    total(l, 0)
                    spread(l, 3)
                    lookup(l, 3)
                for i in range(NT):
                    for q in range(PER_TILE):
                        u = PER_TILE * i + q
                        if b is not None and i + 1 < NT and q % 2 == 1:
                            chunk(b, i + 1, q // 2)
                        if l is not None:
                            if u > 1 and u + 2 < UNITS:
                                spread(l, u + 2)
                            if u >= 4:
                                total(l, u - 3)
                                lookup(l, u)
                if l is not None:
                    total(l, UNITS - 3)
                    total(l, UNITS - 2)
                    total(l, UNITS - 1)
                    if b is not None:
                        pe.wait_ge(S["cw_ev"], NT * CW * b + NT * CW)
                    dense(l)
                if b is not None:
                    if more:
                        turn_adj(b + 1)
                    pe.wait_ge(S["idx_ready"], b + 1)
                    if more:
                        pe.wait_ge(S["adjT_ev"], NT * b + 2 * NT)
                    for u in range(TURNS):
                        if u >= 2:
                            pe.wait_ge(S["idxT_ev"], TURNS * b + u - 1)
                        for i in range(NT):
                            src = idx[:, i, u, :, :].rearrange(flat) if u < K else idx_b[:, i, P * (u - K):P * (u - K) + P]
                            ins = tp(bcast[:, u % 2, :].bitcast(BF16)[:, P * i:P * i + P], src, identb[:, :])
                        ins.then_inc(S["idxT_ps"], 1)
                    pe.wait_ge(S["idxT_ev"], TURNS * b + TURNS)

            turn_adj(0)
            body(0, None)
            with pe.Fori(1, B - 1) as b:
                body(b, b - 1)
            body(B - 1, B - 2, more=False)
            body(None, B - 1)

            pe.wait_ge(S["l1_done"], 1)
            for s in range(4):
                ins = tp(bank[0][0:C, 0, 96 * s:96 * s + 96], stage_w[0:96, s, :], ident[0:96, 0:96])
            ins.then_inc(S["wT_ps"], 1)
            pe.wait_ge(S["w23_ready"], 2)
            for b in range(B):
                if b >= 2:
                    pe.wait_ge(S["bn_read"], b - 1)
                for i in range(NT):
                    ins = tp(bank[b % 2][0:C, 0, P * i:P * i + P], x_all[:, i, b, :], ident[:, :])
                ins.then_inc(S["bT_ps"], 1)
            pe.wait_ge(S["bn_shift"], 1)
            mm(bank[2][C:C + 1, 0, 0:C], bn_s[:, 3:4], w2_s[:, :], start=True, stop=True).then_inc(S["b2f_ps"], 1)
            pe.wait_ge(S["w2f_ready"], 1)

            def turn(q, k, src):
                for i in range(NT):
                    ins = tp(bank[q][0:C, k, P * i:P * i + P], src[:, i, :], ident[:, :])
                return ins

            def stage(new, old):
                for q, b, g in old:
                    hold(pe, S["x3_ready"], b + 1, S["pe_passed"])
                    turn(q, 1, cur[q]).then_inc(S["ht_ps"], 1)
                for q, b, g in old:
                    hold(pe, S["ht_ev"], b + 1, S["pe_passed"])
                    mm(bank[q][0:C, 0, :], w3a_s[:, :], cur_t[q][0:C, :], start=True, stop=True).then_inc(S["m1_ps"], 1)
                for q, b, g in old:
                    pe.wait_ge(S["m1_ev"], b + 1)
                    for i in range(NT):
                        ins = mm(bank[q][:, 1, C * i:C * i + C], mid_t[q][:, P * i:P * i + P], w3b_s[:, :], start=True, stop=True)
                    ins.then_inc(S["m2_ps"], 1)
                for q, b, g in new:
                    hold(pe, S["cur_ready"], b + 1, S["pe_passed"])
                    turn(q, 0, cur[q]).then_inc(S["xt_ps"], 1)
                for q, b, g in new:
                    pe.wait_ge(S["xt_ev"], b + 1)
                    for i in range(NT):
                        ins = mm(bank[q][:, 1, C * i:C * i + C], cur_t[q][:, P * i:P * i + P], w2f_s[:, :], start=True, stop=True)
                    ins.then_inc(S["lin_ps"], 1)
                for q, b, g in old:
                    pe.wait_ge(S["cut2_ready"], b + 1)
                    for j in range(NT):
                        for s in range(3):
                            ins = mm(bank[q][0:C, 0, :], cut[q][:, s, j, :], adj_s[q][:, j, :], start=(j == 0 and s == 0), stop=(j == NT - 1 and s == 2))
                    ins.then_inc(S["msg_ps"], 1)
                for q, b, g in new:
                    pe.wait_ge(adjs_in[q], 16 * (g + 1))
                    pe.wait_ge(S["cut_ready"], b + 1)
                    for i in range(NT):
                        for j in range(NT):
                            for s in range(3):
                                ins = mm(bank[q][:, 0, C * i:C * i + C], adj_s[q][:, j, P * i:P * i + P], cut[q][:, s, j, :],
                                         start=(j == 0 and s == 0), stop=(j == NT - 1 and s == 2))
                    ins.then_inc(S["agg_ps"], 1)
                for q, b, g in old:
                    pe.wait_ge(S["msg_ev"], b + 1)
                    for i in range(NT):
                        dst = bank[q][:, i // 2, 256 * (i % 2):256 * (i % 2) + 256]
                        mm(dst[:, 0:3 * C], msg_t[q][:, P * i:P * i + P], wih_s[:, :], start=True, stop=False, skip_group_check=True)
                        mm(dst[:, 0:2 * C], cur_t[q][:, P * i:P * i + P], whh_s[:, 0:2 * C], start=False, stop=True, skip_group_check=True)
                        ins = mm(dst[:, 3 * C:4 * C], cur_t[q][:, P * i:P * i + P], whh_s[:, 2 * C:3 * C], start=True, stop=True, skip_group_check=True)
                    ins.then_inc(S["gate_ps"], 1)

            stage(half(0, 0), [])
            stage(half(0, 1), half(0, 0))
            with pe.Fori(1, B // SLOTS) as g0:
                stage(half(g0, 0), half(g0 - 1, 1))
                stage(half(g0, 1), half(g0, 0))
            stage([], half(B // SLOTS - 1, 1))

        @block.scalar
        def _(act):
            run = nc.scalar.activation
            for t in range(1, NT, 2):
                act.dma_start(x_all[:, t], x_in.rearrange("b (t p) c -> t p b c", p=P)[t]).then_inc(S["x_loaded"], 16)
            for a in range(PAIRS):
                act.wait_ge(S["xT_ps"], a + 1)
                run(keys[0][:, a, :], ring[a % 2][:, :], ACT.Copy).then_inc(S["xT_ev"], 1)
            act.wait_ge(S["w_loaded"], 16 * 18)
            run(mask_f[:, :], mask_u[:, :], ACT.Copy).then_inc(S["mask_ready"], 1)
            act.wait_ge(S["mT_ps"], 1)
            run(mask_t[:, :, :].rearrange(flat), bcast[:, 0, 0:NT * B], ACT.Copy).then_inc(S["mask_ready"], 1)
            stays = 0
            for n, (p, r, d, m, at) in enumerate(steps):
                if r:
                    act.wait_ge(S["step_done"], n)
                    wait(act, S["stay_done"], stays)
                    for src, dst in zip(staying(keys[n % 2], p, d), staying(keys[1 - n % 2], p, d)):
                        ins = run(dst, src, ACT.Copy)
                    ins.then_inc(S["stay_done"], 1)
                    stays += 1
            act.wait_ge(S["step_done"], len(steps))
            for e, (p, r, d, m, at) in enumerate(reversed(steps)):
                if e >= 2:
                    act.wait_ge(S["swap_used"], e - 1)
                run(swap[:, e % 2, 0:PAIRS * m * p], swapped[:, at:at + PAIRS * m * p], ACT.Copy).then_inc(S["swap_ready"], 1)
            for a in range(PAIRS):
                act.wait_ge(S["rankT_ps"], a + 1)
                run(rank_t[:, :, 2 * a:2 * a + 2, :].rearrange("p t b c -> p t (b c)"),
                    ring[a % 2][:, :].rearrange("p (t q) -> p t q", t=NT), ACT.Copy).then_inc(S["rankT_ev"], 1)

            def convert(b):
                act.wait_ge(S["adj_loaded"], 16 * b + 16)
                if not (isinstance(b, int) and b == 0):
                    act.wait_ge(S["rs_ps"], NT * b)
                else:
                    act.wait_ge(S["parts_out"], 96)
                for i in range(NT):
                    run(adj_b[:, i, :], adj_f[:, i, :], ACT.Copy, accum_out=rowsum[:, b, i:i + 1]).then_inc(S["adjb_ready"], 1)
                if not (isinstance(b, int) and b == 0):
                    act.wait_ge(S["adj_out"], 16 * b)
                for j in range(NT):
                    act.wait_ge(S["adjT_ps"], NT * b + j + 1)
                    run(adj_t[:, j, :], bcast[:, j % 2, :].bitcast(BF16)[:, 0:N], ACT.Copy).then_inc(S["adjT_ev"], 1)

            def chunk(b, i, n):
                u = CW * i + n
                if n == 0:
                    wait(act, S["tile_read"], NT * b + i - 1)
                    wait(act, S["mask_made"], MASKS * b + 2 * i - 2)
                if n == 2:
                    wait(act, S["tile_read"], NT * b + i)
                act.wait_ge(S["cw_ps"], NT * CW * b + u + 1)
                dst = cnt2[:, i % 2, 512 * n:512 * n + 512] if n < 2 else words[:, n // 2, 512 * (n % 2):512 * (n % 2) + 512]
                run(dst, ring[u % 2][:, :], ACT.Copy).then_inc(S["cw_ev"], 1)

            def mask(b, i, h, k):
                if k == 0:
                    act.wait_ge(S["limit_ready"], b + 1)
                    act.wait_ge(S["cw_ev"], NT * CW * b + CW * i + 2)
                    wait(act, S["mask_used"], 2 * (NT * b + i - 1) + h + 1)
                q = 3 * h + k
                ins = run(below[:, h, k, 0:(G - 1) * C], cnt2[:, i % 2, 0:(G - 1) * C], ACT.Sigmoid,
                          bias=edge[:, i, q // 2, q % 2:q % 2 + 1], scale=-STEEP)
                if k == 2:
                    ins.then_inc(S["mask_made"], 1)

            def spread(l, u):
                act.wait_ge(S["place_ps"], UNITS * l + u + 1)
                if u >= DEEP:
                    act.wait_ge(S["prod_ready"], UNITS * l + u - DEEP + 1)
                run(near[:, u % DEEP], bcast[:, 2, :], ACT.Copy).then_inc(S["near_ready"], 1)
                act.wait_ge(S["bc_ps"], UNITS * l + u + 1)
                run(hot[:, u % DEEP].rearrange(flat), bcast[:, 0:2, :].rearrange(flat), ACT.Relu, bias=eq_bias[:, :]).then_inc(S["hot_ready"], 1)

            def dense(l):
                act.wait_ge(S["fx_ps"], 2 * l + 1)
                run(feat_t[:, :], ring[0][0:C, :], ACT.Copy).then_inc(S["fx_ev"], 1)
                act.wait_ge(S["h_ps"], l + 1)
                run(hid_t[:, :], ring[1][:, :], ACT.Relu, bias=b0a_s[:, :]).then_inc(S["h_ev"], 1)
                act.wait_ge(S["z_ready"], 3 * l + 1)
                run(inv[:, 0, :], small[:, 14, :], ACT.Sqrt).then_inc(S["sd_ready"], 1)
                act.wait_ge(S["z_ready"], 3 * l + 2)
                run(inv[:, 1, :], small[:, 13, :], ACT.Sqrt).then_inc(S["sd_ready"], 1)
                act.wait_ge(S["fx_ps"], 2 * l + 2)
                run(feat_t[:, :], ring[1][0:C, :], ACT.Copy).then_inc(S["fx_ev"], 1)
                act.wait_ge(S["z_ready"], 3 * l + 3)
                run(inv[:, 0, :], small[:, 14, :], ACT.Sqrt).then_inc(S["sd_ready"], 1)

            def body(b, l, more=True):
                if l is not None:
                    spread(l, 0)
                    spread(l, 1)
                if b is not None:
                    for n in range(CW):
                        chunk(b, 0, n)
                        if n == 1 and l is not None:
                            spread(l, 2)
                elif l is not None:
                    spread(l, 2)
                if l is not None:
                    spread(l, 3)
                for i in range(NT):
                    for q in range(PER_TILE):
                        if b is not None and i + 1 < NT and q % 2 == 1:
                            chunk(b, i + 1, q // 2)
                        if b is not None and q in (0, 2, 4):
                            mask(b, i, 1, q // 2)
                        if b is not None and i + 1 < NT and q in (6, 8, 10):
                            mask(b, i + 1, 0, q // 2 - 3)
                        if l is not None:
                            u = PER_TILE * i + q
                            if u > 1 and u + 2 < UNITS:
                                spread(l, u + 2)
                if l is not None:
                    dense(l)
                if b is not None:
                    if more:
                        convert(b + 1)
                    for u in range(TURNS):
                        act.wait_ge(S["idxT_ps"], TURNS * b + u + 1)
                        run(idx_t[:, u, :] if u < K else idx_bt[:, u - K, :], bcast[:, u % 2, :].bitcast(BF16)[:, 0:N], ACT.Copy).then_inc(S["idxT_ev"], 1)

            convert(0)
            body(0, None)
            with act.Fori(1, B - 1) as b:
                body(b, b - 1)
            body(B - 1, B - 2, more=False)
            body(None, B - 1)

            act.wait_ge(S["wT_ps"], 1)
            run(wih_s[0:C, :], bank[0][0:C, 0, 0:3 * C], ACT.Copy).then_inc(S["w23_ready"], 1)
            run(whh_s[0:C, :], bank[0][0:C, 0, 3 * C:6 * C], ACT.Copy).then_inc(S["w23_ready"], 1)
            run(root[:, :, :], rowsum[:, :, :], ACT.Sqrt).then_inc(S["roots2"], 1)
            act.wait_ge(S["bn_var"], 1)
            run(bn_s[:, 1:2], bn_s[:, 0:1], ACT.Sqrt).then_inc(S["bn_dev"], 1)

            def stage(new, old):
                for q, b, g in old:
                    act.wait_ge(S["ht_ps"], b + 1)
                    run(cur_t[q][0:C, :], bank[q][0:C, 1, :], ACT.Copy).then_inc(S["ht_ev"], 1)
                for q, b, g in old:
                    act.wait_ge(S["m1_ps"], b + 1)
                    run(mid_t[q][0:C, :], bank[q][0:C, 0, :], ACT.Relu, bias=b3a_s[:, :]).then_inc(S["m1_ev"], 1)
                for q, b, g in new:
                    act.wait_ge(S["xt_ps"], b + 1)
                    run(cur_t[q][0:C, :], bank[q][0:C, 0, :], ACT.Copy).then_inc(S["xt_ev"], 1)
                for q, b, g in old:
                    act.wait_ge(S["msg_ps"], b + 1)
                    run(msg_t[q][0:C, :], bank[q][0:C, 0, :], ACT.Relu).then_inc(S["msg_ev"], 1)
                for q, b, g in new:
                    act.wait_ge(S["var_ready"], b + 1)
                    run(dev[q][:, 1, :], dev[q][:, 0, :], ACT.Sqrt).then_inc(S["dev_ready"], 1)
                for q, b, g in old:
                    act.wait_ge(S["gate_ps"], b + 1)
                    run(gate[q][:, :, :], bank[q][:, :, :].rearrange("p k (i n) -> p (k i) n", i=2)[:, :, 0:2 * C], ACT.Sigmoid).then_inc(S["rz_ready"], 1)
                for q, b, g in old:
                    act.wait_ge(S["cand_ready"], b + 1)
                    run(cand[q][:, :, :], scl[q][:, :, :], ACT.Tanh).then_inc(S["new_ready"], 1)

            stage(half(0, 0), [])
            stage(half(0, 1), half(0, 0))
            with act.Fori(1, B // SLOTS) as g0:
                stage(half(g0, 0), half(g0 - 1, 1))
                stage(half(g0, 1), half(g0, 0))
            stage([], half(B // SLOTS - 1, 1))
            act.wait_ge(S["last_var"], 1)
            run(last_dev[:, :, :], last_mom[:, 1], ACT.Sqrt).then_inc(S["last_dev_ready"], 1)

        @block.vector
        def _(dve):
            v = nc.vector
            tt, ts, stt = v.tensor_tensor, v.tensor_scalar, v.scalar_tensor_tensor
            count = [0]

            def did(ins):
                ins.then_inc(S["dve_chain"], 1)
                count[0] += 1
                return count[0]

            def need(n):
                if n > 0:
                    dve.wait_ge(S["dve_chain"], n)

            def then(ins):
                need(did(ins))

            def restart():
                need(count[0])
                dve.sem_clear(S["dve_chain"])
                count[0] = 0

            def tell(name):
                need(count[0])
                v.engine_nop().then_inc(S[name], 1)

            dve.wait_ge(S["cdone"], 1)
            dve.wait_ge(S["xT_ev"], PAIRS)

            def apart(t, m, p):
                return t.rearrange("q (a m w) -> q a m w", a=PAIRS, w=p)

            stays = 0
            for n, (p, r, d, m, at) in enumerate(steps):
                lo, hi, _ = sides(keys[n % 2], p, r, d)
                new_lo, new_hi, _ = sides(keys[1 - n % 2], p, r, d)
                wait(dve, S["step_done"], n)
                wait(dve, S["stay_done"], stays)
                tt(apart(swapped[:, at:at + PAIRS * m * p], m, p), lo, hi, ALU.is_gt)
                tt(new_lo, lo, hi, ALU.min)
                tt(new_hi, lo, hi, ALU.max).then_inc(S["step_done"], 1)
                stays += 1 if r else 0
            dve.wait_ge(S["step_done"], len(steps))
            dve.wait_ge(S["stay_done"], stays)
            ordered = keys[len(steps) % 2]
            then(v.tensor_copy(parts[:, 0], ordered[:, :, :]))
            tell("parts_ready")
            then(tt(ordered[:, :, :], ordered[:, :, :], parts[:, 0], ALU.subtract))
            then(v.tensor_copy(parts[:, 1], ordered[:, :, :]))
            tell("parts_ready")
            then(tt(parts[:, 2], ordered[:, :, :], parts[:, 1], ALU.subtract))
            tell("parts_ready")
            for e, (p, r, d, m, at) in enumerate(reversed(steps)):
                plo, phi, _ = sides(perm, p, r, d)
                de, sw = apart(delta[:, 0:PAIRS * m * p], m, p), apart(swap[:, e % 2, 0:PAIRS * m * p], m, p)
                need(count[0])
                then(tt(de, phi, plo, ALU.subtract))
                dve.wait_ge(S["swap_ready"], e + 1)
                tt(de, de, sw, ALU.mult).then_inc(S["swap_used"], 1)
                dve.wait_ge(S["swap_used"], e + 1)
                did(tt(plo, plo, de, ALU.add))
                did(tt(phi, phi, de, ALU.subtract))
            need(count[0])
            then(v.tensor_copy(ranks, perm[:, :, :]))
            tell("rank_ready")
            dve.wait_ge(S["cdone"], 2)
            did(ts(iota_m[:, 0:1], iota_p[:, :], 31, None, ALU.bitwise_and))
            then(ts(iota_m[:, 1:2], iota_p[:, :], 15, None, ALU.bitwise_and))
            did(v.tensor_copy(iota_a[:, :], iota_m[:, 0:1]))
            then(v.tensor_copy(iota_b[:, :], iota_m[:, 1:2]))
            then(ts(iota_a[:, :], iota_a[:, :], -16.0, None, ALU.add))
            then(tt(iota_a[:, :], iota_a[:, :], iota_a[:, :], ALU.mult))
            then(ts(eq_bias[:, :], iota_a[:, :], -1.0, 1.0, ALU.mult, ALU.add))
            dve.wait_ge(S["mask_ready"], 2)
            dve.wait_ge(S["rankT_ev"], PAIRS)
            restart()

            def rank_bits(b):
                did(v.tensor_copy(rank_u[:, 0], rank_t[:, :, b, :]))
                need(count[0])
                then(ts(rank_u[:, 1], rank_u[:, 0], 4, None, ALU.logical_shift_right))
                did(v.tensor_copy(half_of[:, :, :], rank_u[:, 1]))
                then(ts(rank_u[:, 0], rank_u[:, 0], WORD - 1, None, ALU.bitwise_and))
                then(tt(rank_u[:, 1], one_u[:, :].unsqueeze(1).to_broadcast([P, NT, C]), rank_u[:, 0], ALU.logical_shift_left))

            def members(b, j):
                if j == 0:
                    if not (isinstance(b, int) and b == 0):
                        dve.wait_ge(S["cw_ps"], NT * CW * b)
                    rank_bits(b)
                spread_r = rank_t[:, j, b, :].unsqueeze(1).to_broadcast([P, G, C])
                halves = member[:, j, 1:3, :].rearrange("p s (g c) -> p (s g) c", g=G)
                did(tt(halves, half_of[:, j].unsqueeze(1).to_broadcast([P, 2 * G, C]), half_id[:, :, :, :].rearrange("p s g c -> p (s g) c"), ALU.is_equal))
                did(tt(member[:, j, 0, :].rearrange("p (g c) -> p g c", g=G), spread_r, group_end[:, :, :], ALU.is_lt))
                need(count[0] - 1)
                tt(halves, halves, rank_u[:, 1, j].unsqueeze(1).to_broadcast([P, 2 * G, C]), ALU.mult).then_inc(S["member_ready"], 1)

            nb, en, f1, f2, s1, s2 = (small[:, n, :] for n in range(6))

            def graph(b):
                members(b, 0)
                dve.wait_ge(S["adjb_ready"], NT * b + NT)
                then(tt(neigh[:, :, :], adj_b[:, :, :], eye[:, :, :], ALU.is_gt))
                dve.wait_ge(S["adjT_ev"], NT * b + NT)
                then(tt(neigh_t[:, :, :], adj_t[:, :, :], eye[:, :, :], ALU.is_gt))
                tell("neighT_ready")
                members(b, 1)
                members(b, 2)
                dve.wait_ge(S["nb_ps"], b + 1)
                did(ts(en, nb_sum, float(TRIM), None, ALU.is_gt))
                then(ts(small_u[:, 0, :], nb_sum, 1.0, None, ALU.add))
                did(tt(en, en, mask_t[:, :, b], ALU.mult))
                then(ts(small_u[:, 1, :], small_u[:, 0, :], 1, None, ALU.logical_shift_right))
                did(ts(f1, small_u[:, 1, :], 1.0, None, ALU.add))
                then(ts(f2, small_u[:, 1, :], 2.0, 1.0, ALU.mult, ALU.add))
                did(tt(f1, f1, en, ALU.mult))
                then(tt(f2, f2, en, ALU.mult))
                did(ts(s1, f1, -1.0, None, ALU.add))
                then(ts(s2, f2, -1.0, None, ALU.add))
                for i in range(NT):
                    dve.wait_ge(S["cnt_ps"], NT * b + i + 1)
                    if i:
                        dve.wait_ge(S["drop_ready"], NT * b + i)
                    did(stt(out=drop1[:, i, :], in0=ring[i % 2][:, :], scalar=s1[:, i:i + 1], in1=neigh[:, i, :], op0=ALU.is_equal, op1=ALU.mult))
                    then(stt(out=drop2[:, :], in0=ring[i % 2][:, :], scalar=s2[:, i:i + 1], in1=neigh[:, i, :], op0=ALU.is_equal, op1=ALU.mult))
                    tt(drop1[:, i, :], drop1[:, i, :], drop2[:, :], ALU.add).then_inc(S["drop_ready"], 1)
                members(b, 3)
                for j in range(NT):
                    dve.wait_ge(S["rs_ps"], NT * b + j + 1)
                    then(stt(out=kept_t[:, j, :], in0=ring[j % 2][:, :], scalar=0.0, in1=neigh_t[:, j, :], op0=ALU.is_equal, op1=ALU.mult))
                    tt(kept_t[:, j, P * j:P * j + P], kept_t[:, j, P * j:P * j + P], eye[:, j, P * j:P * j + P], ALU.add).then_inc(S["kept_ready"], 1)
                dve.wait_ge(S["nv_ps"], b + 1)
                for t in range(3):
                    did(ts(mult3[:, :, t], nv_sum, float(t + 1), -float(t + 1), ALU.mult, ALU.add))
                tell("nv_read")
                did(ts(low3[:, :, :], mult3[:, :, :], 2, None, ALU.logical_shift_right))
                then(ts(frac3[:, :, :], mult3[:, :, :], 3, None, ALU.bitwise_and))
                did(v.tensor_copy(weight_old[:, :, :, :], weight[:, :, :, :]) if not (isinstance(b, int) and b == 0) else v.memset(weight_old[:, :, :, :], 0.0))
                did(ts(limit[:, :, :, 0], low3[:, :, :], 0.0, None, ALU.add))
                then(ts(limit[:, :, :, 1], low3[:, :, :], 1.0, None, ALU.add))
                ts(edge[:, :, :, :], limit[:, :, :, :], 0.5, STEEP, ALU.add, ALU.mult).then_inc(S["limit_ready"], 1)
                for t in range(3):
                    did(ts(weight[:, :, t, 1], frac3[:, :, t], QW[t] / 4, None, ALU.mult))
                need(count[0])
                for t in range(3):
                    did(ts(weight[:, :, t, 0], weight[:, :, t, 1], -1.0, QW[t], ALU.mult, ALU.add))
                need(count[0])

            def value(l, u):
                dve.wait_ge(S["row_ps"], UNITS * l + u + 1)
                if u >= 3:
                    dve.wait_ge(S["found_ps"], UNITS * l + u - 2)
                stt(out=prod[:, u % 3, :], in0=near[:, u % DEEP, :], scalar=iota_b[:, :], in1=rows[u % 2][:, :], op0=ALU.is_equal, op1=ALU.mult).then_inc(S["prod_ready"], 1)

            def add_up(l, k):
                dve.wait_ge(S["found_ps"], UNITS * l + GROUPS * (k + 1))
                if k:
                    dve.wait_ge(S["acc_done"], K * l + k)
                for i in range(NT):
                    w = weight_old[:, i, k // 2, k % 2:k % 2 + 1]
                    if k == 0:
                        ins = ts(agg[:, i, :], found[:, i, :], w, None, ALU.mult)
                    else:
                        ins = stt(out=agg[:, i, :], in0=found[:, i, :], scalar=w, in1=agg[:, i, :], op0=ALU.mult, op1=ALU.add)
                ins.then_inc(S["acc_done"], 1)

            def unit(l, u):
                if l is None:
                    return
                value(l, u)
                if u % GROUPS == 1 and u > GROUPS:
                    add_up(l, u // GROUPS - 1)

            def select(b, i, l):
                u = PER_TILE * i
                if b is None:
                    for q in range(PER_TILE):
                        unit(l, u + q)
                    return
                cnt = cnt2[:, i % 2]
                if i == 0:
                    unit(l, 0)
                dve.wait_ge(S["cw_ev"], NT * CW * b + CW * i + 2)
                did(v.tensor_copy(words[:, 0, 0:C], group_tag[:, 0, :]))
                did(tt(words[:, 0, C:], cnt[:, 0:(G - 1) * C], group_tag[:, 1:, :].rearrange(flat), ALU.add))
                need(count[0])
                last = (G - 1) * C
                if i == 0:
                    for q in range(3):
                        did(ts(below[:, 0, q, 0:last], cnt[:, 0:last], limit[:, 0, q // 2, q % 2:q % 2 + 1], None, ALU.is_le))
                for h in range(2):
                    early = 3 if i == 0 and h == 0 else 1
                    at = u + 6 * h
                    for q in range(1 if early == 3 else 0, early):
                        unit(l, at + q)
                    if h == 0:
                        dve.wait_ge(S["cw_ev"], NT * CW * b + CW * i + CW)
                        did(tt(change[:, :, 0:last], words[:, :, 0:last], words[:, :, C:], ALU.bitwise_xor))
                        v.tensor_copy(change[:, :, last:], words[:, :, 0:C]).then_inc(S["tile_read"], 1)
                        dve.wait_ge(S["tile_read"], NT * b + i + 1)
                    need(count[0])
                    if i or h:
                        dve.wait_ge(S["mask_made"], MASKS * b + 2 * i + h)
                    for w in range(3):
                        ins = tt(picked[:, w], below[:, h], change[:, w, :].unsqueeze(1).to_broadcast([P, 3, G * C]), ALU.mult)
                        if w < 2:
                            did(ins)
                        else:
                            ins.then_inc(S["mask_used"], 1)
                        if w + 1 >= early:
                            unit(l, at + w + 1)
                    dve.wait_ge(S["mask_used"], 2 * (NT * b + i) + h + 1)
                    a = picked[:, :, :, :].rearrange("p w k n -> p (w k) n")
                    n = G * C // 2
                    while n > C:
                        then(tt(a[:, :, 0:n], a[:, :, 0:n], a[:, :, n:2 * n], ALU.bitwise_xor))
                        if n >= G * C // 4:
                            unit(l, at + (4 if n == G * C // 2 else 5))
                        n //= 2
                    did(tt(result[:, :, i, 3 * h:3 * h + 3, :], picked[:, :, :, 0:C], picked[:, :, :, C:2 * C], ALU.bitwise_xor))

            big = NT * K * C

            def r3(n):
                return result[:, n].rearrange("p t k c -> p (t k c)")

            pool9 = picked[:, :, :, :].rearrange("p w k n -> p (w k n)")
            more = change[:, :, :].rearrange(flat)
            tmp = [pool9[:, big * n:big * n + big] for n in range(6)] + [more[:, big * n:big * n + big] for n in range(2)] + [words[:, 0:2, :].rearrange(flat)[:, 0:big]]

            def pop(word, x2, x4, x8, t):
                then(ts(t, word, 1, 0x5555, ALU.logical_shift_right, ALU.bitwise_and))
                then(tt(x2, word, t, ALU.subtract))
                did(ts(t, x2, 2, 0x3333, ALU.logical_shift_right, ALU.bitwise_and))
                then(ts(x4, x2, 0x3333, None, ALU.bitwise_and))
                then(tt(x4, x4, t, ALU.add))
                then(ts(t, x4, 4, None, ALU.logical_shift_right))
                then(tt(t, t, x4, ALU.add))
                then(ts(x8, t, 0x0F0F, None, ALU.bitwise_and))

            cx, wl, wh = r3(0), r3(1), r3(2)
            x2, x4, x8, t, r, bit, sh, blk, t2 = tmp

            def bits_start():
                then(ts(t, cx, 1023, None, ALU.bitwise_and))
                rr = r.rearrange("p (q c) -> p q c", c=C)
                lim = limit[:, :, :, :].rearrange("p i t s -> p (i t s)").unsqueeze(2).to_broadcast([P, NT * K, C])
                then(tt(rr, lim, t.rearrange("p (q c) -> p q c", c=C), ALU.subtract))

            def bits_first():
                pop(wl, x2, x4, x8, t)
                did(ts(t, x8, 8, None, ALU.logical_shift_right))
                need(count[0])
                then(tt(t, t, x8, ALU.add))
                then(ts(t, t, 31, None, ALU.bitwise_and))
                then(tt(bit, r, t, ALU.is_ge))
                did(ts(blk, cx, 10, 1, ALU.logical_shift_right, ALU.logical_shift_left))
                then(tt(t, t, bit, ALU.mult))
                did(tt(wh, wl, wh, ALU.bitwise_xor))
                then(tt(r, r, t, ALU.subtract))
                then(ts(t.bitcast(I16), bit, -1.0, None, ALU.mult))
                q3 = "p (q c) -> p q c"
                x16 = idx[:, :, :, 0, :].rearrange("p t k c -> p (t k) c")
                did(stt(out=x16, in0=blk.rearrange(q3, c=C), scalar=-16.0, in1=bit.rearrange(q3, c=C), op0=ALU.add, op1=ALU.add))
                then(tt(t, t, wh, ALU.bitwise_and))
                then(tt(wl, wl, t, ALU.bitwise_xor))
                did(tt(idx[:, :, :, 1, :].rearrange("p t k c -> p (t k) c"), x16, x16, ALU.mult))

            def bits_second():
                then(ts(t, x8, 255, None, ALU.bitwise_and))
                then(tt(bit, r, t, ALU.is_ge))
                did(tt(t, t, bit, ALU.mult))
                then(ts(sh, bit, 3, None, ALU.logical_shift_left))
                then(tt(r, r, t, ALU.subtract))

            def bits_third():
                for field, size in ((x4, 4), (x2, 2)):
                    then(tt(t, field, sh, ALU.logical_shift_right))
                    then(ts(t, t, 2 ** size - 1, None, ALU.bitwise_and))
                    then(tt(bit, r, t, ALU.is_ge))
                    did(tt(t, t, bit, ALU.mult))
                    then(ts(bit, bit, size // 2, None, ALU.logical_shift_left))
                    did(tt(r, r, t, ALU.subtract))
                    then(tt(sh, sh, bit, ALU.add))
                then(tt(t, wl, sh, ALU.logical_shift_right))
                then(ts(t, t, 1, None, ALU.bitwise_and))
                then(tt(bit, r, t, ALU.is_ge))
                then(tt(idx_b[:, :, :].rearrange(flat), sh, bit, ALU.add))

            def norm_a():
                for i in range(NT):
                    did(v.bn_stats(stats[:, i, :], pre[:, i, :]))
                need(count[0])
                for i in range(NT):
                    did(v.bn_aggr(moments[:, i, :], stats[:, i, :]))
                need(count[0])
                then(ts(small[:, 14, :], moments[:, :, 1], EPS, None, ALU.add))
                tell("z_ready")

            def norm_b():
                then(v.reciprocal(inv[:, 0, :], inv[:, 0, :]))
                for i in range(NT):
                    did(ts(pre[:, i, :], pre[:, i, :], moments[:, i, 0:1], inv[:, 0, i:i + 1], ALU.subtract, ALU.mult))
                need(count[0])

            def ffn_start(l):
                add_up(l, K - 1)
                dve.wait_ge(S["acc_done"], K * l + K)
                then(tt(scaled[:, :, :], xb(l), agg[:, :, :], ALU.add))
                tell("ffn_x")

            def ffn_end(l):
                dve.wait_ge(S["y_ps"], l + 1)
                for i in range(NT):
                    did(stt(out=pre[:, i, :], in0=ring[0][:, C * i:C * i + C], scalar=mask_t[:, i, bass.ds(l, 1)], in1=x_all[:, i, l, :], op0=ALU.mult, op1=ALU.add))
                need(count[0])
                norm_a()

            def gcn_start(l):
                dve.wait_ge(S["sd_ready"], 3 * l + 1)
                norm_b()
                tell("x1_ready")
                then(ts(small[:, 12, :], rowsum[:, l, :], 1.0, None, ALU.add))
                did(ts(small[:, 11, :], small[:, 12, :], 0.0, None, ALU.is_gt))
                then(ts(small[:, 13, :], small[:, 12, :], 1e-30, None, ALU.max))
                tell("z_ready")
                dve.wait_ge(S["sd_ready"], 3 * l + 2)
                then(v.reciprocal(inv[:, 1, :], inv[:, 1, :]))
                then(tt(inv[:, 1, :], inv[:, 1, :], small[:, 11, :], ALU.mult))

            def gcn_middle(l):
                dve.wait_ge(S["tr_ps"], l + 1)
                product = ring[0][:, 0:NT * C].rearrange("p (t c) -> p t c", t=NT)
                then(tt(scaled[:, :, :], product, inv[:, 1, :].unsqueeze(2).to_broadcast([P, NT, C]), ALU.mult))
                split()
                tell("split_ready")

            def split():
                then(v.tensor_copy(split3[:, 0], scaled[:, :, :]))
                then(tt(agg[:, :, :], scaled[:, :, :], split3[:, 0], ALU.subtract))
                then(v.tensor_copy(split3[:, 1], agg[:, :, :]))
                then(tt(split3[:, 2], agg[:, :, :], split3[:, 1], ALU.subtract))

            def gcn_end(l):
                dve.wait_ge(S["g_ps"], NT * l + NT)
                then(tt(scaled[:, :, :].rearrange(flat), ring[1][:, 0:NT * C], scaled[:, :, :].rearrange(flat), ALU.add))
                for i in range(NT):
                    did(ts(scaled[:, i, :], scaled[:, i, :], inv[:, 1, i:i + 1], 0.0, ALU.mult, ALU.max))
                need(count[0])
                then(tt(pre[:, :, :], pre[:, :, :], scaled[:, :, :], ALU.add))
                norm_a()
                dve.wait_ge(S["sd_ready"], 3 * l + 3)
                norm_b()
                then(v.tensor_copy(xb(l), pre[:, :, :]))

            def body(b, l):
                if b is not None:
                    graph(b)
                for i in range(NT):
                    select(b, i, l)
                need(count[0]) if count[0] else None
                if b is not None:
                    bits_start()
                if l is not None:
                    ffn_start(l)
                if b is not None:
                    bits_first()
                if l is not None:
                    ffn_end(l)
                if b is not None:
                    pop(wl, x2, x4, x8, t)
                if l is not None:
                    gcn_start(l)
                if b is not None:
                    bits_second()
                if l is not None:
                    gcn_middle(l)
                if b is not None:
                    bits_third()
                    tell("idx_ready")
                if l is not None:
                    gcn_end(l)
                restart()

            body(0, None)
            with dve.Fori(1, B) as b:
                body(b, b - 1)
            dve.wait_ge(S["idxT_ev"], TURNS * B)
            then(v.tensor_copy(weight_old[:, :, :, :], weight[:, :, :, :]))
            body(None, B - 1)

            for q in range(SLOTS):
                for t in (cur_t, mid_t, msg_t):
                    did(v.memset(t[q][C:C + 1, :], 1.0))
            tell("l1_done")
            for b in range(B):
                dve.wait_ge(S["bT_ps"], b + 1)
                v.bn_stats(bn_stat[:, b, :], bank[b % 2][0:C, 0, :]).then_inc(S["bn_read"], 1)
            dve.wait_ge(S["bn_read"], B)
            then(v.bn_aggr(bn_mom[:, :], bn_stat[:, :, :].rearrange(flat)))
            then(ts(bn_s[:, 0:1], bn_mom[:, 1:2], EPS, None, ALU.add))
            tell("bn_var")
            dve.wait_ge(S["bn_dev"], 1)
            then(v.reciprocal(bn_s[:, 1:2], bn_s[:, 1:2]))
            then(tt(bn_s[:, 2:3], bn_s[:, 1:2], gamma_s[:, :], ALU.mult))
            then(tt(bn_s[:, 3:4], bn_s[:, 2:3], bn_mom[:, 0:1], ALU.mult))
            then(tt(bn_s[:, 3:4], beta_s[:, :], bn_s[:, 3:4], ALU.subtract))
            tell("bn_shift")
            did(ts(w2f_s[0:C, :], w2_s[:, :], bn_s[:, 2:3], None, ALU.mult))
            dve.wait_ge(S["b2f_ps"], 1)
            did(tt(w2f_s[C:C + 1, :], bank[2][C:C + 1, 0, 0:C], b2_s[C:C + 1, :], ALU.add))
            dve.wait_ge(S["roots2"], 1)
            did(v.reciprocal(inv_root[:, :, :], root[:, :, :]))
            tell("w2f_ready")
            dve.wait_ge(S["w23_ready"], 2)
            v.engine_nop().then_inc(S["graph_done"], SLOTS)
            restart()

            def cut3(q, name):
                then(v.tensor_copy(cut[q][:, 0], scl[q][:, :, :]))
                then(tt(rest[q][:, :, :], scl[q][:, :, :], cut[q][:, 0], ALU.subtract))
                then(v.tensor_copy(cut[q][:, 1], rest[q][:, :, :]))
                tt(cut[q][:, 2], rest[q][:, :, :], cut[q][:, 1], ALU.subtract).then_inc(S[name], 1)

            def moments_of(q, src):
                for i in range(NT):
                    did(v.bn_stats(stat[q][:, i, :], src[:, i, :]))
                need(count[0])
                for i in range(NT):
                    did(v.bn_aggr(mom[q][:, i, :], stat[q][:, i, :]))
                need(count[0])

            def spread_of(t):
                return t.unsqueeze(2).to_broadcast([P, NT, C])

            def per_tile(bank_half):
                return bank_half[:, 0:NT * C].rearrange("p (t c) -> p t c", t=NT)

            def stage(new, old, done):
                for q, b, g in new:
                    v.tensor_copy(cur[q][:, :, :], x_all[:, :, b, :]).then_inc(S["cur_ready"], 1)
                for q, b, g in old:
                    dve.wait_ge(S["m2_ps"], b + 1)
                    then(ts(scl[q][:, :, :], per_tile(bank[q][:, 1]), 0.0, None, ALU.max))
                    cut3(q, "cut2_ready")
                for q, b, g in new:
                    dve.wait_ge(S["lin_ps"], b + 1)
                    did(v.tensor_copy(lin[q][:, :, :], per_tile(bank[q][:, 1])))
                    then(tt(scl[q][:, :, :], per_tile(bank[q][:, 1]), spread_of(inv_root[:, b, :]), ALU.mult))
                    cut3(q, "cut_ready")
                for q, b, g in done:
                    moments_of(q, x_all[:, :, b, :])
                    did(v.tensor_copy(last_mom[:, 0, b, :], mom[q][:, :, 0]))
                    did(ts(last_mom[:, 1, b, :], mom[q][:, :, 1], EPS, None, ALU.add))
                for q, b, g in new:
                    dve.wait_ge(S["agg_ps"], b + 1)
                    dve.wait_ge(S["cut_ready"], b + 1)
                    then(tt(rest[q][:, :, :], per_tile(bank[q][:, 0]), spread_of(root[:, b, :]), ALU.mult))
                    then(tt(lin[q][:, :, :], lin[q][:, :, :], rest[q][:, :, :], ALU.subtract))
                    then(stt(out=lin[q][:, :, :], in0=lin[q][:, :, :], scalar=0.01, in1=lin[q][:, :, :], op0=ALU.mult, op1=ALU.max))
                    then(tt(cur[q][:, :, :], cur[q][:, :, :], lin[q][:, :, :], ALU.add))
                    moments_of(q, cur[q])
                    ts(dev[q][:, 0, :], mom[q][:, :, 1], EPS, None, ALU.add).then_inc(S["var_ready"], 1)
                for q, b, g in new:
                    then(tt(cur[q][:, :, :], cur[q][:, :, :], spread_of(mom[q][:, :, 0]), ALU.subtract))
                for q, b, g in new:
                    dve.wait_ge(S["dev_ready"], b + 1)
                    then(v.reciprocal(dev[q][:, 1, :], dev[q][:, 1, :]))
                    tt(cur[q][:, :, :], cur[q][:, :, :], spread_of(dev[q][:, 1, :]), ALU.mult).then_inc(S["x3_ready"], 1)
                for q, b, g in old:
                    dve.wait_ge(S["rz_ready"], b + 1)
                    dve.wait_ge(S["cut2_ready"], b + 1)
                    pieces = bank[q][:, :, :].rearrange("p k (i n) -> p (k i) n", i=2)
                    then(tt(scl[q][:, :, :], pieces[:, :, 3 * C:4 * C], gate[q][:, :, 0:C], ALU.mult))
                    tt(scl[q][:, :, :], pieces[:, :, 2 * C:3 * C], scl[q][:, :, :], ALU.add).then_inc(S["cand_ready"], 1)
                for q, b, g in old:
                    dve.wait_ge(S["new_ready"], b + 1)
                    then(tt(rest[q][:, :, :], cur[q][:, :, :], cand[q][:, :, :], ALU.subtract))
                    then(tt(rest[q][:, :, :], rest[q][:, :, :], gate[q][:, :, C:2 * C], ALU.mult))
                    then(tt(cand[q][:, :, :], cand[q][:, :, :], rest[q][:, :, :], ALU.add))
                    did(tt(x_all[:, :, b, :], cur[q][:, :, :], cand[q][:, :, :], ALU.add))
                    tell("graph_done")

            stage(half(0, 0), [], [])
            stage(half(0, 1), half(0, 0), [])
            restart()
            with dve.Fori(1, B // SLOTS) as g0:
                stage(half(g0, 0), half(g0 - 1, 1), half(g0 - 1, 0))
                stage(half(g0, 1), half(g0, 0), half(g0 - 1, 1))
                restart()
            stage([], half(B // SLOTS - 1, 1), half(B // SLOTS - 1, 0))
            stage([], [], half(B // SLOTS - 1, 1))
            restart()
            v.engine_nop().then_inc(S["last_var"], 1)
            dve.wait_ge(S["last_dev_ready"], 1)
            then(v.reciprocal(last_dev[:, :, :], last_dev[:, :, :]))
            for i in range(NT):
                then(tt(x_all[:, i], x_all[:, i], last_mom[:, 0, :, i].unsqueeze(2).to_broadcast([P, B, C]), ALU.subtract))
                then(tt(x_all[:, i], x_all[:, i], last_dev[:, :, i].unsqueeze(2).to_broadcast([P, B, C]), ALU.mult))
                tell("tile_done")


_INS = ['x', 'adj', 'nodemask', 'L0_gnn_W1', 'L0_gnn_b1', 'L0_gnn_W2', 'L0_gnn_b2', 'L1_gnn_kernel', 'L2_gnn_gamma',
        'L2_gnn_beta', 'L2_gnn_W', 'L2_gnn_b', 'L3_gnn_W1', 'L3_gnn_b1', 'L3_gnn_W2', 'L3_gnn_b2', 'L3_gnn_W_ih',
        'L3_gnn_b_ih', 'L3_gnn_W_hh', 'L3_gnn_b_hh']
_OUTS = [((B, N, C), 'float32')]


def kernel(**inputs):
    import numpy as _np
    import concourse.bacc as _bacc
    from concourse import mybir as _mybir
    from concourse.bass_utils import run_bass_kernel_spmd as _run

    nc = _bacc.Bacc("TRN2", target_bir_lowering=False, num_devices=1)
    arrays, args = {}, []
    for name in _INS:
        a = _np.ascontiguousarray(inputs[name])
        if a.dtype.kind == "b":
            a = a.view(_np.uint8)
        arrays[f"in_{name}_dram"] = a
        args.append(nc.dram_tensor(f"in_{name}_dram", a.shape, _mybir.dt.from_np(a.dtype), kind="ExternalInput").ap())
    for i, (shape, dtype) in enumerate(_OUTS):
        dt = _mybir.dt.from_np(_np.dtype(dtype))
        args.append(nc.dram_tensor(f"out_{i}_dram", shape, dt, kind="ExternalOutput").ap())
    build(nc, *args)
    r = _run(nc, [arrays], core_ids=[0])
    return r.results[0]["out_0_dram"]
```
